# Optimizing a Trainium2 kernel written in Bass

```python
import numpy as np
import jax
import jax.numpy as jnp

def _softmax(x, axis=-1):
    return jax.nn.softmax(x, axis=axis)

def _gelu(x):
    return jax.nn.gelu(x, approximate=True)

def _silu(x):
    return jax.nn.silu(x)

def _sigmoid(x):
    return jax.nn.sigmoid(x)

def _layernorm(x, axis=-1, eps=1e-05):
    m = jnp.mean(x, axis=axis, keepdims=True)
    v = jnp.var(x, axis=axis, keepdims=True)
    return (x - m) / jnp.sqrt(v + eps)

def _scatter_add(tgt, idx, src, axis=0):
    return tgt.at[idx].add(src)

def _segment_sum(src, seg, n):
    return jax.ops.segment_sum(src, seg, n)
kernel_name = 'mk_gnn_ffn_d2_gnn_r8_ffebd7'

def setup_inputs(seed: int=0):
    np.random.seed(seed)
    _w = jnp.asarray

    def _rec_inputs():
        import jax
        import jax.numpy as jnp
        _gk = jax.random.key(seed)
        x = -0.0003713 + 1 * jax.random.normal(jax.random.fold_in(_gk, 1), (6250, 256), jnp.float32)
        src = jax.random.randint(jax.random.fold_in(_gk, 2), (100000,), 0, 6250, jnp.int32)
        dst = jax.random.randint(jax.random.fold_in(_gk, 3), (100000,), 0, 6250, jnp.int32)
        _o = jnp.argsort(dst, stable=True)
        src = src[_o]
        dst = dst[_o]
        edge_attr_50 = 0.000154925 + 1.00009 * jax.random.normal(jax.random.fold_in(_gk, 11), (100000, 50), jnp.float32)
        edge_weight = jax.random.uniform(jax.random.fold_in(_gk, 13), (100000,), jnp.float32, 0.0, 9.99998)
        return (x, src, dst, edge_attr_50, edge_weight)
    x, src, dst, edge_attr_50, edge_weight = _rec_inputs()

    def _L0_gnn_setup():
        import jax, jax.numpy as jnp
        import numpy as np
        N, E, H, G = (6250, 100000, 256, 50)
        CUTOFF = 10.0
        PI = float(np.pi)
        LOG2 = float(np.log(2.0))

        def ssp(x):
            return jax.nn.softplus(x) - LOG2
        key = jax.random.key(seed)
        ks = jax.random.split(key, 16)

        def lin(kw, kb, fan_in, fan_out):
            s = float(np.sqrt(6.0 / (fan_in + fan_out)))
            W = jax.random.uniform(kw, (fan_in, fan_out), minval=-s, maxval=s, dtype=jnp.float32)
            b = jnp.zeros((fan_out,), jnp.float32)
            return (W, b)
        h = jax.random.normal(ks[0], (N, H), dtype=jnp.float32)
        edge_index = jax.random.randint(ks[1], (2, E), 0, N, dtype=jnp.int64)
        edge_weight = jax.random.uniform(ks[2], (E,), dtype=jnp.float32) * CUTOFF
        edge_attr = jax.random.normal(ks[3], (E, G), dtype=jnp.float32)
        aw_W, aw_b = lin(ks[4], ks[5], H, H)
        m1_W, m1_b = lin(ks[6], ks[7], G, H)
        m2_W, m2_b = lin(ks[8], ks[9], H, H)
        o1_W, o1_b = lin(ks[10], ks[11], H, H)
        o2_W, o2_b = lin(ks[12], ks[13], H, H)
        return {'h': h, 'edge_index': edge_index, 'edge_weight': edge_weight, 'edge_attr': edge_attr, 'aw_W': aw_W, 'aw_b': aw_b, 'm1_W': m1_W, 'm1_b': m1_b, 'm2_W': m2_W, 'm2_b': m2_b, 'o1_W': o1_W, 'o1_b': o1_b, 'o2_W': o2_W, 'o2_b': o2_b}
    _L0_gnn_all = _L0_gnn_setup()
    _L0_gnn_in = {k: v for k, v in _L0_gnn_all.items() if k in ('aw_W', 'aw_b', 'm1_W', 'm1_b', 'm2_W', 'm2_b', 'o1_W', 'o1_b', 'o2_W', 'o2_b')}
    del _L0_gnn_all

    def _L0_ffn_setup():
        import jax, jax.numpy as jnp
        import numpy as np
        B, S, D = (8, 512, 256)
        H = 4 * D
        CAPACITY = 0.5
        key = jax.random.key(seed)
        ks = jax.random.split(key, 6)
        x = jax.random.normal(ks[0], (B, S, D), dtype=jnp.float32)
        attention_mask = jnp.zeros((B, 1, 1, S), dtype=jnp.float32)
        wr = jax.random.normal(ks[1], (D, 1), dtype=jnp.float32) * 0.02
        br = jnp.zeros((1,), dtype=jnp.float32)
        w1 = jax.random.normal(ks[2], (D, H), dtype=jnp.float32) * 0.02
        b1 = jnp.zeros((H,), dtype=jnp.float32)
        w2 = jax.random.normal(ks[3], (H, D), dtype=jnp.float32) * 0.02
        b2 = jnp.zeros((D,), dtype=jnp.float32)
        return {'x': x, 'attention_mask': attention_mask, 'wr': wr, 'br': br, 'w1': w1, 'b1': b1, 'w2': w2, 'b2': b2}
    _L0_ffn_all = _L0_ffn_setup()
    _L0_ffn_in = {k: v for k, v in _L0_ffn_all.items() if k in ('attention_mask', 'wr', 'br', 'w1', 'b1', 'w2', 'b2')}
    del _L0_ffn_all

    def _L1_gnn_setup():
        import jax, jax.numpy as jnp
        import numpy as np
        key = jax.random.key(seed)
        k1, k2, k3 = jax.random.split(key, 3)
        N, E, D_IN, D_OUT = (12500, 400000, 256, 256)
        x = jax.random.normal(k1, (N, D_IN), dtype=jnp.float32)
        W = jax.random.normal(k2, (D_OUT, D_IN), dtype=jnp.float32) * (1.0 / np.sqrt(D_IN))
        edge_index = jax.random.randint(k3, (2, E), 0, N, dtype=jnp.int32)
        return {'x': x, 'W': W, 'edge_index': edge_index}
    _L1_gnn_all = _L1_gnn_setup()
    _L1_gnn_in = {k: v for k, v in _L1_gnn_all.items() if k in ('W',)}
    del _L1_gnn_all

    def _L1_ffn_setup():
        import math
        import jax, jax.numpy as jnp
        import numpy as np
        CAPACITY_FACTOR = 1.25
        TOP_K = 2
        LN_EPS = 1e-05

        def _layer_norm(x, gamma, beta):
            mu = jnp.mean(x, axis=-1, keepdims=True)
            var = jnp.var(x, axis=-1, keepdims=True)
            return (x - mu) * jax.lax.rsqrt(var + LN_EPS) * gamma + beta
        key = jax.random.key(seed)
        ks = jax.random.split(key, 4)
        B, S, D, F, E = (8, 512, 256, 512, 8)
        x = jax.random.normal(ks[0], (B, S, D), dtype=jnp.float32)
        Wr = jax.random.normal(ks[1], (D, E), dtype=jnp.float32) / np.sqrt(D)
        br = jnp.zeros((E,), jnp.float32)
        W1 = jax.random.normal(ks[2], (E, D, F), dtype=jnp.float32) / np.sqrt(D)
        b1 = jnp.zeros((E, F), jnp.float32)
        W2 = jax.random.normal(ks[3], (E, F, D), dtype=jnp.float32) / np.sqrt(F)
        b2 = jnp.zeros((E, D), jnp.float32)
        gamma = jnp.ones((D,), jnp.float32)
        beta = jnp.zeros((D,), jnp.float32)
        return {'x': x, 'Wr': Wr, 'br': br, 'W1': W1, 'b1': b1, 'W2': W2, 'b2': b2, 'gamma': gamma, 'beta': beta}
    _L1_ffn_all = _L1_ffn_setup()
    _L1_ffn_in = {k: v for k, v in _L1_ffn_all.items() if k in ('Wr', 'br', 'W1', 'b1', 'W2', 'b2', 'gamma', 'beta')}
    del _L1_ffn_all
    return {'x': x, 'src': src, 'dst': dst, 'edge_attr_50': edge_attr_50, 'edge_weight': edge_weight, 'L0_gnn_aw_W': _L0_gnn_in['aw_W'], 'L0_gnn_aw_b': _L0_gnn_in['aw_b'], 'L0_gnn_m1_W': _L0_gnn_in['m1_W'], 'L0_gnn_m1_b': _L0_gnn_in['m1_b'], 'L0_gnn_m2_W': _L0_gnn_in['m2_W'], 'L0_gnn_m2_b': _L0_gnn_in['m2_b'], 'L0_gnn_o1_W': _L0_gnn_in['o1_W'], 'L0_gnn_o1_b': _L0_gnn_in['o1_b'], 'L0_gnn_o2_W': _L0_gnn_in['o2_W'], 'L0_gnn_o2_b': _L0_gnn_in['o2_b'], 'L0_ffn_attention_mask': _L0_ffn_in['attention_mask'], 'L0_ffn_wr': _L0_ffn_in['wr'], 'L0_ffn_br': _L0_ffn_in['br'], 'L0_ffn_w1': _L0_ffn_in['w1'], 'L0_ffn_b1': _L0_ffn_in['b1'], 'L0_ffn_w2': _L0_ffn_in['w2'], 'L0_ffn_b2': _L0_ffn_in['b2'], 'L1_gnn_W': _L1_gnn_in['W'], 'L1_ffn_Wr': _L1_ffn_in['Wr'], 'L1_ffn_br': _L1_ffn_in['br'], 'L1_ffn_W1': _L1_ffn_in['W1'], 'L1_ffn_b1': _L1_ffn_in['b1'], 'L1_ffn_W2': _L1_ffn_in['W2'], 'L1_ffn_b2': _L1_ffn_in['b2'], 'L1_ffn_gamma': _L1_ffn_in['gamma'], 'L1_ffn_beta': _L1_ffn_in['beta']}

def reference(x, src, dst, edge_attr_50, edge_weight, L0_gnn_aw_W, L0_gnn_aw_b, L0_gnn_m1_W, L0_gnn_m1_b, L0_gnn_m2_W, L0_gnn_m2_b, L0_gnn_o1_W, L0_gnn_o1_b, L0_gnn_o2_W, L0_gnn_o2_b, L0_ffn_attention_mask, L0_ffn_wr, L0_ffn_br, L0_ffn_w1, L0_ffn_b1, L0_ffn_w2, L0_ffn_b2, L1_gnn_W, L1_ffn_Wr, L1_ffn_br, L1_ffn_W1, L1_ffn_b1, L1_ffn_W2, L1_ffn_b2, L1_ffn_gamma, L1_ffn_beta):
    import jax
    import jax.numpy as jnp

    def _L0_gnn_ref(h, edge_index, edge_weight, edge_attr, aw_W, aw_b, m1_W, m1_b, m2_W, m2_b, o1_W, o1_b, o2_W, o2_b):
        import jax, jax.numpy as jnp
        import numpy as np
        N, E, H, G = (6250, 100000, 256, 50)
        CUTOFF = 10.0
        PI = float(np.pi)
        LOG2 = float(np.log(2.0))

        def ssp(x):
            return jax.nn.softplus(x) - LOG2
        n_nodes = h.shape[0]
        h1 = h @ aw_W + aw_b
        C = 0.5 * (jnp.cos(edge_weight * (PI / CUTOFF)) + 1.0)
        Wf = ssp(ssp(edge_attr @ m1_W + m1_b) @ m2_W + m2_b)
        Wf = Wf * C[:, None]
        src, dst = (edge_index[0], edge_index[1])
        msg = h1[src] * Wf
        agg = jax.ops.segment_sum(msg, dst, num_segments=n_nodes)
        out = ssp(agg @ o1_W + o1_b) @ o2_W + o2_b
        return out

    def _L0_ffn_ref(x, attention_mask, wr, br, w1, b1, w2, b2):
        import jax, jax.numpy as jnp
        import numpy as np
        B, S, D = (8, 512, 256)
        H = 4 * D
        CAPACITY = 0.5
        b, s, d = x.shape
        weights = (jnp.einsum('bsd,do->bso', x, wr) + br)[..., 0]
        k = max(1, int(CAPACITY * s))
        kk = k - 1 if k > 1 else 1
        _, idx = jax.lax.top_k(weights, k)
        sel_idx = idx[:, :kk]
        sel = jnp.take_along_axis(x, sel_idx[:, :, None], axis=1)
        h = jax.nn.gelu(jnp.einsum('bkd,dh->bkh', sel, w1) + b1)
        y = jnp.einsum('bkh,hd->bkd', h, w2) + b2
        w_sel = jnp.take_along_axis(weights, sel_idx, axis=1)
        y = y * w_sel[..., None]
        batch_idx = jnp.arange(b)[:, None]
        processed = jnp.zeros_like(x).at[batch_idx, sel_idx].set(y)
        return processed + x

    def _L1_gnn_ref(x, W, edge_index):
        import jax, jax.numpy as jnp
        import numpy as np
        N = x.shape[0]
        loops = jnp.arange(N, dtype=edge_index.dtype)
        src = jnp.concatenate([edge_index[0], loops])
        dst = jnp.concatenate([edge_index[1], loops])
        deg = jax.ops.segment_sum(jnp.ones_like(src, dtype=x.dtype), src, num_segments=N)
        deg_rsqrt = jax.lax.rsqrt(deg)
        vals = deg_rsqrt[src] * deg_rsqrt[dst]
        h = x @ W.T
        msgs = vals[:, None] * h[dst]
        out = jax.ops.segment_sum(msgs, src, num_segments=N)
        return out

    def _L1_ffn_ref(x, Wr, br, W1, b1, W2, b2, gamma, beta):
        import math
        import jax, jax.numpy as jnp
        import numpy as np
        CAPACITY_FACTOR = 1.25
        TOP_K = 2
        LN_EPS = 1e-05

        def _layer_norm(x, gamma, beta):
            mu = jnp.mean(x, axis=-1, keepdims=True)
            var = jnp.var(x, axis=-1, keepdims=True)
            return (x - mu) * jax.lax.rsqrt(var + LN_EPS) * gamma + beta
        B, S, D = x.shape
        E = Wr.shape[1]
        N = B * S
        K = TOP_K
        logits = jnp.mean(x, axis=1) @ Wr + br
        routing_weights = jax.nn.softmax(logits, axis=-1)
        capacity = float(math.ceil(N * CAPACITY_FACTOR / E))
        expected_loads = routing_weights.sum(axis=0) * (N / B)
        scale = jnp.where(expected_loads > capacity, capacity / expected_loads, 1.0)
        routing_weights = jax.nn.softmax(routing_weights * scale, axis=-1)
        rw_tok = jnp.broadcast_to(routing_weights[:, None, :], (B, S, E)).reshape(N, E)
        top_w, top_i = jax.lax.top_k(rw_tok, K)
        top_w = jax.nn.softmax(top_w, axis=-1)
        xf = x.reshape(N, D)
        h = jax.nn.gelu(jnp.einsum('nd,edf->enf', xf, W1) + b1[:, None, :], approximate=False)
        y = jnp.einsum('enf,efd->end', h, W2) + b2[:, None, :]
        w_dense = jnp.zeros((N, E), x.dtype).at[jnp.arange(N)[:, None], top_i].add(top_w)
        out = jnp.einsum('ne,end->nd', w_dense, y).reshape(B, S, D)
        out = _layer_norm(out + x, gamma, beta)
        return out
    edge_index = jnp.stack([src, dst])
    x = x + _L0_gnn_ref(_layernorm(x, axis=-1), edge_index, edge_weight, edge_attr_50, L0_gnn_aw_W, L0_gnn_aw_b, L0_gnn_m1_W, L0_gnn_m1_b, L0_gnn_m2_W, L0_gnn_m2_b, L0_gnn_o1_W, L0_gnn_o1_b, L0_gnn_o2_W, L0_gnn_o2_b)
    x = x + _L0_ffn_ref(_layernorm(x, axis=-1)[None], L0_ffn_attention_mask, L0_ffn_wr, L0_ffn_br, L0_ffn_w1, L0_ffn_b1, L0_ffn_w2, L0_ffn_b2)[0]
    x = x + _L1_gnn_ref(_layernorm(x, axis=-1), L1_gnn_W, edge_index)
    x = x + _L1_ffn_ref(_layernorm(x, axis=-1)[None], L1_ffn_Wr, L1_ffn_br, L1_ffn_W1, L1_ffn_b1, L1_ffn_W2, L1_ffn_b2, L1_ffn_gamma, L1_ffn_beta)[0]
    return x

_drawn_inputs = setup_inputs


def setup_inputs(seed=0):
    import zlib

    import numpy as np

    out = dict(_drawn_inputs(seed))
    spreads = {'L0_gnn_aw_b': (0.0, 0.1),
     'L0_gnn_m1_b': (0.0, 0.1),
     'L0_gnn_m2_b': (0.0, 0.1),
     'L0_gnn_o1_b': (0.0, 0.1),
     'L0_gnn_o2_b': (0.0, 0.1),
     'L0_ffn_b1': (0.0, 0.8),
     'L0_ffn_b2': (0.0, 0.635),
     'L1_ffn_br': (0.0, 0.8),
     'L1_ffn_b1': (0.0, 0.518),
     'L1_ffn_b2': (0.0, 0.376),
     'L1_ffn_gamma': (1.0, 0.2),
     'L1_ffn_beta': (0.0, 0.343)}
    factors = {'L0_ffn_wr': 3.686, 'L0_ffn_w1': 4.124, 'L0_ffn_w2': 3.82}
    for name, (base, spread) in spreads.items():
        noise = np.random.default_rng([zlib.crc32(name.encode()), seed]).standard_normal(out[name].shape)
        drawn = base * np.exp(spread * noise) if base else spread * noise
        out[name] = jnp.asarray(drawn.astype(out[name].dtype))
    for name, factor in factors.items():
        out[name] = (out[name] * factor).astype(out[name].dtype)
    return out
```

```python
from contextlib import ExitStack

import concourse.bass as bass
from concourse import mybir

F32 = mybir.dt.float32
BF16 = mybir.dt.bfloat16
I32 = mybir.dt.int32
U32 = mybir.dt.uint32
ALU = mybir.AluOpType
ACT = mybir.ActivationFunctionType
AX = mybir.AxisListType

P = 128
LOG2 = 0.6931471805599453
TWO_PI = 6.283185
ROUND = 12582912.0
LN_EPS = 1e-5
EXP_TOP = float(2 ** 60)
CUTOFF = 10.0
LOW = -3.0e38
FAR = 1000000
LSET = 4
TILES = 50
NPAD = TILES * P
PAIRS = TILES // 2
ROWS, COLS = 125, 800
GRP = 2
SUP = GRP * P
CHUNK = 8


def wait(eng, sem, value):
    if isinstance(value, int) and value <= 0:
        return
    eng.wait_ge(sem, value)


def standing(eng, sem_apart):
    eng.sem_inc(sem_apart, 1)


class Chain:

    def __init__(self, eng, sem):
        self.eng, self.sem, self.n, self.base = eng, sem, 0, 0

    def __call__(self, ins):
        ins.then_inc(self.sem, 1)
        self.n += 1
        self.eng.wait_ge(self.sem, self.base + self.n if not isinstance(self.base, int) else self.n)

    def enter(self, i, first, per_turn):
        self.base, self.at, self.per_turn = (i - first) * per_turn, self.n, per_turn

    def leave(self, turns):
        assert self.n - self.at == self.per_turn, (self.n - self.at, self.per_turn)
        self.n, self.base = self.at + self.per_turn * turns, 0


def gnn_ffn_kernel(nc, x, src, dst, edge_attr, edge_weight, aw_W, aw_b, m1_W, m1_b, m2_W, m2_b,
                   o1_W, o1_b, o2_W, o2_b, wr, br, w1, b1, w2, b2, L_WT, Wr, br1, W1, B1, W2, B2,
                   gamma, beta, out):
    N, H = x.shape
    E, GI = edge_attr.shape
    assert ROWS * COLS == E and NPAD >= N and H == 2 * P
    FULL = N // P
    TAIL = N - FULL * P
    K_SEL = max(1, N // 2) - 1
    NQ = -(-E // SUP) + TILES - 1
    NQ += (-NQ) % LSET
    NEXP = Wr.shape[1]
    FE = W1.shape[2]
    CAPACITY = float(-(-N * 5 // (4 * NEXP)))
    FCH = w1.shape[1] // P

    h1 = nc.dram_tensor("h1", (NPAD, H), F32, kind="Internal").ap()
    h2 = nc.dram_tensor("h2", (NPAD, H), F32, kind="Internal").ap()
    attr_s = nc.dram_tensor("attr_s", (E + SUP, GI), F32, kind="Internal").ap()
    rec_d = nc.dram_tensor("rec_d", (E + SUP, 3), I32, kind="Internal").ap()
    rec_s = nc.dram_tensor("rec_s", (E + SUP, 3), I32, kind="Internal").ap()

    ctx = ExitStack()
    with ctx:
        ctx.enter_context(nc.allow_non_contiguous_dma(reason="bias vectors onto partitions, a few hundred numbers"))
        def sb(name, shape, dt=F32):
            return ctx.enter_context(nc.sbuf_tensor(name, shape, dt))

        def sem(name):
            return ctx.enter_context(nc.semaphore(name))

        X = sb("X", [P, TILES, H])
        XT = sb("XT", [P, 2, NPAD])
        R = sb("R", [P, TILES * H])
        W = sb("W", [P, 7168])

        def col(at, dt=F32, n=COLS):
            v = R[0:ROWS, at:at + n]
            return v if dt is F32 else v.bitcast(dt)

        rec = col(0, I32, 3 * COLS).rearrange("p (c k) -> p c k", k=3)
        recf = col(0, F32, 3 * COLS).rearrange("p (c k) -> p c k", k=3)
        dst_i, src_i, nxt_i = col(2400, I32), col(3200, I32), col(4000, I32)
        ew, tmpc, tmpc_i = col(4800), col(5600), col(5600, I32)
        src_lo, src_hi, dst_hi = col(6400), col(7200), col(8000)
        maskc, maskc_i, scanc, rankc = col(8800), col(8800, I32), col(9600), col(10400)
        pos_src, pos_dst = col(11200, I32), col(12000, I32)
        w1_sb = R[:, 0:2048].rearrange("p (k n) -> p k n", k=2)
        w2_sb = R[:, 2048:4096].rearrange("p (c n) -> p c n", n=H)
        Hb = R[:, 4096:8192].rearrange("p (a c n) -> p a c n", a=2, c=FCH)
        cmpb = R[:, 8192:8192 + 15 * TILES].rearrange("p (j t) -> p j t", t=TILES)
        o1_sb = R[:, 9800:10312].rearrange("p (k n) -> p k n", k=2)
        o2_sb = R[:, 10312:10824].rearrange("p (k n) -> p k n", k=2)
        gates = R[:, 9000:9000 + 16 * TILES].rearrange("p (k t) -> p k t", t=TILES)
        Gt = W[:, 0:2048].rearrange("p (a g n) -> p a g n", a=4, g=GRP)
        Eb1 = W[:, 2048:3072].rearrange("p (a n) -> p a n", a=2)
        Eb2 = W[:, 3072:4096].rearrange("p (a n) -> p a n", a=2)
        S1 = W[:, 4096:5120].rearrange("p (a k n) -> p a k n", a=2, k=2)
        Mb = W[:, 5120:6144].rearrange("p (a g n) -> p a g n", a=2, g=GRP)
        Ob = W[:, 6144:6656].rearrange("p (a g n) -> p a g n", a=2, g=GRP)
        attrT = W[:, 6656:7168].rearrange("p (a n) -> p a n", a=2)
        xn = W[:, 0:512].rearrange("p (a n) -> p a n", a=2)
        xT = W[:, 512:1024].rearrange("p (a k n) -> p a k n", a=2, k=2)
        ob = W[:, 1024:1536].rearrange("p (a n) -> p a n", a=2)
        tmp = W[:, 1536:2048]
        Mq = W[:, 2560:2560 + NQ]
        dcast, vcast = W[:, 3072:3200], W[:, 3200:3328]
        iota_i = W[:, 3328:3840].bitcast(I32)
        node_i = W[:, 3840:3840 + TILES].bitcast(I32)

        attr = sb("attr", [P, LSET, GRP * GI])
        erec = sb("erec", [P, LSET, GRP * 3], I32)
        stat = sb("stat", [P, TILES, 6])
        st = sb("st", [P, 4, TILES])
        mean, rstd, vtmp, dtmp = (st[:, k, :] for k in range(4))
        wA = sb("wA", [P, 2, H])
        m1e = sb("m1e", [GI + 1, H])
        m2_sb = sb("m2_sb", [P, 2, H])
        rowA = sb("rowA", [P, H])
        rowB = sb("rowB", [P, H])
        rowC = sb("rowC", [P, H])
        rowD = sb("rowD", [P, H])
        bcol = sb("bcol", [P, 16])
        b2row = sb("b2row", [3, H])
        b2spl = sb("b2spl", [3, H], BF16)
        ones_b = sb("ones_b", [3, P], BF16)
        iota_f = sb("iota_f", [P, 512])
        iota_b = sb("iota_b", [P, P], BF16)
        pidx_i = sb("pidx_i", [P, 1], I32)
        pidx = sb("pidx", [P, 1])
        valid = sb("valid", [P, TILES])
        ident = sb("ident", [P, P])
        tri = sb("tri", [P, P])
        ones = sb("ones", [P, P])
        iota16 = sb("iota16", [P, 16], I32)
        offs_i = sb("offs_i", [P, NQ], I32)
        blk_i = sb("blk_i", [P, NQ], I32)
        nbase = sb("nbase", [P, NQ])
        cnt = sb("cnt", [P, 2, TILES])
        tot = sb("tot", [P, 2, TILES])
        s50 = sb("s50", [P, 8, TILES])
        s50_i = sb("s50_i", [P, TILES], I32)
        zero50 = sb("zero50", [P, TILES])
        off0 = sb("off0", [P, TILES])
        c1 = sb("c1", [P, 8])
        flag_i = sb("flag_i", [P, 1], I32)
        ohl = sb("ohl", [P, 2, P], BF16)
        ohh = sb("ohh", [P, 2, TILES], BF16)
        rs = sb("rs", [P, TILES])
        rs_t = sb("rs_t", [P, TILES])
        wrt = sb("wrt", [P, TILES])
        gate = sb("gate", [P, TILES])
        key_i = sb("key_i", [P, 4, 16], I32)
        dl = sb("dl", [P, 2, GRP])
        sidx = sb("sidx", [P, CHUNK], I32)
        srec = sb("srec", [P, CHUNK, 3], I32)
        sm = sb("sm", [1, 12, NEXP])
        sm_i = sb("sm_i", [1, NEXP], U32)
        ex_i = sb("ex_i", [1, 2], I32)
        zst = sb("zst", [1, 4])
        WrS = sb("WrS", [P, 2, NEXP])

        bank = [ctx.enter_context(nc.psum_tensor(f"bank{k}", [P, 512], F32)) for k in range(8)]

        s_phase = sem("s_phase")
        s_const = sem("s_const")
        s_dve = sem("s_dve")
        s_act = sem("s_act")
        s_pe = sem("s_pe")
        s_edges = sem("s_edges")
        s_big = sem("s_big")
        s_x = sem("s_x")
        s_w = sem("s_w")
        s_wo = sem("s_wo")
        s_w2 = sem("s_w2")
        s_w3 = sem("s_w3")
        s_w4 = sem("s_w4")
        s_w5 = sem("s_w5")
        s_zero = sem("s_zero")
        s_sent = sem("s_sent")
        s_cosv = sem("s_cosv")
        s_cos = sem("s_cos")
        s_recs = sem("s_recs")
        s_cnt = sem("s_cnt")
        s_tot = sem("s_tot")
        s_flag = sem("s_flag")
        s_ctr = sem("s_ctr")
        s_dstpos = sem("s_dstpos")
        s_dorder = sem("s_dorder")
        s_srcpos = sem("s_srcpos")
        s_ohl = sem("s_ohl")
        s_deg = sem("s_deg")
        s_sel = sem("s_sel")
        s_scat = sem("s_scat")
        s_gl = sem("s_gl")
        s_mq = sem("s_mq")
        s_mqp = sem("s_mqp")
        s_sched = sem("s_sched")
        s_var = sem("s_var")
        s_rstd = sem("s_rstd")
        s_ld = [sem(f"s_ld{k}") for k in range(LSET)]
        s_ldr = [sem(f"s_ldr{k}") for k in range(LSET)]
        s_g = [sem(f"s_g{k}") for k in range(LSET)]
        names = ("T cT L1 exp1 clamp1 ln1 S1 L2 exp2 clamp2 ln2 max2 oh msg agg add").split()
        e1 = {n: sem("e1_" + n) for n in names}
        e2 = {n: sem("e2_" + n) for n in ("oh", "agg", "add", "g")}
        p1 = {n: sem("p1_" + n) for n in ("xn", "T", "cT", "mm", "out")}
        p2 = {n: sem("p2_" + n) for n in ("xn", "T", "cT", "mm", "out")}
        n2 = {n: sem("n2_" + n) for n in ("xn", "T", "cT", "use")}
        n3 = {n: sem("n3_" + n) for n in ("xn", "T", "cT", "use")}
        s_h = [[sem(f"s_h{k}{a}") for a in range(2)] for k in range(3)]
        o = {n: sem("o_" + n) for n in ("L1", "exp", "clamp", "ln", "S", "L2", "add")}
        f1 = {n: sem("f1_" + n) for n in ("L1", "act", "L2", "y")}
        f2 = {n: sem("f2_" + n) for n in ("L1", "act", "L2", "y")}
        s_ctrd, s_ctr2, s_ctp, s_dvu, s_dl, s_jk = (sem("s_" + n) for n in ("degree", "topk", "topp", "dvu", "dl", "jk"))
        s_tmp, s_x1, s_y2, s_zz, s_z = (sem("s_" + n) for n in ("tmp", "x1", "y2", "zz", "z"))
        apart_pe, apart_pool, apart_dve = (sem("apart_" + n) for n in ("pe", "pool", "dve"))
        s_stage, s_att, s_perm = (sem("s_" + n) for n in ("stage", "att", "perm"))

        def phase_end(eng, k):
            eng.drain().then_inc(s_phase, 1)
            eng.wait_ge(s_phase, 5 * (k + 1))

        block = ctx.enter_context(nc.Block())

        def at(s, u, d=0):
            k = s + d
            u = u + k // LSET
            return u * LSET + k % LSET, u, k % LSET

        def steps(eng, step, *parts):
            lo, hi = max(k for _, k in parts) + 2, NQ + min(k for _, k in parts)
            names = lambda s: tuple(n for n, k in parts if 0 <= s - k < NQ)
            for s in range(min(k for _, k in parts), lo):
                step(s, 0, names(s))
            turns = (hi - lo) // LSET
            with eng.Fori(0, turns) as u:
                for j in range(LSET):
                    step(lo + j, u, names(lo))
            for s in range(lo + turns * LSET, NQ + max(k for _, k in parts)):
                step(s, 0, names(s))

        def pair_steps(eng, step):
            for q in range(3):
                step(q, q % 2, ("L1", "L2") if q else ("L1",))
            with eng.Fori(0, (PAIRS - 3) // 2) as u:
                for j in range(2):
                    step(u * 2 + 3 + j, (1 + j) % 2, ("L1", "L2"))
            step(PAIRS, PAIRS % 2, ("L2",))

        @block.sync
        def _(eng):
            eng.wait_ge(s_big, 1)
            two = lambda a: a.rearrange("(p c) -> p c", c=COLS)
            eng.dma_start(dst_i, two(dst)).then_inc(s_edges, 16)
            eng.dma_start(src_i, two(src)).then_inc(s_edges, 16)
            eng.dma_start(nxt_i[0:ROWS - 1, :], two(dst[1:1 + (ROWS - 1) * COLS])).then_inc(s_edges, 16)
            eng.dma_start(nxt_i[ROWS - 1:ROWS, 0:COLS - 1],
                          dst[1 + (ROWS - 1) * COLS:E].rearrange("(p c) -> p c", p=1)).then_inc(s_edges, 16)
            eng.dma_start(ew, two(edge_weight)).then_inc(s_edges, 16)
            eng.dma_start(X[:, 0:FULL, :], x[0:FULL * P, :].rearrange("(t p) f -> p t f", p=P)).then_inc(s_x, 16)
            eng.wait_ge(s_zero, 1)
            eng.dma_start(X[0:TAIL, FULL, :], x[FULL * P:N, :]).then_inc(s_x, 16)
            eng.wait_ge(s_zero, 4)
            eng.dma_start(attr_s[E:E + SUP, :].rearrange("(p g) f -> p (g f)", g=GRP), attr[:, 0, :]).then_inc(s_sent, 16)
            for k, r in enumerate((rec_d, rec_s)):
                eng.dma_start(r[E:E + SUP, :].rearrange("(p g) f -> p (g f)", g=GRP), erec[:, k, :]).then_inc(s_sent, 16)

            def store_h(table, s_out, s_dma):
                def store(t, u, a):
                    wait(eng, s_out, t + 1)
                    eng.dma_start(table[bass.ds(t * P, P), :], ob[:, a, :]).then_inc(s_dma[a], 16)
                with eng.Fori(0, PAIRS) as u:
                    for a in range(2):
                        store(u * 2 + a, u, a)
                for a in range(2):
                    eng.wait_ge(s_dma[a], 16 * PAIRS)

            store_h(h1, p1["out"], s_h[0])
            eng.wait_ge(s_sent, 48)
            eng.wait_ge(s_dorder, 1)
            phase_end(eng, 0)

            def load1(q, u, a):
                if not isinstance(q, int) or q >= LSET:
                    eng.wait_ge(e1["T"], q - LSET + 1)
                    eng.wait_ge(e1["msg"], q - LSET + 1)
                s = eng.value_load(offs_i[0:1, bass.ds(q, 1)], min_val=0, max_val=E)
                eng.dma_start(attr[:, a, :], attr_s[bass.ds(s, SUP), :].rearrange("(p g) f -> p (g f)", g=GRP))\
                   .then_inc(s_ld[a], 16)
                eng.dma_start(erec[:, a, :], rec_d[bass.ds(s, SUP), :].rearrange("(p g) f -> p (g f)", g=GRP))\
                   .then_inc(s_ldr[a], 16)

            for a in range(LSET):
                load1(a, 0, a)
            with eng.Fori(1, NQ // LSET) as u:
                for a in range(LSET):
                    load1(u * LSET + a, u, a)
            phase_end(eng, 1)
            for k in range(2, 5):
                phase_end(eng, k)
            store_h(h2, p2["out"], s_h[1])
            phase_end(eng, 5)

            def load2(q, u, a):
                if not isinstance(q, int) or q >= LSET:
                    eng.wait_ge(e2["oh"], q - LSET + 1)
                    eng.wait_ge(s_g[a], 32 * (NQ // LSET) + 32 * u)
                s = eng.value_load(offs_i[0:1, bass.ds(q, 1)], min_val=0, max_val=E)
                eng.dma_start(erec[:, a, :], rec_s[bass.ds(s, SUP), :].rearrange("(p g) f -> p (g f)", g=GRP))\
                   .then_inc(s_ldr[a], 16)

            for a in range(LSET):
                load2(a, 0, a)
            with eng.Fori(1, NQ // LSET) as u:
                for a in range(LSET):
                    load2(u * LSET + a, u, a)
            phase_end(eng, 6)
            eng.wait_ge(s_sel, 1)
            for j in range(2):
                e = eng.value_load(ex_i[0:1, j:j + 1], min_val=0, max_val=NEXP - 1)
                eng.dma_start(w1_sb[:, :, j * FE:(j + 1) * FE],
                              W1[bass.ds(e, 1), :, :].rearrange("e (k p) n -> p (e k) n", p=P)).then_inc(s_w4, 16)
                eng.dma_start(w2_sb[:, 4 * j:4 * j + 4, :],
                              W2[bass.ds(e, 1), :, :].rearrange("e (c p) n -> p (e c) n", p=P)).then_inc(s_w4, 16)
                eng.dma_start(bcol[:, 8 + 4 * j:12 + 4 * j],
                              B1[bass.ds(e, 1), :].rearrange("e (c p) -> p (e c)", p=P)).then_inc(s_w4, 16)
                eng.dma_start(rowC[:, :] if j == 0 else rowD[:, :],
                              B2[bass.ds(e, 1), :].to_broadcast([P, H])).then_inc(s_w4, 16)
            phase_end(eng, 7)

            def store_out(t, a):
                eng.wait_ge(f2["y"], t + PAIRS + 1)
                return ob[:, a, :]
            with eng.Fori(0, FULL // 2) as u:
                for a in range(2):
                    v = store_out(u * 2 + a, a)
                    eng.dma_start(out[bass.ds((u * 2 + a) * P, P), :], v).then_inc(s_h[2][a], 16)
            v = store_out(FULL, 0)
            eng.dma_start(out[FULL * P:N, :], v[0:TAIL, :]).then_inc(s_h[2][0], 16)
            eng.wait_ge(s_h[2][0], 16 * (FULL // 2 + 1))
            eng.wait_ge(s_h[2][1], 16 * (FULL // 2))
            phase_end(eng, 8)

        @block.gpsimd
        def _(eng):
            eng.memset(col(4000, I32), FAR).then_inc(s_big, 1)
            eng.memset(X[:, FULL:TILES, :], 0.0).then_inc(s_zero, 1)
            eng.memset(attr[:, 0, :], 0.0).then_inc(s_zero, 1)
            eng.memset(erec[:, 0:2, :], 0).then_inc(s_gl, 1)
            eng.wait_ge(s_gl, 1)
            eng.memset(erec[:, 0, :].rearrange("p (g k) -> p g k", k=3)[:, :, 1], FAR).then_inc(s_zero, 1)
            eng.memset(erec[:, 1, :].rearrange("p (g k) -> p g k", k=3)[:, :, 0], FAR).then_inc(s_zero, 1)
            eng.iota(iota_i[:, :], [[1, 512]], base=0, channel_multiplier=0).then_inc(s_const, 1)
            eng.iota(pidx_i[:, :], [[0, 1]], base=0, channel_multiplier=1).then_inc(s_const, 1)
            eng.iota(node_i[:, :], [[P, TILES]], base=0, channel_multiplier=1).then_inc(s_const, 1)
            eng.memset(ones[:, :], 1.0).then_inc(s_const, 1)
            eng.memset(ones_b[:, :], 1.0).then_inc(s_const, 1)
            eng.memset(zero50[:, :], 0.0).then_inc(s_const, 1)
            eng.memset(cnt[:, :, :], 0.0).then_inc(s_const, 1)
            eng.memset(XT[:, :, :], 0.0).then_inc(s_zero, 1)
            eng.memset(attrT[:, :, :], 1.0).then_inc(s_const, 1)

            eng.wait_ge(s_recs, 1)
            eng.wait_ge(s_flag, 1)
            unsorted = eng.value_load(flag_i[0:1, 0:1], min_val=0, max_val=1)
            with eng.If(unsorted > 0):
                eng.wait_ge(s_dstpos, 1)
                ev = edge_attr.rearrange("(p c) f -> p c f", c=COLS)
                staged = W[0:ROWS, 2048:2048 + CHUNK * GI].rearrange("p (c f) -> p c f", f=GI)
                with eng.Fori(0, COLS // CHUNK) as t:
                    eng.tensor_copy(sidx[0:ROWS, :], pos_dst[:, bass.ds(t * CHUNK, CHUNK)]).then_inc(s_stage, 1)
                    eng.tensor_copy(srec[0:ROWS, :, :], rec[:, bass.ds(t * CHUNK, CHUNK), :]).then_inc(s_stage, 1)
                    eng.dma_start(staged, ev[:, bass.ds(t * CHUNK, CHUNK), :]).then_inc(s_att, 16)
                    eng.wait_ge(s_stage, t * 2 + 2)
                    eng.wait_ge(s_att, t * 16 + 16)
                    standing(eng, apart_pool)
                    for c in range(CHUNK):
                        where = bass.IndirectOffsetOnAxis(ap=sidx[0:ROWS, c:c + 1], axis=0)
                        eng.indirect_dma_start(out=rec_d[:, :], out_offset=where, in_=srec[0:ROWS, c, :],
                                               in_offset=None).then_inc(s_perm, 16)
                        eng.indirect_dma_start(out=attr_s[:, :], out_offset=where, in_=staged[:, c, :],
                                               in_offset=None).then_inc(s_perm, 16)
                    eng.wait_ge(s_perm, (t + 1) * (32 * CHUNK))
            with eng.Else():
                eng.dma_start(rec_d[0:E, :].rearrange("(p c) k -> p c k", c=COLS), rec).then_inc(s_perm, 16)
                eng.dma_start(attr_s[0:E, :].rearrange("(p c) f -> p (c f)", c=COLS),
                              edge_attr.rearrange("(p c) f -> p (c f)", c=COLS)).then_inc(s_perm, 16)
                eng.wait_ge(s_perm, 32)
            eng.sem_inc(s_dorder, 1)
            phase_end(eng, 0)

            eng.wait_ge(s_srcpos, 1)

            def gather1(q, u, a):
                eng.wait_ge(s_ldr[a], u * 16 + 16)
                if not isinstance(q, int) or q >= LSET:
                    eng.wait_ge(e1["msg"], q - LSET + 1)
                standing(eng, apart_pool)
                for g in range(GRP):
                    where = bass.IndirectOffsetOnAxis(ap=erec[:, a, 3 * g:3 * g + 1], axis=0)
                    eng.indirect_dma_start(out=Gt[:, a, g, :], out_offset=None, in_=h1[:, :],
                                           in_offset=where).then_inc(s_g[a], 16)

            def scatter_src(t):
                eng.wait_ge(s_gl, t * 2 + 3)
                standing(eng, apart_pool)
                for c in range(CHUNK):
                    where = bass.IndirectOffsetOnAxis(ap=sidx[0:ROWS, c:c + 1], axis=0)
                    eng.indirect_dma_start(out=rec_s[:, :], out_offset=where, in_=srec[0:ROWS, c, :],
                                           in_offset=None).then_inc(s_scat, 16)

            def stage_src(t):
                if not isinstance(t, int) or t > 0:
                    eng.wait_ge(s_scat, t * (16 * CHUNK))
                eng.tensor_copy(sidx[0:ROWS, :], pos_src[:, bass.ds(t * CHUNK, CHUNK)]).then_inc(s_gl, 1)
                eng.tensor_copy(srec[0:ROWS, :, :], rec[:, bass.ds(t * CHUNK, CHUNK), :]).then_inc(s_gl, 1)

            CH = COLS // CHUNK
            assert CH <= NQ // LSET

            def turn1(u):
                stage_src(u)
                for a in range(LSET):
                    gather1(u * LSET + a, u, a)
                    if a == 1:
                        scatter_src(u)

            turn1(0)
            with eng.Fori(1, CH) as u:
                turn1(u)
            with eng.Fori(CH, NQ // LSET) as u:
                for a in range(LSET):
                    gather1(u * LSET + a, u, a)
            eng.wait_ge(s_scat, 16 * COLS)
            phase_end(eng, 1)
            for k in range(2, 6):
                phase_end(eng, k)

            def gather2(q, u, a):
                eng.wait_ge(s_ldr[a], u * 16 + 16 * (NQ // LSET) + 16)
                if not isinstance(q, int) or q >= LSET:
                    eng.wait_ge(e2["agg"], q - LSET + 1)
                standing(eng, apart_pool)
                for g in range(GRP):
                    where = bass.IndirectOffsetOnAxis(ap=erec[:, a, 3 * g + 1:3 * g + 2], axis=0)
                    eng.indirect_dma_start(out=Gt[:, a, g, :], out_offset=None, in_=h2[:, :],
                                           in_offset=where).then_inc(s_g[a], 16)

            for a in range(LSET):
                gather2(a, 0, a)
            with eng.Fori(1, NQ // LSET) as u:
                for a in range(LSET):
                    gather2(u * LSET + a, u, a)
            for k in range(6, 9):
                phase_end(eng, k)

        @block.scalar
        def _(eng):
            chain = Chain(eng, s_act)
            mat = lambda a: a.rearrange("(k p) n -> p k n", p=P)
            line = lambda a: a.rearrange("(e n) -> e n", e=1)
            down = lambda a: a.rearrange("(c p) -> p c", p=P)
            for t, v in ((wA, mat(aw_W)), (m2_sb, mat(m2_W)), (WrS, mat(Wr))):
                eng.dma_start(t[:, :, :], v).then_inc(s_w, 16)
            eng.dma_start(m1e[0:GI, :], m1_W).then_inc(s_w, 16)
            eng.dma_start(m1e[GI:GI + 1, :], line(m1_b)).then_inc(s_w, 16)
            eng.dma_start(bcol[:, 0:2], down(o1_b)).then_inc(s_w, 16)
            eng.dma_start(b2row[:, :], line(m2_b).to_broadcast([3, H])).then_inc(s_w, 16)
            eng.dma_start(rowA[:, :], line(aw_b).to_broadcast([P, H])).then_inc(s_w, 16)
            eng.dma_start(rowB[:, :], line(o2_b).to_broadcast([P, H])).then_inc(s_w, 16)
            eng.dma_start(rowD[:, :], wr.rearrange("f e -> e f").to_broadcast([P, H])).then_inc(s_w, 16)
            eng.dma_start(c1[:, 7:8], br.rearrange("(e n) -> e n", e=1).to_broadcast([P, 1])).then_inc(s_w, 16)
            eng.dma_start(sm[0:1, 11, :], line(br1)).then_inc(s_w, 16)
            eng.wait_ge(s_cosv, 1)
            eng.activation(tmpc, ew, ACT.Sin, scale=TWO_PI).then_inc(s_cos, 1)
            eng.wait_ge(s_deg, 2)
            eng.activation(rs[:, :], rs_t[:, :], ACT.Sqrt).then_inc(s_deg, 1)

            def root(k):
                eng.wait_ge(s_var, k)
                eng.activation(rstd, vtmp, ACT.Sqrt).then_inc(s_rstd, 1)

            def transposed(s, dest, limit=None):
                def step(t, a):
                    eng.wait_ge(s["T"], t + 1)
                    if limit is not None:
                        wait(eng, s[limit], t - 1)
                    eng.activation(dest(t, a), bank[a][:, 0:H].rearrange("p (k n) -> p k n", k=2),
                                   ACT.Copy).then_inc(s["cT"], 1)
                for a in range(2):
                    step(a, a)
                with eng.Fori(1, PAIRS) as u:
                    for a in range(2):
                        step(u * 2 + a, a)

            root(1)
            transposed(p1, lambda t, a: xT[:, a, :, :], "mm")
            phase_end(eng, 0)

            eng.preload_act_table_set("natural_log_exp_and_others")

            def step1(s, u, do):
                q, _, a = at(s, u)
                b = a % 2
                if "exp1" in do:
                    eng.wait_ge(e1["L1"], q + 1)
                    wait(eng, e1["S1"], q - 1)
                    eng.activation(Eb1[:, b, :], bank[2 + b][:, :], ACT.Exp).then_inc(e1["exp1"], 1)
                q1, _, a1 = at(s, u, -1)
                b1_ = a1 % 2
                if "exp2" in do:
                    eng.wait_ge(e1["L2"], q1 + 1)
                    wait(eng, e1["msg"], q1 - 1)
                    eng.activation(Eb2[:, b1_, :], bank[4 + b1_][:, :], ACT.Exp).then_inc(e1["exp2"], 1)
                if "exp1" in do:
                    eng.wait_ge(e1["clamp1"], q + 1)
                    eng.activation(Eb1[:, b, :], Eb1[:, b, :], ACT.Ln, bias=1.0).then_inc(e1["ln1"], 1)
                if "exp2" in do:
                    eng.wait_ge(e1["clamp2"], q1 + 1)
                    eng.activation(Eb2[:, b1_, :], Eb2[:, b1_, :], ACT.Ln, bias=1.0).then_inc(e1["ln2"], 1)
                q2, _, a2 = at(s, u, 2)
                b2_ = a2 % 2
                if "copy" in do:
                    eng.wait_ge(e1["T"], q2 + 1)
                    wait(eng, e1["L1"], q2 - 1)
                    eng.activation(attrT[0:GI, b2_, :], bank[b2_][0:GI, 0:256],
                                   ACT.Copy).then_inc(e1["cT"], 1)

            steps(eng, step1, ("exp1", 0), ("exp2", 1), ("copy", -2))
            phase_end(eng, 1)

            eng.dma_start(o1_sb, mat(o1_W)).then_inc(s_wo, 16)
            eng.dma_start(o2_sb, mat(o2_W)).then_inc(s_wo, 16)

            def out1(q, b, do):
                if "L1" in do:
                    eng.wait_ge(o["L1"], q + 1)
                    wait(eng, o["S"], q - 1)
                    for h in range(2):
                        ins = eng.activation(Eb1[:, b, h * 256:h * 256 + 256],
                                             bank[2 + b][:, h * 256:h * 256 + 256], ACT.Exp, bias=bcol[:, h:h + 1])
                    ins.then_inc(o["exp"], 1)
                    eng.wait_ge(o["clamp"], q + 1)
                    eng.activation(Eb1[:, b, :], Eb1[:, b, :], ACT.Ln, bias=1.0).then_inc(o["ln"], 1)

            for q in range(3):
                out1(q, q % 2, ("L1",))
            with eng.Fori(0, (PAIRS - 3) // 2) as u:
                for j in range(2):
                    out1(u * 2 + 3 + j, (1 + j) % 2, ("L1",))
            phase_end(eng, 2)
            eng.dma_start(w1_sb, mat(w1)).then_inc(s_w2, 16)
            eng.dma_start(w2_sb, w2.rearrange("(c p) n -> p c n", p=P)).then_inc(s_w2, 16)
            eng.dma_start(bcol[:, 8:16], down(b1)).then_inc(s_w2, 16)
            eng.dma_start(rowC[:, :], line(b2).to_broadcast([P, H])).then_inc(s_w2, 16)
            eng.dma_start(wA[:, :, :], mat(L_WT)).then_inc(s_w2, 16)
            root(2)
            block_of = lambda t, a: XT[:, :, bass.ds(t * P, P)]
            transposed(n2, block_of)
            eng.wait_ge(s_w2, 80)
            phase_end(eng, 3)

            def ffn_act(f, func):
                def step(q, b):
                    for c in range(FCH):
                        m = FCH * q + c
                        eng.wait_ge(f["L1"], m + 1)
                        if c == 0:
                            wait(eng, f["L2"], q - 1)
                        eng.activation(Hb[:, b, c, :], bank[c % 6][:, 0:256], func,
                                       bias=bcol[:, 8 + c:9 + c]).then_inc(f["act"], 1)
                for q in range(3):
                    step(q, q % 2)
                with eng.Fori(0, (PAIRS - 3) // 2) as u:
                    for j in range(2):
                        step(u * 2 + 3 + j, (1 + j) % 2)

            ffn_act(f1, ACT.Gelu_apprx_tanh)
            phase_end(eng, 4)
            root(3)
            eng.dma_start(rowA[:, :], line(gamma).to_broadcast([P, H])).then_inc(s_w3, 16)
            eng.dma_start(rowB[:, :], line(beta).to_broadcast([P, H])).then_inc(s_w3, 16)
            transposed(p2, lambda t, a: xT[:, a, :, :], "mm")
            eng.wait_ge(s_w3, 32)
            phase_end(eng, 5)
            phase_end(eng, 6)
            root(4)
            transposed(n3, block_of)
            for k in range(3):
                eng.wait_ge(s_w5, k + 1)
                n = 2 if k == 2 else NEXP
                eng.activation(sm[0:1, 3, 0:n], sm[0:1, 2, 0:n], ACT.Exp).then_inc(s_mqp, 1)
            phase_end(eng, 7)
            ffn_act(f2, ACT.Gelu)
            root(5)
            phase_end(eng, 8)

        @block.tensor
        def _(eng):
            eng.wait_ge(s_w, 16 * 12)
            eng.wait_ge(s_const, 8)
            eng.wait_ge(s_cnt, 1)
            for k in range(2):
                eng.matmul(bank[6][0:3, 0:H], ones[:, 0:3], m2_sb[:, k, :], start=(k == 0), stop=(k == 1))
            eng.drain().then_inc(s_pe, 1)
            eng.wait_ge(s_cnt, 2)
            eng.matmul(bank[5][:, 0:TILES], ones[0:ROWS, :], cnt[0:ROWS, 0, :], start=True, stop=True)
            eng.matmul(bank[5][:, 64:64 + TILES], ones[0:ROWS, :], cnt[0:ROWS, 1, :], start=True, stop=True)
            eng.matmul(bank[5][:, 128:129], ones[0:ROWS, :], c1[0:ROWS, 0:1], start=True, stop=True)
            eng.matmul(bank[5][0:ROWS, 192:192 + TILES], tri[0:ROWS, 0:ROWS], cnt[0:ROWS, 0, :], start=True, stop=True)
            eng.matmul(bank[5][0:ROWS, 256:256 + TILES], tri[0:ROWS, 0:ROWS], cnt[0:ROWS, 1, :], start=True, stop=True)\
               .then_inc(s_tot, 1)

            def schedule(k):
                eng.wait_ge(s_mq, k)
                eng.matmul(bank[6][:, 0:NQ], dcast[:, :], Mq[:, :], start=True, stop=True)
                eng.matmul(bank[7][:, 0:NQ], vcast[:, :], Mq[:, :], start=True, stop=True).then_inc(s_sched, 1)

            schedule(1)

            def degree(c, b, first=False, last=False):
                eng.wait_ge(s_ohl, c + 1)
                eng.matmul(bank[4][:, 0:TILES], ohl[0:ROWS, b, :], ohh[0:ROWS, b, :], start=first, stop=last)\
                   .then_inc(s_ctrd, 1)
            degree(0, 0, first=True)
            degree(1, 1)
            with eng.Fori(1, COLS // 2 - 1) as u:
                for b in range(2):
                    degree(u * 2 + b, b)
            degree(COLS - 2, 0)
            degree(COLS - 1, 1, last=True)

            def transposes(s, t, a):
                eng.wait_ge(s["xn"], t + 1)
                wait(eng, s["cT"], t - 1)
                for k in range(2):
                    ins = eng.transpose(bank[a][:, k * P:(k + 1) * P], xn[:, a, k * P:(k + 1) * P], ident[:, :])
                ins.then_inc(s["T"], 1)

            def product(s, t, a):
                eng.wait_ge(s["cT"], t + 1)
                wait(eng, s["out"], t - 1)
                for k in range(2):
                    ins = eng.matmul(bank[2 + a][:, 0:H], xT[:, a, k, :], wA[:, k, :], start=(k == 0), stop=(k == 1))
                ins.then_inc(s["mm"], 1)

            def node_products(s):
                transposes(s, 0, 0)
                transposes(s, 1, 1)
                product(s, 0, 0)

                def pair(u):
                    for a in range(2):
                        transposes(s, u * 2 + a, a)
                        product(s, u * 2 + a - 1, 1 - a)

                pair(1)
                with eng.Fori(2, PAIRS) as u:
                    pair(u)
                product(s, TILES - 1, 1)

            node_products(p1)
            phase_end(eng, 0)

            def step1(s, u, do):
                q1, _, a1 = at(s, u, -1)
                b = a1 % 2
                if "L2" in do:
                    eng.wait_ge(e1["S1"], q1 + 1)
                    wait(eng, e1["max2"], q1 - 1)
                    for g in range(GRP):
                        v = bank[4 + b][:, g * H:(g + 1) * H]
                        for k in range(2):
                            eng.matmul(v, S1[:, b, k, g * P:(g + 1) * P], m2_sb[:, k, :], start=(k == 0), stop=False)
                        ins = eng.matmul(v, ones_b[:, :], b2spl[:, :], start=False, stop=True)
                    ins.then_inc(e1["L2"], 1)
                q2, _, a2 = at(s, u, -2)
                b = a2 % 2
                if "agg" in do:
                    eng.wait_ge(e1["msg"], q2 + 1)
                    eng.wait_ge(e1["oh"], q2 + 1)
                    wait(eng, e1["add"], q2 - 1)
                    for h in range(2):
                        for g in range(GRP):
                            ins = eng.matmul(bank[6 + b][:, h * P:(h + 1) * P], Mb[:, b, g, h * P:(h + 1) * P],
                                             Ob[:, b, g, :], start=(g == 0), stop=(g == GRP - 1))
                    ins.then_inc(e1["agg"], 1)
                q3, u3, a3 = at(s, u, 2)
                b = a3 % 2
                if "T" in do:
                    eng.wait_ge(s_ld[a3], u3 * 16 + 16)
                    wait(eng, e1["cT"], q3 - 1)
                    standing(eng, apart_pe)
                    for g in range(GRP):
                        ins = eng.transpose(bank[b][0:GI, g * P:(g + 1) * P],
                                            attr[:, a3, g * GI:(g + 1) * GI], ident[:, :])
                    ins.then_inc(e1["T"], 1)
                q4, _, a4 = at(s, u, 1)
                b = a4 % 2
                if "L1" in do:
                    eng.wait_ge(e1["cT"], q4 + 1)
                    wait(eng, e1["S1"], q4 - 1)
                    for h in range(2):
                        ins = eng.matmul(bank[2 + b][:, h * 256:h * 256 + 256], m1e[:, h * P:(h + 1) * P],
                                         attrT[0:GI + 1, b, :], start=True, stop=True)
                    ins.then_inc(e1["L1"], 1)

            steps(eng, step1, ("L2", 1), ("agg", 2), ("T", -2), ("L1", -1))
            phase_end(eng, 1)

            eng.wait_ge(s_wo, 32)
            for k in range(2):
                ins = eng.matmul(bank[7][:, 0:H], ones[:, :], o2_sb[:, k, :], start=(k == 0), stop=(k == 1))
            ins.then_inc(s_pe, 1)

            def out1(q, b, do):
                if "L1" in do:
                    wait(eng, o["S"], q - 1)
                    for h in range(2):
                        for k in range(2):
                            ins = eng.matmul(bank[2 + b][:, h * 256:h * 256 + 256], o1_sb[:, k, h * P:(h + 1) * P],
                                             XT[:, k, bass.ds(q * 256, 256)], start=(k == 0), stop=(k == 1))
                    ins.then_inc(o["L1"], 1)
                if "L2" in do:
                    r, c = q - 1, 1 - b
                    eng.wait_ge(o["S"], r + 1)
                    wait(eng, o["add"], r - 1)
                    for g in range(2):
                        for k in range(2):
                            ins = eng.matmul(bank[4 + c][:, g * H:(g + 1) * H], S1[:, c, k, g * P:(g + 1) * P],
                                             o2_sb[:, k, :], start=(k == 0), stop=(k == 1))
                    ins.then_inc(o["L2"], 1)

            pair_steps(eng, out1)
            phase_end(eng, 2)

            def norm_transposes(s):
                for a in range(2):
                    transposes(s, a, a)
                with eng.Fori(1, PAIRS) as u:
                    for a in range(2):
                        transposes(s, u * 2 + a, a)

            norm_transposes(n2)
            for r in range(8):
                eng.wait_ge(s_ctr2, r + 1)
                eng.matmul(bank[4][:, 0:15], ones[:, :], gates[:, 8, 0:15], start=True, stop=True).then_inc(s_ctp, 1)
            eng.wait_ge(s_ctr2, 9)
            eng.matmul(bank[4][:, 0:TILES], ones[:, :], gates[:, 0, :], start=True, stop=True)
            eng.matmul(bank[4][:, 64:64 + TILES], ones[:, :], gates[:, 1, :], start=True, stop=True)
            eng.matmul(bank[4][:, 128:128 + TILES], tri[:, :], gates[:, 1, :], start=True, stop=True).then_inc(s_ctp, 1)
            phase_end(eng, 3)

            def ffn(f):
                def step(q, b, do):
                    if "L1" in do:
                        for c in range(FCH):
                            m = FCH * q + c
                            wait(eng, f["act"], m - 5 if c >= 6 else (m - FCH + (6 if c < 2 else 0) + 1))
                            for k in range(2):
                                ins = eng.matmul(bank[c % 6][:, 0:256], w1_sb[:, k, c * P:(c + 1) * P],
                                                 XT[:, k, bass.ds(q * 256, 256)], start=(k == 0), stop=(k == 1))
                            ins.then_inc(f["L1"], 1)
                    if "L2" in do:
                        r, d = q - 1, 1 - b
                        eng.wait_ge(f["act"], r * FCH + FCH)
                        wait(eng, f["y"], r - 1)
                        for g in range(2):
                            for c in range(FCH):
                                ins = eng.matmul(bank[6 + d][:, g * H:(g + 1) * H], Hb[:, d, c, g * P:(g + 1) * P],
                                                 w2_sb[:, c, :], start=(c == 0), stop=(c == FCH - 1))
                        ins.then_inc(f["L2"], 1)
                pair_steps(eng, step)

            ffn(f1)
            phase_end(eng, 4)
            schedule(2)
            node_products(p2)
            phase_end(eng, 5)

            def agg2(q, u, a):
                b = a % 2
                eng.wait_ge(s_g[a], u * 32 + 32 * (NQ // LSET) + 32)
                eng.wait_ge(e2["oh"], q + 1)
                wait(eng, e2["add"], q - 1)
                for g in range(GRP):
                    ins = eng.matmul(bank[b][:, 0:H], Ob[:, b, g, :], Gt[:, a, g, :], start=(g == 0), stop=(g == GRP - 1))
                ins.then_inc(e2["agg"], 1)

            for a in range(LSET):
                agg2(a, 0, a)
            with eng.Fori(1, NQ // LSET) as u:
                for a in range(LSET):
                    agg2(u * LSET + a, u, a)
            phase_end(eng, 6)
            norm_transposes(n3)
            eng.wait_ge(s_ctr2, 10)
            for k in range(2):
                ins = eng.matmul(bank[4][0:1, 0:NEXP], c1[:, k:k + 1], WrS[:, k, :], start=(k == 0), stop=(k == 1))
            ins.then_inc(s_ctp, 1)
            eng.wait_ge(s_ctr2, 11)
            eng.matmul(bank[4][:, 64:66], ones[0:1, :], sm[0:1, 8, 0:2], start=True, stop=True).then_inc(s_ctp, 1)
            phase_end(eng, 7)
            ffn(f2)
            phase_end(eng, 8)

        @block.vector
        def _(eng):
            chain = Chain(eng, s_dve)
            eng.wait_ge(s_const, 3)
            chain(eng.tensor_copy(iota_f[:, :], iota_i[:, :]))
            chain(eng.tensor_copy(pidx[:, :], pidx_i[:, :]))
            chain(eng.tensor_copy(iota_b[:, :], iota_i[:, 0:P]))
            chain(eng.tensor_scalar(ident[:, :], iota_f[:, 0:P], pidx[:, 0:1], None, ALU.is_equal))
            chain(eng.tensor_scalar(tri[:, :], iota_f[:, 0:P], pidx[:, 0:1], None, ALU.is_gt))
            chain(eng.tensor_scalar(valid[:, :], node_i[:, :], float(N), None, ALU.is_lt))
            chain(eng.tensor_copy(iota16[:, :], iota_i[:, 0:16]))
            eng.sem_inc(s_cnt, 1)
            eng.wait_ge(s_edges, 80)
            eng.wait_ge(s_const, 7)
            chain(eng.tensor_tensor(maskc, dst_i, nxt_i, ALU.is_gt))
            chain(eng.tensor_reduce(c1[0:ROWS, 0:1], maskc, AX.X, ALU.add))
            chain(eng.tensor_scalar(ew, ew, 0.5 / CUTOFF, 0.25, ALU.mult, ALU.add))
            chain(eng.tensor_scalar(tmpc, ew, ROUND, None, ALU.add))
            chain(eng.tensor_scalar(tmpc, tmpc, ROUND, None, ALU.subtract))
            chain(eng.tensor_tensor(ew, ew, tmpc, ALU.subtract))
            eng.sem_inc(s_cosv, 1)
            chain(eng.tensor_copy(rec[:, :, 0], src_i))
            chain(eng.tensor_copy(rec[:, :, 1], dst_i))
            chain(eng.tensor_scalar(nxt_i, dst_i, 7, None, ALU.logical_shift_right))
            chain(eng.tensor_copy(dst_hi, nxt_i))
            chain(eng.tensor_scalar(nxt_i, src_i, 7, None, ALU.logical_shift_right))
            chain(eng.tensor_copy(src_hi, nxt_i))
            chain(eng.tensor_scalar(nxt_i, src_i, P - 1, None, ALU.bitwise_and))
            chain(eng.tensor_copy(src_lo, nxt_i))
            eng.wait_ge(s_cos, 1)
            chain(eng.tensor_scalar(recf[:, :, 2], tmpc, 0.5, 0.5, ALU.mult, ALU.add))
            eng.sem_inc(s_recs, 1)

            for k, key in ((0, dst_hi), (1, src_hi)):
                with eng.Fori(0, TILES) as b:
                    chain.enter(b, 0, 1)
                    chain(eng.tensor_scalar(maskc, key, iota_f[0:ROWS, bass.ds(b, 1)], 0.0, ALU.is_equal,
                                            ALU.add, accum_out=cnt[0:ROWS, k, bass.ds(b, 1)]))
                chain.leave(TILES)
            eng.sem_inc(s_cnt, 1)
            eng.wait_ge(s_pe, 1)
            eng.wait_ge(s_w, 16 * 12)
            chain(eng.scalar_tensor_tensor(b2row[:, :], bank[6][0:3, 0:H], -LOG2, b2row[:, :], ALU.mult, ALU.add))
            part = rowC[0:3, :]
            chain(eng.memset(part, 0.0))
            for k in range(3):
                chain(eng.tensor_copy(b2spl[:, :], b2row[:, :]))
                chain(eng.tensor_tensor(b2row[:, :], b2row[:, :], b2spl[:, :], ALU.subtract))
                chain(eng.tensor_scalar(c1[0:3, 1:2], pidx[0:3, :], float(k), None, ALU.is_equal))
                chain(eng.scalar_tensor_tensor(part, b2spl[:, :], c1[0:3, 1:2], part, ALU.mult, ALU.add))
            chain(eng.tensor_copy(b2spl[:, :], part))
            eng.wait_ge(s_tot, 1)
            chain(eng.tensor_copy(tot[:, :, :], bank[5][:, 0:128].rearrange("p (k t) -> p k t", k=2)[:, :, 0:TILES]))
            chain(eng.tensor_scalar(flag_i[:, :], bank[5][:, 128:129], 0.5, None, ALU.is_gt))
            eng.sem_inc(s_flag, 1)

            def first_of(row, k):
                chain(eng.tensor_tensor_scan(s50[:, 6, :], tot[:, k, :], zero50[:, :], 0.0, ALU.add, ALU.add))
                chain(eng.tensor_tensor(row, s50[:, 6, :], tot[:, k, :], ALU.subtract))

            def schedule(k, turn):
                start, tiles, first, base, delta = (s50[:, j, :] for j in range(5))
                first_of(start, k)
                chain(eng.tensor_scalar(s50_i[:, :], tot[:, k, :], float(SUP - 1), None, ALU.add))
                chain(eng.tensor_scalar(s50_i[:, :], s50_i[:, :], SUP.bit_length() - 1, None, ALU.logical_shift_right))
                chain(eng.tensor_copy(tiles, s50_i[:, :]))
                chain(eng.tensor_tensor_scan(s50[:, 6, :], tiles, zero50[:, :], 0.0, ALU.add, ALU.add))
                chain(eng.tensor_tensor(first, s50[:, 6, :], tiles, ALU.subtract))
                chain(eng.scalar_tensor_tensor(base, first, float(-SUP), start, ALU.mult, ALU.add))
                chain(eng.tensor_copy(delta, base))
                chain(eng.tensor_tensor(delta[:, 1:TILES], base[:, 1:TILES], base[:, 0:TILES - 1], ALU.subtract))
                for v, c in ((first, 2), (delta, 3)):
                    chain(eng.tensor_tensor(s50[:, 5, :], v, ident[:, 0:TILES], ALU.mult))
                    chain(eng.tensor_reduce(c1[:, c:c + 1], s50[:, 5, :], AX.X, ALU.add))
                chain(eng.tensor_scalar(vcast, pidx[:, 0:1].to_broadcast([P, P]), float(TILES), None, ALU.is_lt))
                chain(eng.tensor_scalar(dcast[:, :], c1[:, 3:4].to_broadcast([P, P]), 0.0, None, ALU.add))
                chain(eng.tensor_scalar(Mq[:, :], iota_f[:, 0:NQ], c1[:, 2:3], None, ALU.is_ge))
                eng.sem_inc(s_mq, 1)
                eng.wait_ge(s_sched, turn)
                chain(eng.scalar_tensor_tensor(nbase[:, :], iota_f[:, 0:NQ], float(SUP), bank[6][:, 0:NQ],
                                               ALU.mult, ALU.add))
                chain(eng.tensor_scalar(offs_i[:, :], nbase[:, :], float(E), None, ALU.min))
                chain(eng.tensor_scalar(blk_i[:, :], bank[7][:, 0:NQ], -1.0, None, ALU.add))
                chain(eng.tensor_scalar(nbase[:, :], bank[7][:, 0:NQ], -float(P), float(P), ALU.mult, ALU.add))

            schedule(0, 1)

            def places(link, key, k, pos, off_at):
                link(eng.tensor_tensor_scan(s50[:, 6, :], tot[:, k, :], zero50[:, :], 0.0, ALU.add, ALU.add))
                link(eng.tensor_tensor(s50[:, 0, :], s50[:, 6, :], tot[:, k, :], ALU.subtract))
                link(eng.scalar_tensor_tensor(off0[0:ROWS, :], bank[5][0:ROWS, off_at:off_at + TILES], -1.0,
                                              s50[0:ROWS, 0, :], ALU.add, ALU.add))
                link(eng.memset(tmpc, 0.0))
                link(eng.memset(rankc, 0.0))
                with eng.Fori(0, TILES) as b:
                    link.enter(b, 0, 3)
                    link(eng.tensor_scalar(maskc, key, iota_f[0:ROWS, bass.ds(b, 1)], None, ALU.is_equal))
                    link(eng.tensor_tensor_scan(scanc, maskc, tmpc, off0[0:ROWS, bass.ds(b, 1)], ALU.add, ALU.add))
                    standing(eng, apart_dve)
                    link(eng.copy_predicated(rankc, maskc_i, scanc))
                link.leave(TILES)
                link(eng.tensor_copy(pos, rankc))

            unsorted = eng.value_load(flag_i[0:1, 0:1], min_val=0, max_val=1)
            with eng.If(unsorted > 0):
                places(Chain(eng, s_dvu), dst_hi, 0, pos_dst, 192)
                eng.sem_inc(s_dstpos, 1)
            with eng.Else():
                eng.sem_inc(s_dstpos, 1)
            places(chain, src_hi, 1, pos_src, 256)
            eng.sem_inc(s_srcpos, 1)

            def one_hots(c, b):
                wait(eng, s_ctrd, c - 1)
                eng.tensor_scalar(ohl[0:ROWS, b, :], iota_b[0:ROWS, :], src_lo[:, bass.ds(c, 1)], None, ALU.is_equal)
                eng.tensor_scalar(ohh[0:ROWS, b, :], iota_b[0:ROWS, 0:TILES], src_hi[:, bass.ds(c, 1)], None,
                                  ALU.is_equal).then_inc(s_ohl, 1)
            for b in range(2):
                one_hots(b, b)
            with eng.Fori(1, COLS // 2) as u:
                for b in range(2):
                    one_hots(u * 2 + b, b)
            eng.wait_ge(s_ctrd, COLS)
            chain(eng.tensor_scalar(rs_t[:, :], bank[4][:, 0:TILES], 1.0, None, ALU.add))
            chain(eng.reciprocal(rs_t[:, :], rs_t[:, :]))
            eng.sem_inc(s_deg, 2)
            eng.wait_ge(s_deg, 3)

            def statistics(turn, tile):
                with eng.Fori(0, TILES) as t:
                    chain.enter(t, 0, 1)
                    chain(eng.bn_stats(stat[:, bass.ds(t, 1), :].rearrange("p a k -> p (a k)"), tile(t)))
                chain.leave(TILES)
                combine(turn)

            def combine(turn):
                me, mo, ve, vo = (stat[:, :, k] for k in (1, 4, 2, 5))
                chain(eng.tensor_tensor(mean, me, mo, ALU.add))
                chain(eng.tensor_tensor(dtmp, me, mo, ALU.subtract))
                chain(eng.tensor_tensor(vtmp, ve, vo, ALU.add))
                chain(eng.tensor_scalar(mean, mean, 0.5, None, ALU.mult))
                chain(eng.tensor_tensor(dtmp, dtmp, dtmp, ALU.mult))
                chain(eng.tensor_scalar(dtmp, dtmp, 0.25, LN_EPS, ALU.mult, ALU.add))
                chain(eng.scalar_tensor_tensor(vtmp, vtmp, 1.0 / H, dtmp, ALU.mult, ALU.add))
                chain(eng.reciprocal(vtmp, vtmp))
                eng.sem_inc(s_var, 1)
                eng.wait_ge(s_rstd, turn)
                chain(eng.tensor_tensor(rstd, rstd, valid[:, :], ALU.mult))

            tile_of_x = lambda t: X[:, bass.ds(t, 1), :].rearrange("p a n -> p (a n)")

            def normed(dest, t, source=None):
                return eng.tensor_scalar(dest, source if source is not None else tile_of_x(t),
                                         mean[:, bass.ds(t, 1)], rstd[:, bass.ds(t, 1)], ALU.subtract, ALU.mult)

            def node_tiles(s, s_dma, finish):
                def norm(t, a):
                    wait(eng, s["T"], t - 1)
                    normed(xn[:, a, :], t).then_inc(s["xn"], 1)

                def finished(t, a, stored=0):
                    eng.wait_ge(s["mm"], t + 1)
                    wait(eng, s_dma[a], stored)
                    finish(t, a)

                norm(0, 0)
                norm(1, 1)
                finished(0, 0)
                norm(2, 0)
                finished(1, 1)
                with eng.Fori(1, PAIRS - 1) as u:
                    norm(u * 2 + 1, 1)
                    finished(u * 2, 0, u * 16)
                    norm(u * 2 + 2, 0)
                    finished(u * 2 + 1, 1, u * 16)
                norm(TILES - 1, 1)
                finished(TILES - 2, 0, 16 * (PAIRS - 1))
                finished(TILES - 1, 1, 16 * (PAIRS - 1))

            eng.wait_ge(s_x, 32)
            statistics(1, tile_of_x)

            def finish1(t, a):
                eng.tensor_tensor(ob[:, a, :], bank[2 + a][:, 0:H], rowA[:, :], ALU.add).then_inc(p1["out"], 1)

            node_tiles(p1, s_h[0], finish1)
            phase_end(eng, 0)

            def step1(s, u, do):
                q0, _, a0 = at(s, u)
                b0 = a0 % 2
                q1, u1, a1 = at(s, u, -1)
                b1_ = a1 % 2
                q2, _, a2 = at(s, u, -2)
                b2_ = a2 % 2
                if "one" in do:
                    eng.wait_ge(e1["exp1"], q0 + 1)
                    eng.tensor_scalar(Eb1[:, b0, :], Eb1[:, b0, :], EXP_TOP, None, ALU.min).then_inc(e1["clamp1"], 1)
                if "two" in do:
                    eng.wait_ge(e1["exp2"], q1 + 1)
                    eng.tensor_scalar(Eb2[:, b1_, :], Eb2[:, b1_, :], EXP_TOP, None, ALU.min).then_inc(e1["clamp2"], 1)
                if "one" in do:
                    eng.wait_ge(e1["ln1"], q0 + 1)
                    wait(eng, e1["L2"], q0 - 1)
                    eng.tensor_tensor(S1[:, b0, :, :], bank[2 + b0][:, :].rearrange("p (k n) -> p k n", k=2),
                                      Eb1[:, b0, :].rearrange("p (k n) -> p k n", k=2), ALU.max).then_inc(e1["S1"], 1)
                if "two" in do:
                    eng.wait_ge(s_ldr[a1], u1 * 16 + 16)
                    wait(eng, e1["agg"], q1 - 1)
                    er = erec[:, a1, :].rearrange("p (g k) -> p g k", k=3)
                    eng.tensor_tensor(dl[:, b1_, :], er[:, :, 1], nbase[:, bass.ds(q1, 1)].to_broadcast([P, GRP]),
                                      ALU.add).then_inc(s_dl, 1)
                    eng.wait_ge(s_dl, q1 + 1)
                    for g in range(GRP):
                        ins = eng.tensor_scalar(Ob[:, b1_, g, :], iota_f[:, 0:P], dl[:, b1_, g:g + 1],
                                                erec[:, a1, 3 * g + 2:3 * g + 3].bitcast(F32), ALU.is_equal, ALU.mult)
                    ins.then_inc(e1["oh"], 1)
                    eng.wait_ge(e1["ln2"], q1 + 1)
                    eng.tensor_tensor(Eb2[:, b1_, :], bank[4 + b1_][:, :], Eb2[:, b1_, :], ALU.max).then_inc(e1["max2"], 1)
                if "add" in do:
                    r = eng.value_load(blk_i[0:1, bass.ds(q2, 1)], min_val=0, max_val=TILES - 1)
                    eng.wait_ge(e1["agg"], q2 + 1)
                    wait(eng, e1["add"], q2)
                    v = XT[:, :, bass.ds(r * P, P)]
                    eng.tensor_tensor(v, bank[6 + b2_][:, 0:256].rearrange("p (h n) -> p h n", h=2), v,
                                      ALU.add).then_inc(e1["add"], 1)
                if "two" in do:
                    eng.wait_ge(s_g[a1], u1 * 32 + 32)
                    eng.wait_ge(e1["max2"], q1 + 1)
                    eng.scalar_tensor_tensor(Mb[:, b1_, :, :].rearrange("p g n -> p (g n)"), Eb2[:, b1_, :], -LOG2,
                                             Gt[:, a1, :, :].rearrange("p g n -> p (g n)"), ALU.add, ALU.mult)\
                       .then_inc(e1["msg"], 1)

            steps(eng, step1, ("one", 0), ("two", 1), ("add", 2))
            phase_end(eng, 1)

            eng.wait_ge(s_pe, 2)
            chain(eng.scalar_tensor_tensor(rowB[:, :], bank[7][:, 0:H], -LOG2, rowB[:, :], ALU.mult, ALU.add))

            def out1(q, b, do):
                if "L1" in do:
                    eng.wait_ge(o["exp"], q + 1)
                    eng.tensor_scalar(Eb1[:, b, :], Eb1[:, b, :], EXP_TOP, None, ALU.min).then_inc(o["clamp"], 1)
                if "L2" in do:
                    r, c = q - 1, 1 - b
                    eng.wait_ge(o["L2"], r + 1)
                    wait(eng, o["add"], r)
                    v = X[:, bass.ds(r * 2, 2), :]
                    t3 = tmp.rearrange("p (g n) -> p g n", g=2)
                    eng.tensor_tensor(t3, bank[4 + c][:, :].rearrange("p (g n) -> p g n", g=2),
                                      rowB[:, :].unsqueeze(1).to_broadcast([P, 2, H]), ALU.add).then_inc(s_tmp, 1)
                    eng.wait_ge(s_tmp, r + 1)
                    eng.tensor_tensor(v, v, t3, ALU.add).then_inc(o["add"], 1)
                if "L1" in do:
                    eng.wait_ge(o["ln"], q + 1)
                    wait(eng, o["L2"], q - 1)
                    for h in range(2):
                        ins = eng.scalar_tensor_tensor(S1[:, b, h, :], bank[2 + b][:, h * 256:h * 256 + 256],
                                                       bcol[:, h:h + 1], Eb1[:, b, h * 256:h * 256 + 256],
                                                       ALU.add, ALU.max)
                    ins.then_inc(o["S"], 1)

            pair_steps(eng, out1)
            phase_end(eng, 2)

            statistics(2, tile_of_x)

            def norm2(t, a):
                wait(eng, n2["T"], t - 1)
                normed(xn[:, a, :], t).then_inc(n2["xn"], 1)
                eng.wait_ge(n2["xn"], t + 1)
                eng.tensor_tensor(tile_of_x(t), tile_of_x(t), xn[:, a, :], ALU.add).then_inc(n2["use"], 1)
                wait(eng, s_jk, t)
                eng.scalar_tensor_tensor(tmp[:, 0:H], xn[:, a, :], 1.0, rowD[:, :], ALU.mult, ALU.mult,
                                         accum_out=wrt[:, bass.ds(t, 1)]).then_inc(s_jk, 1)

            for a in range(2):
                norm2(a, a)
            with eng.Fori(1, PAIRS) as u:
                for a in range(2):
                    norm2(u * 2 + a, a)
            eng.wait_ge(s_jk, TILES)
            chain(eng.tensor_scalar(wrt[:, :], wrt[:, :], c1[:, 7:8], None, ALU.add))
            chain(eng.tensor_tensor(gates[:, 2, :], wrt[:, :], valid[:, :], ALU.mult))
            chain(eng.tensor_scalar(gates[:, 3, :], valid[:, :], -LOW, LOW, ALU.mult, ALU.add))
            chain(eng.tensor_tensor(gates[:, 2, :], gates[:, 2, :], gates[:, 3, :], ALU.add))
            cand, sign, best, digit = (key_i[:, k, 0:15] for k in range(4))
            chain(eng.memset(best, 0))
            for r in range(8):
                shift = 28 - 4 * r
                chain(eng.tensor_scalar(cand, iota16[:, 1:16], shift, None, ALU.logical_shift_left))
                chain(eng.tensor_tensor(cand, cand, best, ALU.bitwise_or))
                chain(eng.tensor_scalar(cand, cand, -2 ** 31, None, ALU.bitwise_xor))
                chain(eng.tensor_scalar(sign, cand, 31, 2 ** 31 - 1, ALU.arith_shift_right, ALU.bitwise_and))
                chain(eng.tensor_tensor(cand, cand, sign, ALU.bitwise_xor))
                chain(eng.tensor_tensor(cmpb, gates[:, 2, :].unsqueeze(1).to_broadcast([P, 15, TILES]),
                                        cand.bitcast(F32).unsqueeze(2).to_broadcast([P, 15, TILES]), ALU.is_ge))
                chain(eng.tensor_reduce(gates[:, 8, 0:15], cmpb, AX.X, ALU.add))
                eng.sem_inc(s_ctr2, 1)
                eng.wait_ge(s_ctp, r + 1)
                chain(eng.tensor_scalar(gates[:, 9, 0:15], bank[4][:, 0:15], float(K_SEL), None, ALU.is_ge))
                chain(eng.tensor_reduce(c1[:, 4:5], gates[:, 9, 0:15], AX.X, ALU.add))
                chain(eng.tensor_copy(digit, c1[:, 4:5].to_broadcast([P, 15])))
                chain(eng.tensor_scalar(digit, digit, shift, None, ALU.logical_shift_left))
                chain(eng.tensor_tensor(best, best, digit, ALU.bitwise_or))
            chain(eng.tensor_scalar(cand, best, -2 ** 31, None, ALU.bitwise_xor))
            chain(eng.tensor_scalar(sign, cand, 31, 2 ** 31 - 1, ALU.arith_shift_right, ALU.bitwise_and))
            chain(eng.tensor_tensor(cand, cand, sign, ALU.bitwise_xor))
            least = cand.bitcast(F32)[:, 0:1]
            chain(eng.tensor_scalar(gates[:, 0, :], gates[:, 2, :], least, None, ALU.is_gt))
            chain(eng.tensor_scalar(gates[:, 1, :], gates[:, 2, :], least, None, ALU.is_equal))
            eng.sem_inc(s_ctr2, 1)
            eng.wait_ge(s_ctp, 9)
            chain(eng.tensor_copy(gates[:, 4, :], bank[4][:, 64:64 + TILES]))
            chain(eng.tensor_tensor_scan(gates[:, 5, :], gates[:, 4, :], zero50[:, :], 0.0, ALU.add, ALU.add))
            chain(eng.tensor_tensor(gates[:, 5, :], gates[:, 5, :], gates[:, 4, :], ALU.subtract))
            chain(eng.tensor_tensor(gates[:, 5, :], gates[:, 5, :], bank[4][:, 128:128 + TILES], ALU.add))
            chain(eng.tensor_reduce(c1[:, 5:6], bank[4][:, 0:TILES], AX.X, ALU.add))
            chain(eng.tensor_scalar(gates[:, 5, :], gates[:, 5, :], c1[:, 5:6], None, ALU.add))
            chain(eng.tensor_scalar(gates[:, 5, :], gates[:, 5, :], float(K_SEL), None, ALU.is_lt))
            chain(eng.tensor_tensor(gates[:, 5, :], gates[:, 5, :], gates[:, 1, :], ALU.mult))
            chain(eng.tensor_tensor(gates[:, 5, :], gates[:, 5, :], gates[:, 0, :], ALU.add))
            chain(eng.tensor_tensor(gate[:, :], gates[:, 5, :], wrt[:, :], ALU.mult))
            phase_end(eng, 3)

            def ffn1(q, b, do):
                if "L2" in do:
                    r, c = q - 1, 1 - b
                    eng.wait_ge(f1["L2"], r + 1)
                    wait(eng, s_x1, r * 2)
                    t3 = tmp.rearrange("p (g n) -> p g n", g=2)
                    eng.tensor_tensor(t3, bank[6 + c][:, :].rearrange("p (g n) -> p g n", g=2),
                                      rowC[:, :].unsqueeze(1).to_broadcast([P, 2, H]), ALU.add).then_inc(f1["y"], 1)
                    eng.wait_ge(f1["y"], r + 1)
                    for g in range(2):
                        v = tile_of_x(r * 2 + g)
                        eng.scalar_tensor_tensor(v, tmp[:, g * H:(g + 1) * H], gate[:, bass.ds(r * 2 + g, 1)], v,
                                                 ALU.mult, ALU.add).then_inc(s_x1, 1)

            pair_steps(eng, ffn1)
            phase_end(eng, 4)
            schedule(1, 2)
            statistics(3, tile_of_x)

            def finish2(t, a):
                eng.tensor_scalar(ob[:, a, :], bank[2 + a][:, 0:H], rs[:, bass.ds(t, 1)], None, ALU.mult)\
                   .then_inc(p2["out"], 1)
                eng.wait_ge(p2["out"], t + 1)
                eng.scalar_tensor_tensor(tile_of_x(t), ob[:, a, :], rs[:, bass.ds(t, 1)], tile_of_x(t),
                                         ALU.mult, ALU.add)

            node_tiles(p2, s_h[1], finish2)
            phase_end(eng, 5)

            def hot2(q, u, a):
                b = a % 2
                eng.wait_ge(s_ldr[a], u * 16 + 16 * (NQ // LSET) + 16)
                wait(eng, e2["agg"], q - 1)
                er = erec[:, a, :].rearrange("p (g k) -> p g k", k=3)
                eng.tensor_tensor(dl[:, b, :], er[:, :, 0], nbase[:, bass.ds(q, 1)].to_broadcast([P, GRP]),
                                  ALU.add).then_inc(s_dl, 1)
                eng.wait_ge(s_dl, q + NQ + 1)
                for g in range(GRP):
                    ins = eng.tensor_scalar(Ob[:, b, g, :], iota_f[:, 0:P], dl[:, b, g:g + 1], None, ALU.is_equal)
                ins.then_inc(e2["oh"], 1)

            def add2(q, u, a):
                b = a % 2
                r = eng.value_load(blk_i[0:1, bass.ds(q, 1)], min_val=0, max_val=TILES - 1)
                eng.wait_ge(e2["agg"], q + 1)
                wait(eng, e2["add"], q)
                v = X[:, bass.ds(r, 1), :].rearrange("p a n -> p (a n)")
                eng.scalar_tensor_tensor(v, bank[b][:, 0:H], rs[:, bass.ds(r, 1)], v, ALU.mult, ALU.add)\
                   .then_inc(e2["add"], 1)

            hot2(0, 0, 0)
            for a in range(1, LSET):
                hot2(a, 0, a)
                add2(a - 1, 0, a - 1)
            with eng.Fori(1, NQ // LSET) as u:
                for a in range(LSET):
                    hot2(u * LSET + a, u, a)
                    add2(u * LSET + a - 1, u, (a - 1) % LSET)
            add2(NQ - 1, NQ // LSET - 1, LSET - 1)
            phase_end(eng, 6)

            statistics(4, tile_of_x)

            def norm3(t, a):
                wait(eng, n3["T"], t - 1)
                normed(xn[:, a, :], t).then_inc(n3["xn"], 1)

            for a in range(2):
                norm3(a, a)
            with eng.Fori(1, PAIRS) as u:
                for a in range(2):
                    norm3(u * 2 + a, a)
            eng.wait_ge(n3["cT"], TILES)
            chain(eng.tensor_reduce(c1[:, 0:2], XT[:, :, :], AX.X, ALU.add))
            chain(eng.tensor_scalar(c1[:, 0:2], c1[:, 0:2], 1.0 / N, None, ALU.mult))
            eng.sem_inc(s_ctr2, 1)
            eng.wait_ge(s_ctp, 10)
            row = lambda k, n=NEXP: sm[0:1, k, 0:n]
            one = lambda k: zst[0:1, k:k + 1]

            def softmax(k, v, n):
                chain(eng.tensor_reduce(one(0), v, AX.X, ALU.max))
                chain(eng.tensor_scalar(row(2, n), v, one(0), None, ALU.subtract))
                eng.sem_inc(s_w5, 1)
                eng.wait_ge(s_mqp, k)
                chain(eng.tensor_reduce(one(1), row(3, n), AX.X, ALU.add))
                chain(eng.reciprocal(one(2), one(1)))
                chain(eng.tensor_scalar(row(4, n), row(3, n), one(2), None, ALU.mult))

            chain(eng.tensor_tensor(row(1), bank[4][0:1, 0:NEXP], row(11), ALU.add))
            softmax(1, row(1), NEXP)
            chain(eng.tensor_scalar(row(5), row(4), float(N), None, ALU.mult))
            chain(eng.reciprocal(row(6), row(5)))
            chain(eng.tensor_scalar(row(6), row(6), CAPACITY, -1.0, ALU.mult, ALU.add))
            chain(eng.tensor_scalar(row(5), row(5), CAPACITY, None, ALU.is_gt))
            chain(eng.tensor_tensor(row(6), row(6), row(5), ALU.mult))
            chain(eng.tensor_scalar(row(6), row(6), 1.0, None, ALU.add))
            chain(eng.tensor_tensor(row(7), row(4), row(6), ALU.mult))
            softmax(2, row(7), NEXP)
            chain(eng.tensor_copy(row(9), row(4)))
            chain(eng.max(row(10), row(9)))
            chain(eng.max_index(sm_i[0:1, :], row(10), row(9)))
            chain(eng.tensor_copy(ex_i[0:1, :], sm_i[0:1, 0:2]))
            eng.sem_inc(s_sel, 1)
            softmax(3, row(10, 2), 2)
            chain(eng.tensor_copy(row(8, 2), row(4, 2)))
            eng.sem_inc(s_ctr2, 1)
            eng.wait_ge(s_ctp, 11)
            chain(eng.tensor_copy(c1[:, 4:6], bank[4][:, 64:66]))
            eng.wait_ge(s_w4, 16 * 8)
            for j in range(2):
                v = w2_sb[:, 4 * j:4 * j + 4, :]
                chain(eng.tensor_scalar(v, v, c1[:, 4 + j:5 + j], None, ALU.mult))
            chain(eng.tensor_scalar(rowC[:, :], rowC[:, :], c1[:, 4:5], None, ALU.mult))
            chain(eng.scalar_tensor_tensor(rowC[:, :], rowD[:, :], c1[:, 5:6], rowC[:, :], ALU.mult, ALU.add))
            phase_end(eng, 7)

            def ffn2(q, b, do):
                if "L2" in do:
                    r, c = q - 1, 1 - b
                    wait(eng, s_z, r * 2)
                    for g in range(2):
                        normed(tmp[:, g * H:(g + 1) * H], r * 2 + g).then_inc(s_y2, 1)
                    eng.wait_ge(f2["L2"], r + 1)
                    eng.wait_ge(s_y2, r * 2 + 2)
                    z = XT[:, :, bass.ds(r * 256, 256)]
                    t3 = tmp.rearrange("p (g n) -> p g n", g=2)
                    eng.tensor_tensor(t3, bank[6 + c][:, :].rearrange("p (g n) -> p g n", g=2), t3,
                                      ALU.add).then_inc(f2["y"], 1)
                    eng.wait_ge(f2["y"], r + 1)
                    eng.tensor_tensor(z, t3, rowC[:, :].unsqueeze(1).to_broadcast([P, 2, H]), ALU.add).then_inc(s_zz, 1)
                    eng.wait_ge(s_zz, r + 1)
                    for g in range(2):
                        eng.bn_stats(stat[:, bass.ds(r * 2 + g, 1), :].rearrange("p a k -> p (a k)"),
                                     XT[:, g, bass.ds(r * 256, 256)]).then_inc(s_z, 1)

            pair_steps(eng, ffn2)
            eng.wait_ge(s_z, TILES)
            combine(5)

            def final(u, g, first):
                t = u * 2 + g
                if not first:
                    eng.wait_ge(s_h[2][g], u * 16)
                v = ob[:, g, :]
                chain(normed(v, t, XT[:, g, bass.ds(u * 256, 256)]))
                chain(eng.tensor_tensor(v, v, rowA[:, :], ALU.mult))
                chain(eng.tensor_tensor(v, v, rowB[:, :], ALU.add))
                chain(eng.tensor_tensor(v, v, tile_of_x(t), ALU.add))
                eng.sem_inc(f2["y"], 1)

            for g in range(2):
                final(0, g, True)
            with eng.Fori(1, FULL // 2) as u:
                chain.enter(u, 1, 8)
                for g in range(2):
                    final(u, g, False)
            chain.leave(FULL // 2 - 1)
            final(FULL // 2, 0, False)
            phase_end(eng, 8)


_INS = ["x", "src", "dst", "edge_attr_50", "edge_weight", "L0_gnn_aw_W", "L0_gnn_aw_b", "L0_gnn_m1_W", "L0_gnn_m1_b",
        "L0_gnn_m2_W", "L0_gnn_m2_b", "L0_gnn_o1_W", "L0_gnn_o1_b", "L0_gnn_o2_W", "L0_gnn_o2_b", "L0_ffn_wr",
        "L0_ffn_br", "L0_ffn_w1", "L0_ffn_b1", "L0_ffn_w2", "L0_ffn_b2", "L1_gnn_W", "L1_ffn_Wr", "L1_ffn_br",
        "L1_ffn_W1", "L1_ffn_b1", "L1_ffn_W2", "L1_ffn_b2", "L1_ffn_gamma", "L1_ffn_beta"]


def kernel(**inputs):
    import numpy as _np
    import concourse.bacc as _bacc
    from concourse import mybir as _mybir
    from concourse.bass_utils import run_bass_kernel_spmd as _run

    nc = _bacc.Bacc("TRN2", target_bir_lowering=False, num_devices=1)
    arrays, args = {}, []
    for name in _INS:
        a = _np.asarray(inputs[name])
        a = _np.ascontiguousarray(a.T if name == "L1_gnn_W" else a)
        arrays[f"in_{name}"] = a
        args.append(nc.dram_tensor(f"in_{name}", a.shape, _mybir.dt.from_np(a.dtype), kind="ExternalInput").ap())
    shape = inputs["x"].shape
    args.append(nc.dram_tensor("out_x", shape, _mybir.dt.float32, kind="ExternalOutput").ap())
    gnn_ffn_kernel(nc, *args)
    r = _run(nc, [arrays], core_ids=[0])
    return r.results[0]["out_x"]
```

```python
from contextlib import ExitStack

import concourse.bass as bass
from concourse import mybir

F32 = mybir.dt.float32
BF16 = mybir.dt.bfloat16
I32 = mybir.dt.int32
U32 = mybir.dt.uint32
ALU = mybir.AluOpType
ACT = mybir.ActivationFunctionType
AX = mybir.AxisListType

P = 128
LOG2 = 0.6931471805599453
TWO_PI = 6.283185
ROUND = 12582912.0
LN_EPS = 1e-5
EXP_TOP = float(2 ** 60)
CUTOFF = 10.0
LOW = -3.0e38
FAR = 1000000
LSET = 8
GSET = 4
TILES = 50
NPAD = TILES * P
PAIRS = TILES // 2
ROWS, COLS = 125, 800
GRP = 2
SUP = GRP * P
CHUNK = 16
NSET = 4


def wait(eng, sem, value):
    if isinstance(value, int) and value <= 0:
        return
    eng.wait_ge(sem, value)


def standing(eng, sem_apart):
    eng.sem_inc(sem_apart, 1)


class Chain:

    def __init__(self, eng, sem):
        self.eng, self.sem, self.n, self.base = eng, sem, 0, 0

    def __call__(self, ins):
        ins.then_inc(self.sem, 1)
        self.n += 1
        self.eng.wait_ge(self.sem, self.base + self.n if not isinstance(self.base, int) else self.n)

    def enter(self, i, first, per_turn):
        self.base, self.at, self.per_turn = (i - first) * per_turn, self.n, per_turn

    def leave(self, turns):
        assert self.n - self.at == self.per_turn, (self.n - self.at, self.per_turn)
        self.n, self.base = self.at + self.per_turn * turns, 0


def gnn_ffn_kernel(nc, x, src, dst, edge_attr, edge_weight, aw_W, aw_b, m1_W, m1_b, m2_W, m2_b,
                   o1_W, o1_b, o2_W, o2_b, wr, br, w1, b1, w2, b2, L_WT, Wr, br1, W1, B1, W2, B2,
                   gamma, beta, out):
    N, H = x.shape
    E, GI = edge_attr.shape
    assert ROWS * COLS == E and NPAD >= N and H == 2 * P
    FULL = N // P
    TAIL = N - FULL * P
    K_SEL = max(1, N // 2) - 1
    NQ = -(-E // SUP) + TILES - 1
    NQ += (-NQ) % LSET
    NEXP = Wr.shape[1]
    FE = W1.shape[2]
    CAPACITY = float(-(-N * 5 // (4 * NEXP)))
    FCH = w1.shape[1] // P
    DCOL = COLS // PAIRS

    h1 = nc.dram_tensor("h1", (NPAD, H), F32, kind="Internal").ap()
    h2 = nc.dram_tensor("h2", (NPAD, H), F32, kind="Internal").ap()
    attr_s = nc.dram_tensor("attr_s", (E + SUP, GI), F32, kind="Internal").ap()
    rec_d = nc.dram_tensor("rec_d", (E + SUP, 3), I32, kind="Internal").ap()
    rec_s = nc.dram_tensor("rec_s", (E + SUP, 3), I32, kind="Internal").ap()

    ctx = ExitStack()
    with ctx:
        ctx.enter_context(nc.allow_non_contiguous_dma(reason="bias vectors onto partitions, a few hundred numbers"))
        def sb(name, shape, dt=F32):
            return ctx.enter_context(nc.sbuf_tensor(name, shape, dt))

        def sem(name):
            return ctx.enter_context(nc.semaphore(name))

        X = sb("X", [P, TILES, H])
        XT = sb("XT", [P, 2, NPAD])
        R = sb("R", [P, TILES * H])
        W = sb("W", [P, 7168])

        def col(at, dt=F32, n=COLS):
            v = R[0:ROWS, at:at + n]
            return v if dt is F32 else v.bitcast(dt)

        dst_i, src_i, nxt_i = col(0, I32), col(800, I32), col(1600, I32)
        ew, tmpc = col(2400), col(3200)
        dst_hi = col(4000, BF16, COLS // 2)
        maskc, maskc_i, scanc, rankc = col(4400), col(4400, I32), col(5200), col(6000)
        pos_dst = col(6800, I32)
        rec = col(8192, I32, 3 * COLS).rearrange("p (c k) -> p c k", k=3)
        recf = col(8192, F32, 3 * COLS).rearrange("p (c k) -> p c k", k=3)
        pos_src = col(10592, I32)
        src_lo, src_hi = col(11392, BF16, COLS // 2), col(11792, BF16, COLS // 2)
        w1_sb = R[:, 0:2048].rearrange("p (k n) -> p k n", k=2)
        w2_sb = R[:, 2048:4096].rearrange("p (c n) -> p c n", n=H)
        Hb = R[:, 4096:8192].rearrange("p (a c n) -> p a c n", a=2, c=FCH)
        o1_sb = R[:, 4096:4608].rearrange("p (k n) -> p k n", k=2)
        o2_sb = R[:, 4608:5120].rearrange("p (k n) -> p k n", k=2)
        Gt = W[:, 0:2048].rearrange("p (a g n) -> p a g n", a=4, g=GRP)
        Eb1 = W[:, 2048:3072].rearrange("p (a n) -> p a n", a=2)
        Eb2 = W[:, 3072:4096].rearrange("p (a n) -> p a n", a=2)
        S1 = W[:, 4096:5120].rearrange("p (a k n) -> p a k n", a=2, k=2)
        Mb = W[:, 5120:6144].rearrange("p (a g n) -> p a g n", a=2, g=GRP)
        Ob = W[:, 6144:6656].rearrange("p (a g n) -> p a g n", a=2, g=GRP)
        attrT = W[:, 6656:7168].rearrange("p (a n) -> p a n", a=2)
        xn = W[:, 0:1024].rearrange("p (a n) -> p a n", a=NSET)
        xT = W[:, 1024:2048].rearrange("p (a k n) -> p a k n", a=NSET, k=2)
        ob = W[:, 2048:3072].rearrange("p (a n) -> p a n", a=NSET)
        tmp = W[:, 3072:3584]
        iota_i = W[:, 3584:4096].bitcast(I32)
        cmpb = W[:, 4096:4096 + 15 * TILES].rearrange("p (j t) -> p j t", t=TILES)
        gates = W[:, 2048:2048 + 16 * TILES].rearrange("p (k t) -> p k t", t=TILES)
        stat = W[:, 5120:5120 + 6 * TILES].rearrange("p (t k) -> p t k", k=6)
        s50 = W[:, 5420:5420 + 8 * TILES].rearrange("p (k t) -> p k t", k=8)
        Mq = W[:, 5824:5824 + NQ]
        dcast, vcast = W[:, 6272:6400], W[:, 6400:6528]
        node_i = W[:, 6528:6528 + TILES].bitcast(I32)
        ohl = [W[:, k:k + DCOL * P // 2].bitcast(BF16).rearrange("p (c n) -> p c n", n=P) for k in (0, 3584)]
        ohh = [W[:, k + DCOL * P // 2:k + DCOL * (P + TILES) // 2].bitcast(BF16).rearrange("p (c n) -> p c n", n=TILES)
               for k in (0, 3584)]

        attr = sb("attr", [P, LSET, GRP * GI])
        erec = sb("erec", [P, LSET, GRP * 3], I32)
        st = sb("st", [P, 4, TILES])
        mean, rstd, vtmp, dtmp = (st[:, k, :] for k in range(4))
        wA = sb("wA", [P, 2, H])
        m1e = sb("m1e", [GI + 1, H])
        m2_sb = sb("m2_sb", [P, 2, H])
        rowA = sb("rowA", [P, H])
        rowB = sb("rowB", [P, H])
        rowC = sb("rowC", [P, H])
        rowD = sb("rowD", [P, H])
        bcol = sb("bcol", [P, 16])
        b2row = sb("b2row", [3, H])
        b2spl = sb("b2spl", [3, H], BF16)
        ones_b = sb("ones_b", [3, P], BF16)
        iota_f = sb("iota_f", [P, 512])
        iota_b = sb("iota_b", [P, P], BF16)
        pidx_i = sb("pidx_i", [P, 1], I32)
        pidx = sb("pidx", [P, 1])
        valid = sb("valid", [P, TILES])
        ident = sb("ident", [P, P])
        tri = sb("tri", [P, P])
        ones = sb("ones", [P, P])
        iota16 = sb("iota16", [P, 16], I32)
        offs_i = sb("offs_i", [P, NQ], I32)
        blk_i = sb("blk_i", [P, NQ], I32)
        nbase = sb("nbase", [P, NQ])
        cnt = sb("cnt", [P, 2, TILES])
        tot = sb("tot", [P, 2, TILES])
        s50_i = sb("s50_i", [P, TILES], I32)
        zero50 = sb("zero50", [P, TILES])
        off0 = sb("off0", [P, TILES])
        c1 = sb("c1", [P, 8])
        flag_i = sb("flag_i", [P, 1], I32)
        rs = sb("rs", [P, TILES])
        rs_t = sb("rs_t", [P, TILES])
        wrt = sb("wrt", [P, TILES])
        gate = sb("gate", [P, TILES])
        key_i = sb("key_i", [P, 4, 16], I32)
        dl = sb("dl", [P, 2, GRP])
        sidx = sb("sidx", [P, CHUNK], I32)
        srec = sb("srec", [P, CHUNK, 3], I32)
        sm = sb("sm", [1, 12, NEXP])
        sm_i = sb("sm_i", [1, NEXP], U32)
        ex_i = sb("ex_i", [1, 2], I32)
        zst = sb("zst", [1, 4])
        WrS = sb("WrS", [P, 2, NEXP])

        bank = [ctx.enter_context(nc.psum_tensor(f"bank{k}", [P, 512], F32)) for k in range(8)]

        s_phase = sem("s_phase")
        s_middle = sem("s_middle")
        s_fill = sem("s_fill")
        s_stat = sem("s_stat")
        s_cnts = sem("s_cnts")
        s_const = sem("s_const")
        s_dve = sem("s_dve")
        s_act = sem("s_act")
        s_pe = sem("s_pe")
        s_edges = sem("s_edges")
        s_big = sem("s_big")
        s_x = sem("s_x")
        s_w = sem("s_w")
        s_wo = sem("s_wo")
        s_w2 = sem("s_w2")
        s_w3 = sem("s_w3")
        s_w4 = sem("s_w4")
        s_w5 = sem("s_w5")
        s_zero = sem("s_zero")
        s_sent = sem("s_sent")
        s_cosv = sem("s_cosv")
        s_cos = sem("s_cos")
        s_recs = sem("s_recs")
        s_cnt = sem("s_cnt")
        s_tot = sem("s_tot")
        s_flag = sem("s_flag")
        s_ctr = sem("s_ctr")
        s_dstpos = sem("s_dstpos")
        s_dorder = sem("s_dorder")
        s_srcpos = sem("s_srcpos")
        s_ohl = sem("s_ohl")
        s_deg = sem("s_deg")
        s_sel = sem("s_sel")
        s_scat = sem("s_scat")
        s_gl = sem("s_gl")
        s_mq = sem("s_mq")
        s_mqp = sem("s_mqp")
        s_sched = sem("s_sched")
        s_var = sem("s_var")
        s_rstd = sem("s_rstd")
        s_ld = [sem(f"s_ld{k}") for k in range(LSET)]
        s_ldr = [sem(f"s_ldr{k}") for k in range(LSET)]
        s_g = [sem(f"s_g{k}") for k in range(GSET)]
        names = ("T cT L1 exp1 clamp1 ln1 S1 L2 exp2 clamp2 ln2 max2 oh msg agg add").split()
        e1 = {n: sem("e1_" + n) for n in names}
        e2 = {n: sem("e2_" + n) for n in ("oh", "agg", "add", "g")}
        p1 = {n: sem("p1_" + n) for n in ("xn", "T", "cT", "mm", "out")}
        p2 = {n: sem("p2_" + n) for n in ("xn", "T", "cT", "mm", "out")}
        n2 = {n: sem("n2_" + n) for n in ("xn", "T", "cT", "use")}
        n3 = {n: sem("n3_" + n) for n in ("xn", "T", "cT", "use")}
        s_h = [[sem(f"s_h{k}{a}") for a in range(4)] for k in range(3)]
        o = {n: sem("o_" + n) for n in ("L1", "exp", "clamp", "ln", "S", "L2", "add")}
        f1 = {n: sem("f1_" + n) for n in ("L1", "act", "L2", "y")}
        f2 = {n: sem("f2_" + n) for n in ("L1", "act", "L2", "y")}
        s_ctrd, s_ctr2, s_ctp, s_dvu, s_dl, s_jk = (sem("s_" + n) for n in ("degree", "topk", "topp", "dvu", "dl", "jk"))
        s_tmp, s_x1, s_y2, s_zz, s_z = (sem("s_" + n) for n in ("tmp", "x1", "y2", "zz", "z"))
        apart_pe, apart_pool, apart_dve = (sem("apart_" + n) for n in ("pe", "pool", "dve"))
        s_stage, s_att, s_perm = (sem("s_" + n) for n in ("stage", "att", "perm"))

        def phase_end(eng, k):
            if k in (2, 3, 4):
                eng.drain().then_inc(s_middle, 1)
                eng.wait_ge(s_middle, 4 * (k - 1))
            else:
                n = k + 1 if k < 2 else k - 2
                eng.drain().then_inc(s_phase, 1)
                eng.wait_ge(s_phase, 5 * n)

        block = ctx.enter_context(nc.Block())

        def at(s, u, d=0, per=LSET):
            k = s + d
            u = u + k // per
            return u * per + k % per, u, k % per

        def gathered(u, a):
            return u * (32 * LSET // GSET) + 32 * (a // GSET + 1)

        def steps(eng, step, *parts, count=NQ, per=LSET, fill=None, fills=0):
            lo, hi = max(k for _, k in parts) + (2 if per == LSET else NSET), count + min(k for _, k in parts)
            names = lambda s: tuple(n for n, k in parts if 0 <= s - k < count)
            for s in range(min(k for _, k in parts), lo):
                step(s, 0, names(s))
            turns = (hi - lo) // per
            assert fills < turns
            if fills:
                with eng.Fori(0, fills) as u:
                    for j in range(per):
                        step(lo + j, u, names(lo))
                        fill(j, u)
            with eng.Fori(fills, turns) as u:
                for j in range(per):
                    step(lo + j, u, names(lo))
            for s in range(lo + turns * per, count + max(k for _, k in parts)):
                step(s, 0, names(s))

        def pair_steps(eng, step):
            for q in range(3):
                step(q, q % 2, ("L1", "L2") if q else ("L1",))
            with eng.Fori(0, (PAIRS - 3) // 2) as u:
                for j in range(2):
                    step(u * 2 + 3 + j, (1 + j) % 2, ("L1", "L2"))
            step(PAIRS, PAIRS % 2, ("L2",))

        @block.sync
        def _(eng):
            eng.wait_ge(s_big, 1)
            two = lambda a: a.rearrange("(p c) -> p c", c=COLS)
            eng.dma_start(dst_i, two(dst)).then_inc(s_edges, 16)
            eng.dma_start(src_i, two(src)).then_inc(s_edges, 16)
            eng.dma_start(nxt_i[0:ROWS - 1, :], two(dst[1:1 + (ROWS - 1) * COLS])).then_inc(s_edges, 16)
            eng.dma_start(nxt_i[ROWS - 1:ROWS, 0:COLS - 1],
                          dst[1 + (ROWS - 1) * COLS:E].rearrange("(p c) -> p c", p=1)).then_inc(s_edges, 16)
            eng.dma_start(ew, two(edge_weight)).then_inc(s_edges, 16)
            eng.dma_start(X[:, 0:FULL, :], x[0:FULL * P, :].rearrange("(t p) f -> p t f", p=P)).then_inc(s_x, 16)
            eng.wait_ge(s_zero, 1)
            eng.dma_start(X[0:TAIL, FULL, :], x[FULL * P:N, :]).then_inc(s_x, 16)
            eng.wait_ge(s_zero, 4)
            eng.dma_start(attr_s[E:E + SUP, :].rearrange("(p g) f -> p (g f)", g=GRP), attr[:, 0, :]).then_inc(s_sent, 16)
            for k, r in enumerate((rec_d, rec_s)):
                eng.dma_start(r[E:E + SUP, :].rearrange("(p g) f -> p (g f)", g=GRP), erec[:, k, :]).then_inc(s_sent, 16)

            def store_h(table, s_out, s_dma):
                def store(s, u, do):
                    t, _, a = at(s, u, per=NSET)
                    eng.wait_ge(s_out, t + 1)
                    eng.dma_start(table[bass.ds(t * P, P), :], ob[:, a, :]).then_inc(s_dma[a], 16)
                steps(eng, store, ("store", 0), count=TILES, per=NSET)
                for a in range(NSET):
                    eng.wait_ge(s_dma[a], 16 * len(range(a, TILES, NSET)))

            store_h(h1, p1["out"], s_h[0])
            eng.wait_ge(s_sent, 48)
            eng.wait_ge(s_dorder, 1)
            phase_end(eng, 0)

            def load1(q, u, a):
                if not isinstance(q, int) or q >= LSET:
                    eng.wait_ge(e1["T"], q - LSET + 1)
                    eng.wait_ge(e1["msg"], q - LSET + 1)
                s = eng.value_load(offs_i[0:1, bass.ds(q, 1)], min_val=0, max_val=E)
                eng.dma_start(attr[:, a, :], attr_s[bass.ds(s, SUP), :].rearrange("(p g) f -> p (g f)", g=GRP))\
                   .then_inc(s_ld[a], 16)
                eng.dma_start(erec[:, a, :], rec_d[bass.ds(s, SUP), :].rearrange("(p g) f -> p (g f)", g=GRP))\
                   .then_inc(s_ldr[a], 16)

            for a in range(LSET):
                load1(a, 0, a)
            with eng.Fori(1, NQ // LSET) as u:
                for a in range(LSET):
                    load1(u * LSET + a, u, a)
            phase_end(eng, 1)
            for k in range(2, 5):
                phase_end(eng, k)
            store_h(h2, p2["out"], s_h[1])
            phase_end(eng, 5)

            def load2(q, u, a):
                if not isinstance(q, int) or q >= LSET:
                    eng.wait_ge(e2["oh"], q - LSET + 1)
                    eng.wait_ge(e2["agg"], q - LSET + 1)
                s = eng.value_load(offs_i[0:1, bass.ds(q, 1)], min_val=0, max_val=E)
                eng.dma_start(erec[:, a, :], rec_s[bass.ds(s, SUP), :].rearrange("(p g) f -> p (g f)", g=GRP))\
                   .then_inc(s_ldr[a], 16)

            for a in range(LSET):
                load2(a, 0, a)
            with eng.Fori(1, NQ // LSET) as u:
                for a in range(LSET):
                    load2(u * LSET + a, u, a)
            phase_end(eng, 6)
            eng.wait_ge(s_sel, 1)
            for j in range(2):
                e = eng.value_load(ex_i[0:1, j:j + 1], min_val=0, max_val=NEXP - 1)
                eng.dma_start(w1_sb[:, :, j * FE:(j + 1) * FE],
                              W1[bass.ds(e, 1), :, :].rearrange("e (k p) n -> p (e k) n", p=P)).then_inc(s_w4, 16)
                eng.dma_start(w2_sb[:, 4 * j:4 * j + 4, :],
                              W2[bass.ds(e, 1), :, :].rearrange("e (c p) n -> p (e c) n", p=P)).then_inc(s_w4, 16)
                eng.dma_start(bcol[:, 8 + 4 * j:12 + 4 * j],
                              B1[bass.ds(e, 1), :].rearrange("e (c p) -> p (e c)", p=P)).then_inc(s_w4, 16)
                eng.dma_start(rowC[:, :] if j == 0 else rowD[:, :],
                              B2[bass.ds(e, 1), :].to_broadcast([P, H])).then_inc(s_w4, 16)
            phase_end(eng, 7)

            def store_out(t, a):
                eng.wait_ge(f2["y"], t + PAIRS + 1)
                return ob[:, a, :]
            with eng.Fori(0, FULL // 2) as u:
                for a in range(2):
                    v = store_out(u * 2 + a, a)
                    eng.dma_start(out[bass.ds((u * 2 + a) * P, P), :], v).then_inc(s_h[2][a], 16)
            v = store_out(FULL, 0)
            eng.dma_start(out[FULL * P:N, :], v[0:TAIL, :]).then_inc(s_h[2][0], 16)
            eng.wait_ge(s_h[2][0], 16 * (FULL // 2 + 1))
            eng.wait_ge(s_h[2][1], 16 * (FULL // 2))
            phase_end(eng, 8)

        @block.gpsimd
        def _(eng):
            eng.memset(nxt_i, FAR).then_inc(s_big, 1)
            eng.memset(X[:, FULL:TILES, :], 0.0).then_inc(s_zero, 1)
            eng.memset(attr[:, 0, :], 0.0).then_inc(s_zero, 1)
            eng.memset(erec[:, 0:2, :], 0).then_inc(s_gl, 1)
            eng.wait_ge(s_gl, 1)
            eng.memset(erec[:, 0, :].rearrange("p (g k) -> p g k", k=3)[:, :, 1], FAR).then_inc(s_zero, 1)
            eng.memset(erec[:, 1, :].rearrange("p (g k) -> p g k", k=3)[:, :, 0], FAR).then_inc(s_zero, 1)
            eng.iota(iota_i[:, :], [[1, 512]], base=0, channel_multiplier=0).then_inc(s_const, 1)
            eng.iota(pidx_i[:, :], [[0, 1]], base=0, channel_multiplier=1).then_inc(s_const, 1)
            eng.iota(node_i[:, :], [[P, TILES]], base=0, channel_multiplier=1).then_inc(s_const, 1)
            eng.memset(ones[:, :], 1.0).then_inc(s_const, 1)
            eng.memset(ones_b[:, :], 1.0).then_inc(s_const, 1)
            eng.memset(zero50[:, :], 0.0).then_inc(s_const, 1)
            eng.memset(cnt[:, :, :], 0.0).then_inc(s_const, 1)
            eng.memset(XT[:, :, :], 0.0).then_inc(s_zero, 1)
            eng.memset(attrT[:, :, :], 1.0).then_inc(s_const, 1)

            eng.wait_ge(s_recs, 1)
            eng.wait_ge(s_flag, 1)
            unsorted = eng.value_load(flag_i[0:1, 0:1], min_val=0, max_val=1)
            with eng.If(unsorted > 0):
                eng.wait_ge(s_dstpos, 1)
                ev = edge_attr.rearrange("(p c) f -> p c f", c=COLS)
                staged = W[0:ROWS, 4096:4096 + CHUNK * GI].rearrange("p (c f) -> p c f", f=GI)
                with eng.Fori(0, COLS // CHUNK) as t:
                    eng.tensor_copy(sidx[0:ROWS, :], pos_dst[:, bass.ds(t * CHUNK, CHUNK)]).then_inc(s_stage, 1)
                    eng.tensor_copy(srec[0:ROWS, :, :], rec[:, bass.ds(t * CHUNK, CHUNK), :]).then_inc(s_stage, 1)
                    eng.dma_start(staged, ev[:, bass.ds(t * CHUNK, CHUNK), :]).then_inc(s_att, 16)
                    eng.wait_ge(s_stage, t * 2 + 2)
                    eng.wait_ge(s_att, t * 16 + 16)
                    standing(eng, apart_pool)
                    for c in range(CHUNK):
                        where = bass.IndirectOffsetOnAxis(ap=sidx[0:ROWS, c:c + 1], axis=0)
                        eng.indirect_dma_start(out=rec_d[:, :], out_offset=where, in_=srec[0:ROWS, c, :],
                                               in_offset=None).then_inc(s_perm, 16)
                        eng.indirect_dma_start(out=attr_s[:, :], out_offset=where, in_=staged[:, c, :],
                                               in_offset=None).then_inc(s_perm, 16)
                    eng.wait_ge(s_perm, (t + 1) * (32 * CHUNK))
            with eng.Else():
                eng.dma_start(rec_d[0:E, :].rearrange("(p c) k -> p c k", c=COLS), rec).then_inc(s_perm, 16)
                eng.dma_start(attr_s[0:E, :].rearrange("(p c) f -> p (c f)", c=COLS),
                              edge_attr.rearrange("(p c) f -> p (c f)", c=COLS)).then_inc(s_perm, 16)
                eng.wait_ge(s_perm, 32)
            eng.sem_inc(s_dorder, 1)
            phase_end(eng, 0)

            def gather1(q, u, a):
                eng.wait_ge(s_ldr[a], u * 16 + 16)
                if not isinstance(q, int) or q >= GSET:
                    eng.wait_ge(e1["msg"], q - GSET + 1)
                standing(eng, apart_pool)
                for g in range(GRP):
                    where = bass.IndirectOffsetOnAxis(ap=erec[:, a, 3 * g:3 * g + 1], axis=0)
                    eng.indirect_dma_start(out=Gt[:, a % GSET, g, :], out_offset=None, in_=h1[:, :],
                                           in_offset=where).then_inc(s_g[a % GSET], 16)

            def scatter_src(t):
                eng.wait_ge(s_gl, t * 2 + 3)
                standing(eng, apart_pool)
                for c in range(CHUNK):
                    where = bass.IndirectOffsetOnAxis(ap=sidx[0:ROWS, c:c + 1], axis=0)
                    eng.indirect_dma_start(out=rec_s[:, :], out_offset=where, in_=srec[0:ROWS, c, :],
                                           in_offset=None).then_inc(s_scat, 16)

            def stage_src(t):
                if not isinstance(t, int) or t > 0:
                    eng.wait_ge(s_scat, t * (16 * CHUNK))
                eng.tensor_copy(sidx[0:ROWS, :], pos_src[:, bass.ds(t * CHUNK, CHUNK)]).then_inc(s_gl, 1)
                eng.tensor_copy(srec[0:ROWS, :, :], rec[:, bass.ds(t * CHUNK, CHUNK), :]).then_inc(s_gl, 1)

            for a in range(LSET):
                gather1(a, 0, a)
            with eng.Fori(1, NQ // LSET) as u:
                for a in range(LSET):
                    gather1(u * LSET + a, u, a)
            phase_end(eng, 1)
            eng.wait_ge(s_srcpos, 1)
            stage_src(0)
            scatter_src(0)
            with eng.Fori(1, COLS // CHUNK) as t:
                stage_src(t)
                scatter_src(t)
            eng.wait_ge(s_scat, 16 * COLS)
            phase_end(eng, 5)

            def gather2(q, u, a):
                eng.wait_ge(s_ldr[a], u * 16 + 16 * (NQ // LSET) + 16)
                if not isinstance(q, int) or q >= GSET:
                    eng.wait_ge(e2["agg"], q - GSET + 1)
                standing(eng, apart_pool)
                for g in range(GRP):
                    where = bass.IndirectOffsetOnAxis(ap=erec[:, a, 3 * g + 1:3 * g + 2], axis=0)
                    eng.indirect_dma_start(out=Gt[:, a % GSET, g, :], out_offset=None, in_=h2[:, :],
                                           in_offset=where).then_inc(s_g[a % GSET], 16)

            for a in range(LSET):
                gather2(a, 0, a)
            with eng.Fori(1, NQ // LSET) as u:
                for a in range(LSET):
                    gather2(u * LSET + a, u, a)
            for k in range(6, 9):
                phase_end(eng, k)

        @block.scalar
        def _(eng):
            chain = Chain(eng, s_act)
            mat = lambda a: a.rearrange("(k p) n -> p k n", p=P)
            line = lambda a: a.rearrange("(e n) -> e n", e=1)
            down = lambda a: a.rearrange("(c p) -> p c", p=P)
            for t, v in ((wA, mat(aw_W)), (m2_sb, mat(m2_W)), (WrS, mat(Wr))):
                eng.dma_start(t[:, :, :], v).then_inc(s_w, 16)
            eng.dma_start(m1e[0:GI, :], m1_W).then_inc(s_w, 16)
            eng.dma_start(m1e[GI:GI + 1, :], line(m1_b)).then_inc(s_w, 16)
            eng.dma_start(bcol[:, 0:2], down(o1_b)).then_inc(s_w, 16)
            eng.dma_start(b2row[:, :], line(m2_b).to_broadcast([3, H])).then_inc(s_w, 16)
            eng.dma_start(rowA[:, :], line(aw_b).to_broadcast([P, H])).then_inc(s_w, 16)
            eng.dma_start(rowB[:, :], line(o2_b).to_broadcast([P, H])).then_inc(s_w, 16)
            eng.dma_start(rowD[:, :], wr.rearrange("f e -> e f").to_broadcast([P, H])).then_inc(s_w, 16)
            eng.dma_start(c1[:, 7:8], br.rearrange("(e n) -> e n", e=1).to_broadcast([P, 1])).then_inc(s_w, 16)
            eng.dma_start(sm[0:1, 11, :], line(br1)).then_inc(s_w, 16)
            eng.wait_ge(s_cosv, 1)
            eng.activation(tmpc, ew, ACT.Sin, scale=TWO_PI).then_inc(s_cos, 1)

            def root(k):
                eng.wait_ge(s_var, k)
                eng.activation(rstd, vtmp, ACT.Sqrt).then_inc(s_rstd, 1)

            def transposed(s, dest, limit=None):
                def step(k, u, do):
                    t, _, a = at(k, u, per=NSET)
                    eng.wait_ge(s["T"], t + 1)
                    if limit is not None:
                        wait(eng, s[limit], t - NSET + 1)
                    eng.activation(dest(t, a), bank[a][:, 0:H].rearrange("p (k n) -> p k n", k=2),
                                   ACT.Copy).then_inc(s["cT"], 1)
                steps(eng, step, ("copy", 0), count=TILES, per=NSET)

            root(1)
            transposed(p1, lambda t, a: xT[:, a, :, :], "mm")
            phase_end(eng, 0)

            eng.preload_act_table_set("natural_log_exp_and_others")

            def step1(s, u, do):
                q, _, a = at(s, u)
                b = a % 2
                if "exp1" in do:
                    eng.wait_ge(e1["L1"], q + 1)
                    wait(eng, e1["S1"], q - 1)
                    eng.activation(Eb1[:, b, :], bank[2 + b][:, :], ACT.Exp).then_inc(e1["exp1"], 1)
                q1, _, a1 = at(s, u, -2)
                b1_ = a1 % 2
                if "exp2" in do:
                    eng.wait_ge(e1["L2"], q1 + 1)
                    wait(eng, e1["msg"], q1 - 1)
                    eng.activation(Eb2[:, b1_, :], bank[4 + b1_][:, :], ACT.Exp).then_inc(e1["exp2"], 1)
                if "exp1" in do:
                    eng.wait_ge(e1["clamp1"], q + 1)
                    eng.activation(Eb1[:, b, :], Eb1[:, b, :], ACT.Ln, bias=1.0).then_inc(e1["ln1"], 1)
                if "exp2" in do:
                    eng.wait_ge(e1["clamp2"], q1 + 1)
                    eng.activation(Eb2[:, b1_, :], Eb2[:, b1_, :], ACT.Ln, bias=1.0).then_inc(e1["ln2"], 1)
                q2, _, a2 = at(s, u, 2)
                b2_ = a2 % 2
                if "copy" in do:
                    eng.wait_ge(e1["T"], q2 + 1)
                    wait(eng, e1["L1"], q2 - 1)
                    eng.activation(attrT[0:GI, b2_, :], bank[b2_][0:GI, 0:256],
                                   ACT.Copy).then_inc(e1["cT"], 1)

            steps(eng, step1, ("exp1", 0), ("exp2", 2), ("copy", -2))
            phase_end(eng, 1)

            eng.dma_start(o1_sb, mat(o1_W)).then_inc(s_wo, 16)
            eng.dma_start(o2_sb, mat(o2_W)).then_inc(s_wo, 16)

            def out1(q, b, do):
                if "L1" in do:
                    eng.wait_ge(o["L1"], q + 1)
                    wait(eng, o["S"], q - 1)
                    for h in range(2):
                        ins = eng.activation(Eb1[:, b, h * 256:h * 256 + 256],
                                             bank[2 + b][:, h * 256:h * 256 + 256], ACT.Exp, bias=bcol[:, h:h + 1])
                    ins.then_inc(o["exp"], 1)
                    eng.wait_ge(o["clamp"], q + 1)
                    eng.activation(Eb1[:, b, :], Eb1[:, b, :], ACT.Ln, bias=1.0).then_inc(o["ln"], 1)

            for q in range(3):
                out1(q, q % 2, ("L1",))
            with eng.Fori(0, (PAIRS - 3) // 2) as u:
                for j in range(2):
                    out1(u * 2 + 3 + j, (1 + j) % 2, ("L1",))
            phase_end(eng, 2)
            eng.dma_start(w1_sb, mat(w1)).then_inc(s_w2, 16)
            eng.dma_start(w2_sb, w2.rearrange("(c p) n -> p c n", p=P)).then_inc(s_w2, 16)
            eng.dma_start(bcol[:, 8:16], down(b1)).then_inc(s_w2, 16)
            eng.dma_start(rowC[:, :], line(b2).to_broadcast([P, H])).then_inc(s_w2, 16)
            eng.dma_start(wA[:, :, :], mat(L_WT)).then_inc(s_w2, 16)
            root(2)
            block_of = lambda t, a: XT[:, :, bass.ds(t * P, P)]
            transposed(n2, block_of)
            eng.wait_ge(s_w2, 80)
            phase_end(eng, 3)

            def ffn_act(f, func):
                def step(q, b):
                    for c in range(FCH):
                        m = FCH * q + c
                        eng.wait_ge(f["L1"], m + 1)
                        if c == 0:
                            wait(eng, f["L2"], q - 1)
                        eng.activation(Hb[:, b, c, :], bank[c % 4][:, 0:256], func,
                                       bias=bcol[:, 8 + c:9 + c]).then_inc(f["act"], 1)
                for q in range(3):
                    step(q, q % 2)
                with eng.Fori(0, (PAIRS - 3) // 2) as u:
                    for j in range(2):
                        step(u * 2 + 3 + j, (1 + j) % 2)

            ffn_act(f1, ACT.Gelu_apprx_tanh)
            phase_end(eng, 4)
            eng.wait_ge(s_deg, 1)
            eng.activation(rs[:, :], rs_t[:, :], ACT.Sqrt).then_inc(s_deg, 1)
            root(3)
            eng.dma_start(rowA[:, :], line(gamma).to_broadcast([P, H])).then_inc(s_w3, 16)
            eng.dma_start(rowB[:, :], line(beta).to_broadcast([P, H])).then_inc(s_w3, 16)
            transposed(p2, lambda t, a: xT[:, a, :, :], "mm")
            eng.wait_ge(s_w3, 32)
            phase_end(eng, 5)
            phase_end(eng, 6)
            root(4)
            transposed(n3, block_of)
            for k in range(3):
                eng.wait_ge(s_w5, k + 1)
                n = 2 if k == 2 else NEXP
                eng.activation(sm[0:1, 3, 0:n], sm[0:1, 2, 0:n], ACT.Exp).then_inc(s_mqp, 1)
            phase_end(eng, 7)
            ffn_act(f2, ACT.Gelu)
            root(5)
            phase_end(eng, 8)

        @block.tensor
        def _(eng):
            eng.wait_ge(s_w, 16 * 12)
            eng.wait_ge(s_const, 8)
            eng.wait_ge(s_cnt, 1)
            for k in range(2):
                eng.matmul(bank[6][0:3, 0:H], ones[:, 0:3], m2_sb[:, k, :], start=(k == 0), stop=(k == 1))
            eng.drain().then_inc(s_pe, 1)
            eng.wait_ge(s_cnt, 2)
            eng.matmul(bank[5][:, 0:TILES], ones[0:ROWS, :], cnt[0:ROWS, 0, :], start=True, stop=True)
            eng.matmul(bank[5][:, 64:64 + TILES], ones[0:ROWS, :], cnt[0:ROWS, 1, :], start=True, stop=True)
            eng.matmul(bank[5][:, 128:129], ones[0:ROWS, :], c1[0:ROWS, 0:1], start=True, stop=True)
            eng.matmul(bank[5][0:ROWS, 192:192 + TILES], tri[0:ROWS, 0:ROWS], cnt[0:ROWS, 0, :], start=True, stop=True)
            eng.matmul(bank[5][0:ROWS, 256:256 + TILES], tri[0:ROWS, 0:ROWS], cnt[0:ROWS, 1, :], start=True, stop=True)\
               .then_inc(s_tot, 1)

            def schedule(k):
                eng.wait_ge(s_mq, k)
                eng.matmul(bank[6][:, 0:NQ], dcast[:, :], Mq[:, :], start=True, stop=True)
                eng.matmul(bank[7][:, 0:NQ], vcast[:, :], Mq[:, :], start=True, stop=True).then_inc(s_sched, 1)

            schedule(1)

            def transposes(s, t, a):
                eng.wait_ge(s["xn"], t + 1)
                wait(eng, s["cT"], t - NSET + 1)
                for k in range(2):
                    ins = eng.transpose(bank[a][:, k * P:(k + 1) * P], xn[:, a, k * P:(k + 1) * P], ident[:, :])
                ins.then_inc(s["T"], 1)

            def node_products(s):
                def step(k, u, do):
                    if "T" in do:
                        t, _, a = at(k, u, per=NSET)
                        transposes(s, t, a)
                    if "mm" in do:
                        t, _, a = at(k, u, -2, per=NSET)
                        eng.wait_ge(s["cT"], t + 1)
                        wait(eng, s["out"], t - NSET + 1)
                        for c in range(2):
                            ins = eng.matmul(bank[4 + a][:, 0:H], xT[:, a, c, :], wA[:, c, :],
                                             start=(c == 0), stop=(c == 1))
                        ins.then_inc(s["mm"], 1)
                steps(eng, step, ("T", 0), ("mm", 2), count=TILES, per=NSET)

            node_products(p1)
            phase_end(eng, 0)

            def step1(s, u, do):
                q1, _, a1 = at(s, u, -1)
                b = a1 % 2
                if "L2" in do:
                    eng.wait_ge(e1["S1"], q1 + 1)
                    wait(eng, e1["max2"], q1 - 1)
                    for g in range(GRP):
                        v = bank[4 + b][:, g * H:(g + 1) * H]
                        for k in range(2):
                            eng.matmul(v, S1[:, b, k, g * P:(g + 1) * P], m2_sb[:, k, :], start=(k == 0), stop=False)
                        ins = eng.matmul(v, ones_b[:, :], b2spl[:, :], start=False, stop=True)
                    ins.then_inc(e1["L2"], 1)
                q2, _, a2 = at(s, u, -3)
                b = a2 % 2
                if "agg" in do:
                    eng.wait_ge(e1["msg"], q2 + 1)
                    eng.wait_ge(e1["oh"], q2 + 1)
                    wait(eng, e1["add"], q2 - 1)
                    for h in range(2):
                        for g in range(GRP):
                            ins = eng.matmul(bank[6 + b][:, h * P:(h + 1) * P], Mb[:, b, g, h * P:(h + 1) * P],
                                             Ob[:, b, g, :], start=(g == 0), stop=(g == GRP - 1))
                    ins.then_inc(e1["agg"], 1)
                q3, u3, a3 = at(s, u, 2)
                b = a3 % 2
                if "T" in do:
                    eng.wait_ge(s_ld[a3], u3 * 16 + 16)
                    wait(eng, e1["cT"], q3 - 1)
                    standing(eng, apart_pe)
                    for g in range(GRP):
                        ins = eng.transpose(bank[b][0:GI, g * P:(g + 1) * P],
                                            attr[:, a3, g * GI:(g + 1) * GI], ident[:, :])
                    ins.then_inc(e1["T"], 1)
                q4, _, a4 = at(s, u, 1)
                b = a4 % 2
                if "L1" in do:
                    eng.wait_ge(e1["cT"], q4 + 1)
                    wait(eng, e1["S1"], q4 - 1)
                    for h in range(2):
                        ins = eng.matmul(bank[2 + b][:, h * 256:h * 256 + 256], m1e[:, h * P:(h + 1) * P],
                                         attrT[0:GI + 1, b, :], start=True, stop=True)
                    ins.then_inc(e1["L1"], 1)

            steps(eng, step1, ("L2", 1), ("agg", 3), ("T", -2), ("L1", -1))
            phase_end(eng, 1)

            eng.wait_ge(s_wo, 32)
            for k in range(2):
                ins = eng.matmul(bank[7][:, 0:H], ones[:, :], o2_sb[:, k, :], start=(k == 0), stop=(k == 1))
            ins.then_inc(s_pe, 1)

            def out1(q, b, do):
                if "L1" in do:
                    wait(eng, o["S"], q - 1)
                    for h in range(2):
                        for k in range(2):
                            ins = eng.matmul(bank[2 + b][:, h * 256:h * 256 + 256], o1_sb[:, k, h * P:(h + 1) * P],
                                             XT[:, k, bass.ds(q * 256, 256)], start=(k == 0), stop=(k == 1))
                    ins.then_inc(o["L1"], 1)
                if "L2" in do:
                    r, c = q - 1, 1 - b
                    eng.wait_ge(o["S"], r + 1)
                    wait(eng, o["add"], r - 1)
                    for g in range(2):
                        for k in range(2):
                            ins = eng.matmul(bank[4 + c][:, g * H:(g + 1) * H], S1[:, c, k, g * P:(g + 1) * P],
                                             o2_sb[:, k, :], start=(k == 0), stop=(k == 1))
                    ins.then_inc(o["L2"], 1)

            pair_steps(eng, out1)
            phase_end(eng, 2)

            def norm_transposes(s):
                def step(k, u, do):
                    t, _, a = at(k, u, per=NSET)
                    transposes(s, t, a)
                steps(eng, step, ("T", 0), count=TILES, per=NSET)

            norm_transposes(n2)
            for r in range(8):
                eng.wait_ge(s_ctr2, r + 1)
                eng.matmul(bank[4][:, 0:15], ones[:, :], gates[:, 8, 0:15], start=True, stop=True).then_inc(s_ctp, 1)
            eng.wait_ge(s_ctr2, 9)
            eng.matmul(bank[4][:, 0:TILES], ones[:, :], gates[:, 0, :], start=True, stop=True)
            eng.matmul(bank[4][:, 64:64 + TILES], ones[:, :], gates[:, 1, :], start=True, stop=True)
            eng.matmul(bank[4][:, 128:128 + TILES], tri[:, :], gates[:, 1, :], start=True, stop=True).then_inc(s_ctp, 1)
            phase_end(eng, 3)

            def ffn(f, degrees=False):
                def count_degrees(q, b, first=False, last=False):
                    eng.wait_ge(s_ohl, q + 1)
                    for c in range(DCOL):
                        ins = eng.matmul(bank[5][:, 0:TILES], ohl[b][0:ROWS, c, :], ohh[b][0:ROWS, c, :],
                                         start=(first and c == 0), stop=(last and c == DCOL - 1))
                    ins.then_inc(s_ctrd, 1)

                def step(q, b, do):
                    if degrees and "L2" in do:
                        peeled = isinstance(q, int)
                        count_degrees(q - 1, 1 - b, peeled and q == 1, peeled and q == PAIRS)
                    if "L1" in do:
                        for c in range(FCH):
                            m = FCH * q + c
                            wait(eng, f["act"], m - 3)
                            for k in range(2):
                                ins = eng.matmul(bank[c % 4][:, 0:256], w1_sb[:, k, c * P:(c + 1) * P],
                                                 XT[:, k, bass.ds(q * 256, 256)], start=(k == 0), stop=(k == 1))
                            ins.then_inc(f["L1"], 1)
                    if "L2" in do:
                        r, d = q - 1, 1 - b
                        eng.wait_ge(f["act"], r * FCH + FCH)
                        wait(eng, f["y"], r - 1)
                        for g in range(2):
                            for c in range(FCH):
                                ins = eng.matmul(bank[6 + d][:, g * H:(g + 1) * H], Hb[:, d, c, g * P:(g + 1) * P],
                                                 w2_sb[:, c, :], start=(c == 0), stop=(c == FCH - 1))
                        ins.then_inc(f["L2"], 1)
                pair_steps(eng, step)

            ffn(f1, degrees=True)
            phase_end(eng, 4)
            schedule(2)
            node_products(p2)
            phase_end(eng, 5)

            def agg2(q, u, a):
                b = a % 2
                eng.wait_ge(s_g[a % GSET], gathered(u, a) + 32 * (NQ // GSET))
                eng.wait_ge(e2["oh"], q + 1)
                wait(eng, e2["add"], q - 1)
                for g in range(GRP):
                    ins = eng.matmul(bank[b][:, 0:H], Ob[:, b, g, :], Gt[:, a % GSET, g, :], start=(g == 0), stop=(g == GRP - 1))
                ins.then_inc(e2["agg"], 1)

            for a in range(LSET):
                agg2(a, 0, a)
            with eng.Fori(1, NQ // LSET) as u:
                for a in range(LSET):
                    agg2(u * LSET + a, u, a)
            phase_end(eng, 6)
            norm_transposes(n3)
            eng.wait_ge(s_ctr2, 10)
            for k in range(2):
                ins = eng.matmul(bank[4][0:1, 0:NEXP], c1[:, k:k + 1], WrS[:, k, :], start=(k == 0), stop=(k == 1))
            ins.then_inc(s_ctp, 1)
            eng.wait_ge(s_ctr2, 11)
            eng.matmul(bank[4][:, 64:66], ones[0:1, :], sm[0:1, 8, 0:2], start=True, stop=True).then_inc(s_ctp, 1)
            phase_end(eng, 7)
            ffn(f2)
            phase_end(eng, 8)

        @block.vector
        def _(eng):
            chain = Chain(eng, s_dve)
            eng.wait_ge(s_const, 3)
            chain(eng.tensor_copy(iota_f[:, :], iota_i[:, :]))
            chain(eng.tensor_copy(pidx[:, :], pidx_i[:, :]))
            chain(eng.tensor_copy(iota_b[:, :], iota_i[:, 0:P]))
            chain(eng.tensor_scalar(ident[:, :], iota_f[:, 0:P], pidx[:, 0:1], None, ALU.is_equal))
            chain(eng.tensor_scalar(tri[:, :], iota_f[:, 0:P], pidx[:, 0:1], None, ALU.is_gt))
            chain(eng.tensor_scalar(valid[:, :], node_i[:, :], float(N), None, ALU.is_lt))
            chain(eng.tensor_copy(iota16[:, :], iota_i[:, 0:16]))
            eng.sem_inc(s_cnt, 1)
            eng.wait_ge(s_edges, 80)
            eng.wait_ge(s_const, 7)
            chain(eng.tensor_tensor(maskc, dst_i, nxt_i, ALU.is_gt))
            chain(eng.tensor_reduce(c1[0:ROWS, 0:1], maskc, AX.X, ALU.add))
            chain(eng.tensor_scalar(ew, ew, 0.5 / CUTOFF, 0.25, ALU.mult, ALU.add))
            chain(eng.tensor_scalar(tmpc, ew, ROUND, None, ALU.add))
            chain(eng.tensor_scalar(tmpc, tmpc, ROUND, None, ALU.subtract))
            chain(eng.tensor_tensor(ew, ew, tmpc, ALU.subtract))
            eng.sem_inc(s_cosv, 1)
            chain(eng.tensor_copy(rec[:, :, 0], src_i))
            chain(eng.tensor_copy(rec[:, :, 1], dst_i))
            chain(eng.tensor_scalar(nxt_i, dst_i, 7, None, ALU.logical_shift_right))
            chain(eng.tensor_copy(dst_hi, nxt_i))
            chain(eng.tensor_scalar(nxt_i, src_i, 7, None, ALU.logical_shift_right))
            chain(eng.tensor_copy(src_hi, nxt_i))
            chain(eng.tensor_scalar(nxt_i, src_i, P - 1, None, ALU.bitwise_and))
            chain(eng.tensor_copy(src_lo, nxt_i))
            eng.wait_ge(s_cos, 1)
            chain(eng.tensor_scalar(recf[:, :, 2], tmpc, 0.5, 0.5, ALU.mult, ALU.add))
            eng.sem_inc(s_recs, 1)

            eng.sem_inc(s_cnts, 2)
            with eng.Fori(0, TILES // 5) as b:
                for j in range(5):
                    for k, key, mask in ((0, dst_hi, maskc), (1, src_hi, scanc)):
                        eng.wait_ge(s_cnts, b * 10 + (2 * j + k + 1))
                        eng.tensor_scalar(mask, key, iota_f[0:ROWS, bass.ds(b * 5 + j, 1)], 0.0, ALU.is_equal,
                                          ALU.add, accum_out=cnt[0:ROWS, k, bass.ds(b * 5 + j, 1)]).then_inc(s_cnts, 1)
            eng.wait_ge(s_cnts, 2 * TILES + 2)
            eng.sem_inc(s_cnt, 1)
            eng.wait_ge(s_pe, 1)
            eng.wait_ge(s_w, 16 * 12)
            chain(eng.scalar_tensor_tensor(b2row[:, :], bank[6][0:3, 0:H], -LOG2, b2row[:, :], ALU.mult, ALU.add))
            part = rowC[0:3, :]
            chain(eng.memset(part, 0.0))
            for k in range(3):
                chain(eng.tensor_copy(b2spl[:, :], b2row[:, :]))
                chain(eng.tensor_tensor(b2row[:, :], b2row[:, :], b2spl[:, :], ALU.subtract))
                chain(eng.tensor_scalar(c1[0:3, 1:2], pidx[0:3, :], float(k), None, ALU.is_equal))
                chain(eng.scalar_tensor_tensor(part, b2spl[:, :], c1[0:3, 1:2], part, ALU.mult, ALU.add))
            chain(eng.tensor_copy(b2spl[:, :], part))
            eng.wait_ge(s_tot, 1)
            chain(eng.tensor_copy(tot[:, :, :], bank[5][:, 0:128].rearrange("p (k t) -> p k t", k=2)[:, :, 0:TILES]))
            chain(eng.tensor_scalar(flag_i[:, :], bank[5][:, 128:129], 0.5, None, ALU.is_gt))
            eng.sem_inc(s_flag, 1)

            def first_of(row, k):
                chain(eng.tensor_tensor_scan(s50[:, 6, :], tot[:, k, :], zero50[:, :], 0.0, ALU.add, ALU.add))
                chain(eng.tensor_tensor(row, s50[:, 6, :], tot[:, k, :], ALU.subtract))

            def schedule(k, turn):
                start, tiles, first, base, delta = (s50[:, j, :] for j in range(5))
                first_of(start, k)
                chain(eng.tensor_scalar(s50_i[:, :], tot[:, k, :], float(SUP - 1), None, ALU.add))
                chain(eng.tensor_scalar(s50_i[:, :], s50_i[:, :], SUP.bit_length() - 1, None, ALU.logical_shift_right))
                chain(eng.tensor_copy(tiles, s50_i[:, :]))
                chain(eng.tensor_tensor_scan(s50[:, 6, :], tiles, zero50[:, :], 0.0, ALU.add, ALU.add))
                chain(eng.tensor_tensor(first, s50[:, 6, :], tiles, ALU.subtract))
                chain(eng.scalar_tensor_tensor(base, first, float(-SUP), start, ALU.mult, ALU.add))
                chain(eng.tensor_copy(delta, base))
                chain(eng.tensor_tensor(delta[:, 1:TILES], base[:, 1:TILES], base[:, 0:TILES - 1], ALU.subtract))
                for v, c in ((first, 2), (delta, 3)):
                    chain(eng.tensor_tensor(s50[:, 5, :], v, ident[:, 0:TILES], ALU.mult))
                    chain(eng.tensor_reduce(c1[:, c:c + 1], s50[:, 5, :], AX.X, ALU.add))
                chain(eng.tensor_scalar(vcast, pidx[:, 0:1].to_broadcast([P, P]), float(TILES), None, ALU.is_lt))
                chain(eng.tensor_scalar(dcast[:, :], c1[:, 3:4].to_broadcast([P, P]), 0.0, None, ALU.add))
                chain(eng.tensor_scalar(Mq[:, :], iota_f[:, 0:NQ], c1[:, 2:3], None, ALU.is_ge))
                eng.sem_inc(s_mq, 1)
                eng.wait_ge(s_sched, turn)
                chain(eng.scalar_tensor_tensor(nbase[:, :], iota_f[:, 0:NQ], float(SUP), bank[6][:, 0:NQ],
                                               ALU.mult, ALU.add))
                chain(eng.tensor_scalar(offs_i[:, :], nbase[:, :], float(E), None, ALU.min))
                chain(eng.tensor_scalar(blk_i[:, :], bank[7][:, 0:NQ], -1.0, None, ALU.add))
                chain(eng.tensor_scalar(nbase[:, :], bank[7][:, 0:NQ], -float(P), float(P), ALU.mult, ALU.add))

            schedule(0, 1)

            def places_begin(link, k, off_at):
                link(eng.tensor_tensor_scan(s50[:, 6, :], tot[:, k, :], zero50[:, :], 0.0, ALU.add, ALU.add))
                link(eng.tensor_tensor(s50[:, 0, :], s50[:, 6, :], tot[:, k, :], ALU.subtract))
                link(eng.scalar_tensor_tensor(off0[0:ROWS, :], bank[5][0:ROWS, off_at:off_at + TILES], -1.0,
                                              s50[0:ROWS, 0, :], ALU.add, ALU.add))
                link(eng.memset(tmpc, 0.0))
                link(eng.memset(rankc, 0.0))

            def places_of(key, b, part):
                if part == 0:
                    return eng.tensor_scalar(maskc, key, iota_f[0:ROWS, bass.ds(b, 1)], None, ALU.is_equal)
                if part == 1:
                    return eng.tensor_tensor_scan(scanc, maskc, tmpc, off0[0:ROWS, bass.ds(b, 1)], ALU.add, ALU.add)
                return eng.copy_predicated(rankc, maskc_i, scanc)

            unsorted = eng.value_load(flag_i[0:1, 0:1], min_val=0, max_val=1)
            with eng.If(unsorted > 0):
                link = Chain(eng, s_dvu)
                places_begin(link, 0, 192)
                with eng.Fori(0, TILES) as b:
                    link.enter(b, 0, 3)
                    for part in range(3):
                        if part == 2:
                            standing(eng, apart_dve)
                        link(places_of(dst_hi, b, part))
                link.leave(TILES)
                link(eng.tensor_copy(pos_dst, rankc))
                eng.sem_inc(s_dstpos, 1)
            with eng.Else():
                eng.sem_inc(s_dstpos, 1)
            places_begin(chain, 1, 256)
            def statistics(turn, tile):
                with eng.Fori(0, TILES // 5) as u:
                    for j in range(5):
                        t = u * 5 + j
                        eng.bn_stats(stat[:, bass.ds(t, 1), :].rearrange("p a k -> p (a k)"), tile(t)).then_inc(s_stat, 1)
                eng.wait_ge(s_stat, TILES * turn)
                combine(turn)

            def combine(turn):
                me, mo, ve, vo = (stat[:, :, k] for k in (1, 4, 2, 5))
                chain(eng.tensor_tensor(mean, me, mo, ALU.add))
                chain(eng.tensor_tensor(dtmp, me, mo, ALU.subtract))
                chain(eng.tensor_tensor(vtmp, ve, vo, ALU.add))
                chain(eng.tensor_scalar(mean, mean, 0.5, None, ALU.mult))
                chain(eng.tensor_tensor(dtmp, dtmp, dtmp, ALU.mult))
                chain(eng.tensor_scalar(dtmp, dtmp, 0.25, LN_EPS, ALU.mult, ALU.add))
                chain(eng.scalar_tensor_tensor(vtmp, vtmp, 1.0 / H, dtmp, ALU.mult, ALU.add))
                chain(eng.reciprocal(vtmp, vtmp))
                eng.sem_inc(s_var, 1)
                eng.wait_ge(s_rstd, turn)
                chain(eng.tensor_tensor(rstd, rstd, valid[:, :], ALU.mult))

            tile_of_x = lambda t: X[:, bass.ds(t, 1), :].rearrange("p a n -> p (a n)")

            def normed(dest, t, source=None):
                return eng.tensor_scalar(dest, source if source is not None else tile_of_x(t),
                                         mean[:, bass.ds(t, 1)], rstd[:, bass.ds(t, 1)], ALU.subtract, ALU.mult)

            def node_tiles(s, s_dma, finish):
                def step(k, u, do):
                    if "norm" in do:
                        t, _, a = at(k, u, per=NSET)
                        wait(eng, s["T"], t - NSET + 1)
                        normed(xn[:, a, :], t).then_inc(s["xn"], 1)
                    if "finish" in do:
                        t, v, a = at(k, u, -3, per=NSET)
                        eng.wait_ge(s["mm"], t + 1)
                        wait(eng, s_dma[a], v * 16)
                        finish(t, a)
                steps(eng, step, ("norm", 0), ("finish", 3), count=TILES, per=NSET)

            eng.wait_ge(s_x, 32)
            statistics(1, tile_of_x)

            def finish1(t, a):
                eng.tensor_tensor(ob[:, a, :], bank[4 + a][:, 0:H], rowA[:, :], ALU.add).then_inc(p1["out"], 1)

            node_tiles(p1, s_h[0], finish1)
            phase_end(eng, 0)

            def step1(s, u, do):
                q0, _, a0 = at(s, u)
                b0 = a0 % 2
                q1, u1, a1 = at(s, u, -2)
                b1_ = a1 % 2
                q2, _, a2 = at(s, u, -3)
                b2_ = a2 % 2
                if "one" in do:
                    eng.wait_ge(e1["exp1"], q0 + 1)
                    eng.tensor_scalar(Eb1[:, b0, :], Eb1[:, b0, :], EXP_TOP, None, ALU.min).then_inc(e1["clamp1"], 1)
                if "two" in do:
                    eng.wait_ge(e1["exp2"], q1 + 1)
                    eng.tensor_scalar(Eb2[:, b1_, :], Eb2[:, b1_, :], EXP_TOP, None, ALU.min).then_inc(e1["clamp2"], 1)
                if "one" in do:
                    eng.wait_ge(e1["ln1"], q0 + 1)
                    wait(eng, e1["L2"], q0 - 1)
                    eng.tensor_tensor(S1[:, b0, :, :], bank[2 + b0][:, :].rearrange("p (k n) -> p k n", k=2),
                                      Eb1[:, b0, :].rearrange("p (k n) -> p k n", k=2), ALU.max).then_inc(e1["S1"], 1)
                if "two" in do:
                    eng.wait_ge(s_ldr[a1], u1 * 16 + 16)
                    wait(eng, e1["agg"], q1 - 1)
                    er = erec[:, a1, :].rearrange("p (g k) -> p g k", k=3)
                    eng.tensor_tensor(dl[:, b1_, :], er[:, :, 1], nbase[:, bass.ds(q1, 1)].to_broadcast([P, GRP]),
                                      ALU.add).then_inc(s_dl, 1)
                    eng.wait_ge(s_dl, q1 + 1)
                    for g in range(GRP):
                        ins = eng.tensor_scalar(Ob[:, b1_, g, :], iota_f[:, 0:P], dl[:, b1_, g:g + 1],
                                                erec[:, a1, 3 * g + 2:3 * g + 3].bitcast(F32), ALU.is_equal, ALU.mult)
                    ins.then_inc(e1["oh"], 1)
                    eng.wait_ge(e1["ln2"], q1 + 1)
                    eng.tensor_tensor(Eb2[:, b1_, :], bank[4 + b1_][:, :], Eb2[:, b1_, :], ALU.max).then_inc(e1["max2"], 1)
                if "add" in do:
                    r = eng.value_load(blk_i[0:1, bass.ds(q2, 1)], min_val=0, max_val=TILES - 1)
                    eng.wait_ge(e1["agg"], q2 + 1)
                    wait(eng, e1["add"], q2)
                    v = XT[:, :, bass.ds(r * P, P)]
                    eng.tensor_tensor(v, bank[6 + b2_][:, 0:256].rearrange("p (h n) -> p h n", h=2), v,
                                      ALU.add).then_inc(e1["add"], 1)
                if "two" in do:
                    eng.wait_ge(s_g[a1 % GSET], gathered(u1, a1))
                    eng.wait_ge(e1["max2"], q1 + 1)
                    eng.scalar_tensor_tensor(Mb[:, b1_, :, :].rearrange("p g n -> p (g n)"), Eb2[:, b1_, :], -LOG2,
                                             Gt[:, a1 % GSET, :, :].rearrange("p g n -> p (g n)"), ALU.add, ALU.mult)\
                       .then_inc(e1["msg"], 1)

            def fill(j, u):
                if j in (1, 3, 5):
                    part = j // 2
                    if part:
                        eng.wait_ge(s_fill, u * 3 + part)
                    if part == 2:
                        standing(eng, apart_dve)
                    places_of(src_hi, u, part).then_inc(s_fill, 1)

            steps(eng, step1, ("one", 0), ("two", 2), ("add", 3), fill=fill, fills=TILES)
            phase_end(eng, 1)

            eng.wait_ge(s_fill, 3 * TILES)
            chain(eng.tensor_copy(pos_src, rankc))
            eng.sem_inc(s_srcpos, 1)
            eng.wait_ge(s_pe, 2)
            chain(eng.scalar_tensor_tensor(rowB[:, :], bank[7][:, 0:H], -LOG2, rowB[:, :], ALU.mult, ALU.add))

            def out1(q, b, do):
                if "L1" in do:
                    eng.wait_ge(o["exp"], q + 1)
                    eng.tensor_scalar(Eb1[:, b, :], Eb1[:, b, :], EXP_TOP, None, ALU.min).then_inc(o["clamp"], 1)
                if "L2" in do:
                    r, c = q - 1, 1 - b
                    eng.wait_ge(o["L2"], r + 1)
                    wait(eng, o["add"], r)
                    v = X[:, bass.ds(r * 2, 2), :]
                    t3 = tmp.rearrange("p (g n) -> p g n", g=2)
                    eng.tensor_tensor(t3, bank[4 + c][:, :].rearrange("p (g n) -> p g n", g=2),
                                      rowB[:, :].unsqueeze(1).to_broadcast([P, 2, H]), ALU.add).then_inc(s_tmp, 1)
                    eng.wait_ge(s_tmp, r + 1)
                    eng.tensor_tensor(v, v, t3, ALU.add).then_inc(o["add"], 1)
                if "L1" in do:
                    eng.wait_ge(o["ln"], q + 1)
                    wait(eng, o["L2"], q - 1)
                    for h in range(2):
                        ins = eng.scalar_tensor_tensor(S1[:, b, h, :], bank[2 + b][:, h * 256:h * 256 + 256],
                                                       bcol[:, h:h + 1], Eb1[:, b, h * 256:h * 256 + 256],
                                                       ALU.add, ALU.max)
                    ins.then_inc(o["S"], 1)

            pair_steps(eng, out1)
            phase_end(eng, 2)

            statistics(2, tile_of_x)

            def norm2(k, u, do):
                if "norm" in do:
                    t, _, a = at(k, u, per=NSET)
                    wait(eng, n2["T"], t - NSET + 1)
                    wait(eng, s_jk, t - NSET + 1)
                    normed(xn[:, a, :], t).then_inc(n2["xn"], 1)
                if "use" in do:
                    t, _, a = at(k, u, -1, per=NSET)
                    eng.wait_ge(n2["xn"], t + 1)
                    eng.tensor_tensor(tile_of_x(t), tile_of_x(t), xn[:, a, :], ALU.add).then_inc(n2["use"], 1)
                    wait(eng, s_jk, t - 1)
                    eng.scalar_tensor_tensor(tmp[:, (a % 2) * H:(a % 2 + 1) * H], xn[:, a, :], 1.0, rowD[:, :],
                                             ALU.mult, ALU.mult, accum_out=wrt[:, bass.ds(t, 1)]).then_inc(s_jk, 1)

            steps(eng, norm2, ("norm", 0), ("use", 1), count=TILES, per=NSET)
            eng.wait_ge(s_jk, TILES)
            chain(eng.tensor_scalar(wrt[:, :], wrt[:, :], c1[:, 7:8], None, ALU.add))
            chain(eng.tensor_tensor(gates[:, 2, :], wrt[:, :], valid[:, :], ALU.mult))
            chain(eng.tensor_scalar(gates[:, 3, :], valid[:, :], -LOW, LOW, ALU.mult, ALU.add))
            chain(eng.tensor_tensor(gates[:, 2, :], gates[:, 2, :], gates[:, 3, :], ALU.add))
            cand, sign, best, digit = (key_i[:, k, 0:15] for k in range(4))
            chain(eng.memset(best, 0))
            for r in range(8):
                shift = 28 - 4 * r
                chain(eng.tensor_scalar(cand, iota16[:, 1:16], shift, None, ALU.logical_shift_left))
                chain(eng.tensor_tensor(cand, cand, best, ALU.bitwise_or))
                chain(eng.tensor_scalar(cand, cand, -2 ** 31, None, ALU.bitwise_xor))
                chain(eng.tensor_scalar(sign, cand, 31, 2 ** 31 - 1, ALU.arith_shift_right, ALU.bitwise_and))
                chain(eng.tensor_tensor(cand, cand, sign, ALU.bitwise_xor))
                chain(eng.tensor_tensor(cmpb, gates[:, 2, :].unsqueeze(1).to_broadcast([P, 15, TILES]),
                                        cand.bitcast(F32).unsqueeze(2).to_broadcast([P, 15, TILES]), ALU.is_ge))
                chain(eng.tensor_reduce(gates[:, 8, 0:15], cmpb, AX.X, ALU.add))
                eng.sem_inc(s_ctr2, 1)
                eng.wait_ge(s_ctp, r + 1)
                chain(eng.tensor_scalar(gates[:, 9, 0:15], bank[4][:, 0:15], float(K_SEL), None, ALU.is_ge))
                chain(eng.tensor_reduce(c1[:, 4:5], gates[:, 9, 0:15], AX.X, ALU.add))
                chain(eng.tensor_copy(digit, c1[:, 4:5].to_broadcast([P, 15])))
                chain(eng.tensor_scalar(digit, digit, shift, None, ALU.logical_shift_left))
                chain(eng.tensor_tensor(best, best, digit, ALU.bitwise_or))
            chain(eng.tensor_scalar(cand, best, -2 ** 31, None, ALU.bitwise_xor))
            chain(eng.tensor_scalar(sign, cand, 31, 2 ** 31 - 1, ALU.arith_shift_right, ALU.bitwise_and))
            chain(eng.tensor_tensor(cand, cand, sign, ALU.bitwise_xor))
            least = cand.bitcast(F32)[:, 0:1]
            chain(eng.tensor_scalar(gates[:, 0, :], gates[:, 2, :], least, None, ALU.is_gt))
            chain(eng.tensor_scalar(gates[:, 1, :], gates[:, 2, :], least, None, ALU.is_equal))
            eng.sem_inc(s_ctr2, 1)
            eng.wait_ge(s_ctp, 9)
            chain(eng.tensor_copy(gates[:, 4, :], bank[4][:, 64:64 + TILES]))
            chain(eng.tensor_tensor_scan(gates[:, 5, :], gates[:, 4, :], zero50[:, :], 0.0, ALU.add, ALU.add))
            chain(eng.tensor_tensor(gates[:, 5, :], gates[:, 5, :], gates[:, 4, :], ALU.subtract))
            chain(eng.tensor_tensor(gates[:, 5, :], gates[:, 5, :], bank[4][:, 128:128 + TILES], ALU.add))
            chain(eng.tensor_reduce(c1[:, 5:6], bank[4][:, 0:TILES], AX.X, ALU.add))
            chain(eng.tensor_scalar(gates[:, 5, :], gates[:, 5, :], c1[:, 5:6], None, ALU.add))
            chain(eng.tensor_scalar(gates[:, 5, :], gates[:, 5, :], float(K_SEL), None, ALU.is_lt))
            chain(eng.tensor_tensor(gates[:, 5, :], gates[:, 5, :], gates[:, 1, :], ALU.mult))
            chain(eng.tensor_tensor(gates[:, 5, :], gates[:, 5, :], gates[:, 0, :], ALU.add))
            chain(eng.tensor_tensor(gate[:, :], gates[:, 5, :], wrt[:, :], ALU.mult))
            phase_end(eng, 3)

            def ffn1(q, b, do):
                if "L1" in do:
                    wait(eng, s_ctrd, q - 1)
                    for oh, key, n in ((ohl[b], src_lo, P), (ohh[b], src_hi, TILES)):
                        ins = eng.tensor_tensor(oh[0:ROWS, :, :],
                                                iota_b[0:ROWS, 0:n].unsqueeze(1).to_broadcast([ROWS, DCOL, n]),
                                                key[:, bass.ds(q * DCOL, DCOL)].unsqueeze(2)
                                                .to_broadcast([ROWS, DCOL, n]), ALU.is_equal)
                    ins.then_inc(s_ohl, 1)
                if "L2" in do:
                    r, c = q - 1, 1 - b
                    eng.wait_ge(f1["L2"], r + 1)
                    wait(eng, s_x1, r * 2)
                    t3 = tmp.rearrange("p (g n) -> p g n", g=2)
                    eng.tensor_tensor(t3, bank[6 + c][:, :].rearrange("p (g n) -> p g n", g=2),
                                      rowC[:, :].unsqueeze(1).to_broadcast([P, 2, H]), ALU.add).then_inc(f1["y"], 1)
                    eng.wait_ge(f1["y"], r + 1)
                    for g in range(2):
                        v = tile_of_x(r * 2 + g)
                        eng.scalar_tensor_tensor(v, tmp[:, g * H:(g + 1) * H], gate[:, bass.ds(r * 2 + g, 1)], v,
                                                 ALU.mult, ALU.add).then_inc(s_x1, 1)

            pair_steps(eng, ffn1)
            eng.wait_ge(s_ctrd, PAIRS)
            chain(eng.tensor_scalar(rs_t[:, :], bank[5][:, 0:TILES], 1.0, None, ALU.add))
            chain(eng.reciprocal(rs_t[:, :], rs_t[:, :]))
            phase_end(eng, 4)
            eng.sem_inc(s_deg, 1)
            eng.wait_ge(s_deg, 2)
            schedule(1, 2)
            statistics(3, tile_of_x)

            def finish2(t, a):
                eng.tensor_scalar(ob[:, a, :], bank[4 + a][:, 0:H], rs[:, bass.ds(t, 1)], None, ALU.mult)\
                   .then_inc(p2["out"], 1)
                eng.wait_ge(p2["out"], t + 1)
                eng.scalar_tensor_tensor(tile_of_x(t), ob[:, a, :], rs[:, bass.ds(t, 1)], tile_of_x(t),
                                         ALU.mult, ALU.add)

            node_tiles(p2, s_h[1], finish2)
            phase_end(eng, 5)

            def hot2(q, u, a):
                b = a % 2
                eng.wait_ge(s_ldr[a], u * 16 + 16 * (NQ // LSET) + 16)
                wait(eng, e2["agg"], q - 1)
                er = erec[:, a, :].rearrange("p (g k) -> p g k", k=3)
                eng.tensor_tensor(dl[:, b, :], er[:, :, 0], nbase[:, bass.ds(q, 1)].to_broadcast([P, GRP]),
                                  ALU.add).then_inc(s_dl, 1)
                eng.wait_ge(s_dl, q + NQ + 1)
                for g in range(GRP):
                    ins = eng.tensor_scalar(Ob[:, b, g, :], iota_f[:, 0:P], dl[:, b, g:g + 1], None, ALU.is_equal)
                ins.then_inc(e2["oh"], 1)

            def add2(q, u, a):
                b = a % 2
                r = eng.value_load(blk_i[0:1, bass.ds(q, 1)], min_val=0, max_val=TILES - 1)
                eng.wait_ge(e2["agg"], q + 1)
                wait(eng, e2["add"], q)
                v = X[:, bass.ds(r, 1), :].rearrange("p a n -> p (a n)")
                eng.scalar_tensor_tensor(v, bank[b][:, 0:H], rs[:, bass.ds(r, 1)], v, ALU.mult, ALU.add)\
                   .then_inc(e2["add"], 1)

            hot2(0, 0, 0)
            for a in range(1, LSET):
                hot2(a, 0, a)
                add2(a - 1, 0, a - 1)
            with eng.Fori(1, NQ // LSET) as u:
                for a in range(LSET):
                    hot2(u * LSET + a, u, a)
                    add2(u * LSET + a - 1, u, (a - 1) % LSET)
            add2(NQ - 1, NQ // LSET - 1, LSET - 1)
            phase_end(eng, 6)

            statistics(4, tile_of_x)

            def norm3(k, u, do):
                t, _, a = at(k, u, per=NSET)
                wait(eng, n3["T"], t - NSET + 1)
                normed(xn[:, a, :], t).then_inc(n3["xn"], 1)

            steps(eng, norm3, ("norm", 0), count=TILES, per=NSET)
            eng.wait_ge(n3["cT"], TILES)
            chain(eng.tensor_reduce(c1[:, 0:2], XT[:, :, :], AX.X, ALU.add))
            chain(eng.tensor_scalar(c1[:, 0:2], c1[:, 0:2], 1.0 / N, None, ALU.mult))
            eng.sem_inc(s_ctr2, 1)
            eng.wait_ge(s_ctp, 10)
            row = lambda k, n=NEXP: sm[0:1, k, 0:n]
            one = lambda k: zst[0:1, k:k + 1]

            def softmax(k, v, n):
                chain(eng.tensor_reduce(one(0), v, AX.X, ALU.max))
                chain(eng.tensor_scalar(row(2, n), v, one(0), None, ALU.subtract))
                eng.sem_inc(s_w5, 1)
                eng.wait_ge(s_mqp, k)
                chain(eng.tensor_reduce(one(1), row(3, n), AX.X, ALU.add))
                chain(eng.reciprocal(one(2), one(1)))
                chain(eng.tensor_scalar(row(4, n), row(3, n), one(2), None, ALU.mult))

            chain(eng.tensor_tensor(row(1), bank[4][0:1, 0:NEXP], row(11), ALU.add))
            softmax(1, row(1), NEXP)
            chain(eng.tensor_scalar(row(5), row(4), float(N), None, ALU.mult))
            chain(eng.reciprocal(row(6), row(5)))
            chain(eng.tensor_scalar(row(6), row(6), CAPACITY, -1.0, ALU.mult, ALU.add))
            chain(eng.tensor_scalar(row(5), row(5), CAPACITY, None, ALU.is_gt))
            chain(eng.tensor_tensor(row(6), row(6), row(5), ALU.mult))
            chain(eng.tensor_scalar(row(6), row(6), 1.0, None, ALU.add))
            chain(eng.tensor_tensor(row(7), row(4), row(6), ALU.mult))
            softmax(2, row(7), NEXP)
            chain(eng.tensor_copy(row(9), row(4)))
            chain(eng.max(row(10), row(9)))
            chain(eng.max_index(sm_i[0:1, :], row(10), row(9)))
            chain(eng.tensor_copy(ex_i[0:1, :], sm_i[0:1, 0:2]))
            eng.sem_inc(s_sel, 1)
            softmax(3, row(10, 2), 2)
            chain(eng.tensor_copy(row(8, 2), row(4, 2)))
            eng.sem_inc(s_ctr2, 1)
            eng.wait_ge(s_ctp, 11)
            chain(eng.tensor_copy(c1[:, 4:6], bank[4][:, 64:66]))
            eng.wait_ge(s_w4, 16 * 8)
            for j in range(2):
                v = w2_sb[:, 4 * j:4 * j + 4, :]
                chain(eng.tensor_scalar(v, v, c1[:, 4 + j:5 + j], None, ALU.mult))
            chain(eng.tensor_scalar(rowC[:, :], rowC[:, :], c1[:, 4:5], None, ALU.mult))
            chain(eng.scalar_tensor_tensor(rowC[:, :], rowD[:, :], c1[:, 5:6], rowC[:, :], ALU.mult, ALU.add))
            phase_end(eng, 7)

            def ffn2(q, b, do):
                if "L2" in do:
                    r, c = q - 1, 1 - b
                    wait(eng, s_z, r * 2)
                    for g in range(2):
                        normed(tmp[:, g * H:(g + 1) * H], r * 2 + g).then_inc(s_y2, 1)
                    eng.wait_ge(f2["L2"], r + 1)
                    eng.wait_ge(s_y2, r * 2 + 2)
                    z = XT[:, :, bass.ds(r * 256, 256)]
                    t3 = tmp.rearrange("p (g n) -> p g n", g=2)
                    eng.tensor_tensor(t3, bank[6 + c][:, :].rearrange("p (g n) -> p g n", g=2), t3,
                                      ALU.add).then_inc(f2["y"], 1)
                    eng.wait_ge(f2["y"], r + 1)
                    eng.tensor_tensor(z, t3, rowC[:, :].unsqueeze(1).to_broadcast([P, 2, H]), ALU.add).then_inc(s_zz, 1)
                    eng.wait_ge(s_zz, r + 1)
                    for g in range(2):
                        eng.bn_stats(stat[:, bass.ds(r * 2 + g, 1), :].rearrange("p a k -> p (a k)"),
                                     XT[:, g, bass.ds(r * 256, 256)]).then_inc(s_z, 1)

            pair_steps(eng, ffn2)
            eng.wait_ge(s_z, TILES)
            combine(5)

            def final(u, g, first):
                t = u * 2 + g
                if not first:
                    eng.wait_ge(s_h[2][g], u * 16)
                v = ob[:, g, :]
                chain(normed(v, t, XT[:, g, bass.ds(u * 256, 256)]))
                chain(eng.tensor_tensor(v, v, rowA[:, :], ALU.mult))
                chain(eng.tensor_tensor(v, v, rowB[:, :], ALU.add))
                chain(eng.tensor_tensor(v, v, tile_of_x(t), ALU.add))
                eng.sem_inc(f2["y"], 1)

            for g in range(2):
                final(0, g, True)
            with eng.Fori(1, FULL // 2) as u:
                chain.enter(u, 1, 8)
                for g in range(2):
                    final(u, g, False)
            chain.leave(FULL // 2 - 1)
            final(FULL // 2, 0, False)
            phase_end(eng, 8)


_INS = ["x", "src", "dst", "edge_attr_50", "edge_weight", "L0_gnn_aw_W", "L0_gnn_aw_b", "L0_gnn_m1_W", "L0_gnn_m1_b",
        "L0_gnn_m2_W", "L0_gnn_m2_b", "L0_gnn_o1_W", "L0_gnn_o1_b", "L0_gnn_o2_W", "L0_gnn_o2_b", "L0_ffn_wr",
        "L0_ffn_br", "L0_ffn_w1", "L0_ffn_b1", "L0_ffn_w2", "L0_ffn_b2", "L1_gnn_W", "L1_ffn_Wr", "L1_ffn_br",
        "L1_ffn_W1", "L1_ffn_b1", "L1_ffn_W2", "L1_ffn_b2", "L1_ffn_gamma", "L1_ffn_beta"]


def kernel(**inputs):
    import numpy as _np
    import concourse.bacc as _bacc
    from concourse import mybir as _mybir
    from concourse.bass_utils import run_bass_kernel_spmd as _run

    nc = _bacc.Bacc("TRN2", target_bir_lowering=False, num_devices=1)
    arrays, args = {}, []
    for name in _INS:
        a = _np.asarray(inputs[name])
        a = _np.ascontiguousarray(a.T if name == "L1_gnn_W" else a)
        arrays[f"in_{name}"] = a
        args.append(nc.dram_tensor(f"in_{name}", a.shape, _mybir.dt.from_np(a.dtype), kind="ExternalInput").ap())
    shape = inputs["x"].shape
    args.append(nc.dram_tensor("out_x", shape, _mybir.dt.float32, kind="ExternalOutput").ap())
    gnn_ffn_kernel(nc, *args)
    r = _run(nc, [arrays], core_ids=[0])
    return r.results[0]["out_x"]
```

```python
from contextlib import ExitStack

import concourse.bass as bass
from concourse import mybir

F32 = mybir.dt.float32
BF16 = mybir.dt.bfloat16
I32 = mybir.dt.int32
U32 = mybir.dt.uint32
ALU = mybir.AluOpType
ACT = mybir.ActivationFunctionType
AX = mybir.AxisListType

P = 128
LOG2 = 0.6931471805599453
TWO_PI = 6.283185
ROUND = 12582912.0
LN_EPS = 1e-5
EXP_TOP = float(2 ** 60)
CUTOFF = 10.0
LOW = -3.0e38
FAR = 1000000
LSET = 8
GSET = 4
TILES = 50
NPAD = TILES * P
PAIRS = TILES // 2
ROWS, COLS = 125, 800
GRP = 2
SUP = GRP * P
CHUNK = 20
HALF = CHUNK // 2
NSET = 4
WIN = 64


def wait(eng, sem, value):
    if isinstance(value, int) and value <= 0:
        return
    eng.wait_ge(sem, value)


def standing(eng, sem_apart):
    eng.sem_inc(sem_apart, 1)


class Chain:

    def __init__(self, eng, sem):
        self.eng, self.sem, self.n, self.base = eng, sem, 0, 0

    def __call__(self, ins):
        ins.then_inc(self.sem, 1)
        self.n += 1
        self.eng.wait_ge(self.sem, self.base + self.n if not isinstance(self.base, int) else self.n)

    def enter(self, i, first, per_turn):
        self.base, self.at, self.per_turn = (i - first) * per_turn, self.n, per_turn

    def leave(self, turns):
        assert self.n - self.at == self.per_turn, (self.n - self.at, self.per_turn)
        self.n, self.base = self.at + self.per_turn * turns, 0


def gnn_ffn_kernel(nc, x, src, dst, edge_attr, edge_weight, aw_W, aw_b, m1_W, m1_b, m2_W, m2_b,
                   o1_W, o1_b, o2_W, o2_b, wr, br, w1, b1, w2, b2, L_WT, Wr, br1, W1, B1, W2, B2,
                   gamma, beta, out):
    N, H = x.shape
    E, GI = edge_attr.shape
    assert ROWS * COLS == E and NPAD >= N and H == 2 * P
    FULL = N // P
    TAIL = N - FULL * P
    K_SEL = max(1, N // 2) - 1
    NQ = -(-E // SUP) + TILES - 1
    NQ += (-NQ) % LSET
    NT = -(-E // SUP)
    NEXP = Wr.shape[1]
    FE = W1.shape[2]
    CAPACITY = float(-(-N * 5 // (4 * NEXP)))
    FCH = w1.shape[1] // P
    BATCH = 4
    LAG = BATCH + 1
    BATCHES = (PAIRS - 1) // BATCH
    assert PAIRS == BATCH * BATCHES + 1
    DCOL = COLS // PAIRS
    ORDER_TURNS = TILES // 2
    MOVE_FROM, MOVE_TO = ORDER_TURNS + 1, (NT - GSET) // LSET - 1
    MOVED = 1 + MOVE_TO - MOVE_FROM
    MOVE_PAIRS = (COLS // HALF - MOVED) // 2
    assert MOVED + 2 * MOVE_PAIRS == COLS // HALF

    h1 = nc.dram_tensor("h1", (NPAD, H), F32, kind="Internal").ap()
    h2 = nc.dram_tensor("h2", (NPAD, H), F32, kind="Internal").ap()
    attr_s = nc.dram_tensor("attr_s", (E + SUP, GI), F32, kind="Internal").ap()
    rec_d = nc.dram_tensor("rec_d", (E + SUP, 3), I32, kind="Internal").ap()
    rec_s = nc.dram_tensor("rec_s", (E + SUP, 3), I32, kind="Internal").ap()

    ctx = ExitStack()
    with ctx:
        ctx.enter_context(nc.allow_non_contiguous_dma(reason="bias vectors onto partitions, a few hundred numbers"))
        def sb(name, shape, dt=F32):
            return ctx.enter_context(nc.sbuf_tensor(name, shape, dt))

        def sem(name):
            return ctx.enter_context(nc.semaphore(name))

        X = sb("X", [P, TILES, H])
        XT = sb("XT", [P, 2, NPAD])
        R = sb("R", [P, TILES * H])
        W = sb("W", [P, 7168])

        def col(at, dt=F32, n=COLS):
            v = R[0:ROWS, at:at + n]
            return v if dt is F32 else v.bitcast(dt)

        dst_i, src_i, nxt_i = col(0, I32), col(800, I32), col(1600, I32)
        ew, tmpc = col(2400), col(3200)
        dst_hi = col(4000, BF16, COLS // 2)
        maskc, maskc_i, scanc, rankc = col(4400), col(4400, I32), col(5200), col(6000)
        pos_dst = col(6800, I32)
        rec = col(8192, I32, 3 * COLS).rearrange("p (c k) -> p c k", k=3)
        recf = col(8192, F32, 3 * COLS).rearrange("p (c k) -> p c k", k=3)
        pos_src = col(10592, I32)
        src_lo, src_hi = col(11392, BF16, COLS // 2), col(11792, BF16, COLS // 2)
        w1_sb = R[:, 0:2048].rearrange("p (k n) -> p k n", k=2)
        w2_sb = R[:, 2048:4096].rearrange("p (c n) -> p c n", n=H)
        Hb = R[:, 4096:8192].rearrange("p (a c n) -> p a c n", a=2, c=FCH)
        o1_sb = R[:, 4096:4608].rearrange("p (k n) -> p k n", k=2)
        o2_sb = R[:, 4608:5120].rearrange("p (k n) -> p k n", k=2)
        Gt = W[:, 0:2048].rearrange("p (a g n) -> p a g n", a=4, g=GRP)
        Eb1 = W[:, 2048:3072].rearrange("p (a n) -> p a n", a=2)
        Eb2 = W[:, 3072:4096].rearrange("p (a n) -> p a n", a=2)
        S1 = W[:, 4096:5120].rearrange("p (a k n) -> p a k n", a=2, k=2)
        Mb = W[:, 5120:6144].rearrange("p (a g n) -> p a g n", a=2, g=GRP)
        Ob = W[:, 6144:6656].rearrange("p (a g n) -> p a g n", a=2, g=GRP)
        attrT = W[:, 6912:7168].rearrange("p (a n) -> p a n", a=2)
        xn = W[:, 0:1024].rearrange("p (a n) -> p a n", a=NSET)
        xT = W[:, 1024:2048].rearrange("p (a k n) -> p a k n", a=NSET, k=2)
        ob = W[:, 2048:3072].rearrange("p (a n) -> p a n", a=NSET)
        tmp = W[:, 3072:3584]
        added = W[:, 2048:2304].rearrange("p (k n) -> p k n", k=2)
        iota_i = W[:, 3584:4096].bitcast(I32)
        cmpb = W[:, 4096:4096 + 15 * TILES].rearrange("p (j t) -> p j t", t=TILES)
        gates = W[:, 2048:2048 + 16 * TILES].rearrange("p (k t) -> p k t", t=TILES)
        stat = W[:, 6432:6432 + 6 * TILES].rearrange("p (t k) -> p t k", k=6)
        s50 = W[:, 5420:5420 + 8 * TILES].rearrange("p (k t) -> p k t", k=8)
        Mq = W[:, 5824:5824 + NQ]
        dcast, vcast = W[:, 6272:6400], W[:, 6400:6528]
        node_i = W[:, 6528:6528 + TILES].bitcast(I32)
        ends = W[0:1, 4096:4096 + 2 * NT].bitcast(I32).rearrange("p (k t) -> p k t", k=2)
        spread, first_f = W[0:1, 3072:3072 + NT], W[0:1, 3584:3584 + NT]
        Ow = W[:, 4096:5120].rearrange("p (a g n) -> p a g n", a=2, g=GRP)
        ohl = [W[:, k:k + DCOL * P // 2].bitcast(BF16).rearrange("p (c n) -> p c n", n=P) for k in (0, 3584)]
        ohh = [W[:, k + DCOL * P // 2:k + DCOL * (P + TILES) // 2].bitcast(BF16).rearrange("p (c n) -> p c n", n=TILES)
               for k in (0, 3584)]

        attr = sb("attr", [P, LSET, GRP * GI])
        erec = sb("erec", [P, LSET, GRP * 3], I32)
        st = sb("st", [P, 4, TILES])
        mean, rstd, vtmp, dtmp = (st[:, k, :] for k in range(4))
        wA = sb("wA", [P, 2, H])
        m1e = sb("m1e", [GRP * GI + 1, GRP, H])
        m2_sb = sb("m2_sb", [P, 2, H])
        rowA = sb("rowA", [P, H])
        rowB = sb("rowB", [P, H])
        rowC = sb("rowC", [P, H])
        rowD = sb("rowD", [P, H])
        bcol = sb("bcol", [P, 16])
        b2row = sb("b2row", [3, H])
        b2spl = sb("b2spl", [P, H], BF16)
        ones_b = sb("ones_b", [P, P], BF16)
        iota_f = sb("iota_f", [P, 512])
        iota_b = sb("iota_b", [P, P], BF16)
        pidx_i = sb("pidx_i", [P, 1], I32)
        pidx = sb("pidx", [P, 1])
        valid = sb("valid", [P, TILES])
        ident = sb("ident", [P, P])
        tri = sb("tri", [P, P])
        ones = sb("ones", [P, P])
        iota16 = sb("iota16", [P, 16], I32)
        offs_i = sb("offs_i", [P, NQ], I32)
        blk_i = sb("blk_i", [P, NQ], I32)
        nbase = sb("nbase", [P, NQ])
        cnt = sb("cnt", [P, 2, TILES])
        tot = sb("tot", [P, 2, TILES])
        s50_i = sb("s50_i", [P, TILES], I32)
        zero50 = sb("zero50", [P, TILES])
        off0 = sb("off0", [P, TILES])
        c1 = sb("c1", [P, 8])
        flag_i = sb("flag_i", [P, 4], I32)
        rs = sb("rs", [P, TILES])
        rs_t = sb("rs_t", [P, TILES])
        wrt = sb("wrt", [P, TILES])
        gate = sb("gate", [P, TILES])
        key_i = sb("key_i", [P, 4, 16], I32)
        dl = sb("dl", [P, 2, GRP])
        sidx = sb("sidx", [P, CHUNK], I32)
        srec = sb("srec", [P, CHUNK, 3], I32)
        sm = sb("sm", [1, 12, NEXP])
        sm_i = sb("sm_i", [1, NEXP], U32)
        ex_i = sb("ex_i", [1, 2], I32)
        zst = sb("zst", [1, 4])
        WrS = sb("WrS", [P, 2, NEXP])

        bank = [ctx.enter_context(nc.psum_tensor(f"bank{k}", [P, 512], F32)) for k in range(8)]

        s_phase = sem("s_phase")
        s_middle = sem("s_middle")
        s_fill = sem("s_fill")
        s_stat = sem("s_stat")
        s_cnts = sem("s_cnts")
        s_const = sem("s_const")
        s_dve = sem("s_dve")
        s_act = sem("s_act")
        s_pe = sem("s_pe")
        s_edges = sem("s_edges")
        s_big = sem("s_big")
        s_x = sem("s_x")
        s_w = sem("s_w")
        s_w2 = sem("s_w2")
        s_w4 = sem("s_w4")
        s_w5 = sem("s_w5")
        s_zero = sem("s_zero")
        s_sent = sem("s_sent")
        s_cos = sem("s_cos")
        s_recs = sem("s_recs")
        s_cnt = sem("s_cnt")
        s_tot = sem("s_tot")
        s_flag = sem("s_flag")
        s_dstpos = sem("s_dstpos")
        s_order = sem("s_order")
        s_srcpos = sem("s_srcpos")
        s_ohl = sem("s_ohl")
        s_deg = sem("s_deg")
        s_sel = sem("s_sel")
        s_scat = [sem(f"s_scat{k}") for k in range(2)]
        s_win, s_wfirst, s_wcast = (sem("s_" + n) for n in ("win", "wfirst", "wcast"))
        s_narrow = [sem(f"s_narrow{k}") for k in range(2)]
        s_rec2 = [sem(f"s_rec2{k}") for k in range(LSET)]
        s_g2 = [sem(f"s_g2{k}") for k in range(GSET)]
        s_dl2 = sem("s_dl2")
        s_gl = sem("s_gl")
        s_mq = sem("s_mq")
        s_mqp = sem("s_mqp")
        s_sched = sem("s_sched")
        s_var = sem("s_var")
        s_rstd = sem("s_rstd")
        s_ld = [sem(f"s_ld{k}") for k in range(LSET)]
        s_ldr = [sem(f"s_ldr{k}") for k in range(LSET)]
        s_g = [sem(f"s_g{k}") for k in range(GSET)]
        names = ("T cT L1 abs1 exp1 ln1 S1 L2 exp2 clamp2 ln2 max2 oh msg agg add").split()
        e1 = {n: sem("e1_" + n) for n in names}
        e2 = {n: sem("e2_" + n) for n in ("oh", "agg", "add")}
        p1 = {n: sem("p1_" + n) for n in ("xn", "T", "cT", "mm", "out")}
        p2 = {n: sem("p2_" + n) for n in ("xn", "T", "cT", "mm", "out", "self")}
        n2 = {n: sem("n2_" + n) for n in ("begin", "xn", "T", "cT", "use")}
        n3 = {n: sem("n3_" + n) for n in ("xn", "T", "cT", "sum")}
        s_h = [[sem(f"s_h{k}{a}") for a in range(n)] for k, n in enumerate((NSET, NSET, 2))]
        o = {n: sem("o_" + n) for n in ("L1", "exp", "clamp", "ln", "S", "L2", "add")}
        f1 = {n: sem("f1_" + n) for n in ("L1", "act", "L2", "y")}
        f2 = {n: sem("f2_" + n) for n in ("L1", "act", "L2", "y")}
        s_ctrd, s_topk, s_ctp, s_dvu, s_dl, s_jk = (sem("s_" + n) for n in ("degree", "topk", "topp", "dvu", "dl", "jk"))
        s_tmp, s_x1, s_y2, s_zz, s_z = (sem("s_" + n) for n in ("tmp", "x1", "y2", "zz", "z"))
        apart_pe, apart_pool, apart_dve = (sem("apart_" + n) for n in ("pe", "pool", "dve"))
        s_stage, s_att, s_perm, s_fin = (sem("s_" + n) for n in ("stage", "att", "perm", "fin"))

        def phase_end(eng, k):
            if k in (2, 3, 4):
                eng.drain().then_inc(s_middle, 1)
                eng.wait_ge(s_middle, 4 * (k - 1))
            else:
                n = k + 1 if k < 2 else k - 2
                eng.drain().then_inc(s_phase, 1)
                eng.wait_ge(s_phase, 5 * n)

        block = ctx.enter_context(nc.Block())

        def at(s, u, d=0, per=LSET):
            k = s + d
            u = u + k // per
            return u * per + k % per, u, k % per

        def gathered(u, a):
            return u * (32 * LSET // GSET) + 32 * (a // GSET + 1)

        def steps(eng, step, *parts, count, per=LSET, ahead=2, fill=None, fills=(0, 0), before=None, after=None):
            lo, hi = max(k for _, k in parts) + ahead, count + min(k for _, k in parts)
            names = lambda s: tuple(n for n, k in parts if 0 <= s - k < count)
            for s in range(min(k for _, k in parts), lo):
                step(s, 0, names(s))
            turns = (hi - lo) // per
            assert fills[1] <= turns

            def loop(begin, end, fill):
                if begin < end:
                    with eng.Fori(begin, end) as u:
                        for j in range(per):
                            step(lo + j, u, names(lo))
                            if fill:
                                fill(j, u)

            loop(0, fills[0], None)
            if before:
                before()
            loop(fills[0], fills[1], fill)
            if after:
                after()
            loop(fills[1], turns, None)
            for s in range(lo + turns * per, count + max(k for _, k in parts)):
                step(s, 0, names(s))

        def either(eng, k, phase):
            narrow = eng.value_load(flag_i[0:1, k + 1:k + 2], min_val=0, max_val=1)
            with eng.If(narrow > 0):
                phase(NT, True)
            with eng.Else():
                phase(NQ, False)

        def pair_steps(eng, step):
            for q in range(3):
                step(q, q % 2, ("L1", "L2") if q else ("L1",))
            with eng.Fori(0, (PAIRS - 3) // 2) as u:
                for j in range(2):
                    step(u * 2 + 3 + j, (1 + j) % 2, ("L1", "L2"))
            step(PAIRS, PAIRS % 2, ("L2",))

        @block.sync
        def _(eng):
            eng.wait_ge(s_big, 1)
            two = lambda a: a.rearrange("(p c) -> p c", c=COLS)
            eng.dma_start(dst_i, two(dst)).then_inc(s_edges, 16)
            eng.dma_start(src_i, two(src)).then_inc(s_edges, 16)
            eng.dma_start(nxt_i[0:ROWS - 1, :], two(dst[1:1 + (ROWS - 1) * COLS])).then_inc(s_edges, 16)
            eng.dma_start(nxt_i[ROWS - 1:ROWS, 0:COLS - 1],
                          dst[1 + (ROWS - 1) * COLS:E].rearrange("(p c) -> p c", p=1)).then_inc(s_edges, 16)
            eng.dma_start(ew, two(edge_weight)).then_inc(s_edges, 16)
            eng.dma_start(X[:, 0:FULL, :], x[0:FULL * P, :].rearrange("(t p) f -> p t f", p=P)).then_inc(s_x, 16)
            eng.wait_ge(s_zero, 2)
            eng.dma_start(X[0:TAIL, FULL, :], x[FULL * P:N, :]).then_inc(s_x, 16)
            eng.wait_ge(s_zero, 5)
            eng.dma_start(attr_s[E:E + SUP, :].rearrange("(p g) f -> p (g f)", g=GRP), attr[:, 0, :]).then_inc(s_sent, 16)
            for k, r in enumerate((rec_d, rec_s)):
                eng.dma_start(r[E:E + SUP, :].rearrange("(p g) f -> p (g f)", g=GRP), erec[:, k, :]).then_inc(s_sent, 16)

            def store_h(table, s_out, s_dma):
                def store(s, u, do):
                    t, _, a = at(s, u, per=NSET)
                    eng.wait_ge(s_out, t + 1)
                    eng.dma_start(table[bass.ds(t * P, P), :], ob[:, a, :]).then_inc(s_dma[a], 16)
                steps(eng, store, ("store", 0), count=TILES, per=NSET, ahead=NSET)
                for a in range(NSET):
                    eng.wait_ge(s_dma[a], 16 * len(range(a, TILES, NSET)))

            store_h(h1, p1["out"], s_h[0])
            eng.wait_ge(s_sent, 48)
            eng.wait_ge(s_order, 1)

            def load_ends(rec, field):
                v = rec[0:NT * SUP, field:field + 1].rearrange("(t s) k -> k t s", s=SUP)
                eng.dma_start(ends[:, 0, :], v[:, :, 0]).then_inc(s_win, 16)
                eng.dma_start(ends[:, 1, 0:NT - 1], v[:, 0:NT - 1, SUP - 1]).then_inc(s_win, 16)
                eng.dma_start(ends[:, 1, NT - 1:NT], rec[E - 1:E, field:field + 1]).then_inc(s_win, 16)

            load_ends(rec_d, 1)
            phase_end(eng, 0)

            def loads1(count, narrow):
                def load1(k, u, do):
                    q, _, a = at(k, u)
                    wait(eng, e1["T"], q - LSET + 1)
                    wait(eng, e1["msg"], q - LSET + 1)
                    s = q * SUP if narrow else eng.value_load(offs_i[0:1, bass.ds(q, 1)], min_val=0, max_val=E)
                    edges = E - s if narrow and isinstance(s, int) and s + SUP > E else SUP
                    assert edges % GRP == 0
                    eng.dma_start(attr[0:edges // GRP, a, :], (edge_attr if narrow else attr_s)[bass.ds(s, edges), :]
                                  .rearrange("(p g) f -> p (g f)", g=GRP)).then_inc(s_ld[a], 16)
                    eng.dma_start(erec[:, a, :], rec_d[bass.ds(s, SUP), :].rearrange("(p g) f -> p (g f)", g=GRP))\
                       .then_inc(s_ldr[a], 16)
                steps(eng, load1, ("load", 0), count=count, ahead=LSET)

            either(eng, 0, loads1)
            phase_end(eng, 1)
            for k in range(2, 5):
                phase_end(eng, k)
            store_h(h2, p2["out"], s_h[1])
            eng.wait_ge(s_order, 2)
            load_ends(rec_s, 0)
            phase_end(eng, 5)

            def loads2(count, narrow):
                def load2(k, u, do):
                    q, _, a = at(k, u)
                    wait(eng, e2["oh"], q - LSET + 1)
                    wait(eng, e2["agg"], q - LSET + 1)
                    s = q * SUP if narrow else eng.value_load(offs_i[0:1, bass.ds(q, 1)], min_val=0, max_val=E)
                    eng.dma_start(erec[:, a, :], rec_s[bass.ds(s, SUP), :].rearrange("(p g) f -> p (g f)", g=GRP))\
                       .then_inc(s_rec2[a], 16)
                steps(eng, load2, ("load", 0), count=count, ahead=LSET)

            either(eng, 1, loads2)
            phase_end(eng, 6)
            eng.wait_ge(s_sel, 1)
            for j in range(2):
                e = eng.value_load(ex_i[0:1, j:j + 1], min_val=0, max_val=NEXP - 1)
                eng.dma_start(w1_sb[:, :, j * FE:(j + 1) * FE],
                              W1[bass.ds(e, 1), :, :].rearrange("e (k p) n -> p (e k) n", p=P)).then_inc(s_w4, 16)
                eng.dma_start(w2_sb[:, 4 * j:4 * j + 4, :],
                              W2[bass.ds(e, 1), :, :].rearrange("e (c p) n -> p (e c) n", p=P)).then_inc(s_w4, 16)
                eng.dma_start(bcol[:, 8 + 4 * j:12 + 4 * j],
                              B1[bass.ds(e, 1), :].rearrange("e (c p) -> p (e c)", p=P)).then_inc(s_w4, 16)
                eng.dma_start(rowC[:, :] if j == 0 else rowD[:, :],
                              B2[bass.ds(e, 1), :].to_broadcast([P, H])).then_inc(s_w4, 16)
            phase_end(eng, 7)

            def store_out(p, c):
                eng.wait_ge(s_fin, p * 4 + 4)
                eng.dma_start(out[bass.ds(p * 256, 256), :].rearrange("(g p) f -> p g f", p=P),
                              ob[:, 2 * c:2 * c + 2, :]).then_inc(s_h[2][c], 16)
            with eng.Fori(0, FULL // 4) as u:
                for c in range(2):
                    store_out(u * 2 + c, c)
            eng.wait_ge(s_fin, 4 * PAIRS)
            eng.dma_start(out[FULL * P:N, :], ob[0:TAIL, 0, :]).then_inc(s_h[2][0], 16)
            eng.wait_ge(s_h[2][0], 16 * (FULL // 4 + 1))
            eng.wait_ge(s_h[2][1], 16 * (FULL // 4))
            phase_end(eng, 8)

        @block.gpsimd
        def _(eng):
            eng.memset(nxt_i, FAR).then_inc(s_big, 1)
            eng.memset(m1e[:, :, :], 0.0).then_inc(s_zero, 1)
            eng.memset(X[:, FULL:TILES, :], 0.0).then_inc(s_zero, 1)
            eng.memset(attr[:, 0, :], 0.0).then_inc(s_zero, 1)
            eng.memset(erec[:, 0:2, :], 0).then_inc(s_gl, 1)
            eng.wait_ge(s_gl, 1)
            eng.memset(erec[:, 0, :].rearrange("p (g k) -> p g k", k=3)[:, :, 1], FAR).then_inc(s_zero, 1)
            eng.memset(erec[:, 1, :].rearrange("p (g k) -> p g k", k=3)[:, :, 0], FAR).then_inc(s_zero, 1)
            eng.iota(iota_i[:, :], [[1, 512]], base=0, channel_multiplier=0).then_inc(s_const, 1)
            eng.iota(pidx_i[:, :], [[0, 1]], base=0, channel_multiplier=1).then_inc(s_const, 1)
            eng.iota(node_i[:, :], [[P, TILES]], base=0, channel_multiplier=1).then_inc(s_const, 1)
            eng.memset(ones[:, :], 1.0).then_inc(s_const, 1)
            eng.memset(ones_b[:, :], 1.0).then_inc(s_const, 1)
            eng.memset(b2spl[:, :], 0.0).then_inc(s_const, 1)
            eng.memset(zero50[:, :], 0.0).then_inc(s_const, 1)
            eng.memset(cnt[:, :, :], 0.0).then_inc(s_const, 1)
            eng.memset(XT[:, :, :], 0.0).then_inc(s_zero, 1)
            eng.memset(attrT[:, :, :], 1.0).then_inc(s_const, 1)

            eng.wait_ge(s_recs, 2)
            eng.wait_ge(s_flag, 1)
            unsorted = eng.value_load(flag_i[0:1, 0:1], min_val=0, max_val=1)
            with eng.If(unsorted > 0):
                eng.wait_ge(s_dstpos, 1)
                ev = edge_attr.rearrange("(p c) f -> p c f", c=COLS)
                staged = W[0:ROWS, 4096:4096 + CHUNK * GI].rearrange("p (c f) -> p c f", f=GI)
                with eng.Fori(0, COLS // CHUNK) as t:
                    eng.tensor_copy(sidx[0:ROWS, :], pos_dst[:, bass.ds(t * CHUNK, CHUNK)]).then_inc(s_stage, 1)
                    eng.tensor_copy(srec[0:ROWS, :, :], rec[:, bass.ds(t * CHUNK, CHUNK), :]).then_inc(s_stage, 1)
                    eng.dma_start(staged, ev[:, bass.ds(t * CHUNK, CHUNK), :]).then_inc(s_att, 16)
                    eng.wait_ge(s_stage, t * 2 + 2)
                    eng.wait_ge(s_att, t * 16 + 16)
                    standing(eng, apart_pool)
                    for c in range(CHUNK):
                        where = bass.IndirectOffsetOnAxis(ap=sidx[0:ROWS, c:c + 1], axis=0)
                        eng.indirect_dma_start(out=rec_d[:, :], out_offset=where, in_=srec[0:ROWS, c, :],
                                               in_offset=None).then_inc(s_perm, 16)
                        eng.indirect_dma_start(out=attr_s[:, :], out_offset=where, in_=staged[:, c, :],
                                               in_offset=None).then_inc(s_perm, 16)
                    eng.wait_ge(s_perm, (t + 1) * (32 * CHUNK))
            with eng.Else():
                eng.dma_start(rec_d[0:E, :].rearrange("(p c) k -> p c k", c=COLS), rec).then_inc(s_perm, 16)
                eng.wait_ge(s_perm, 16)
            eng.sem_inc(s_order, 1)
            eng.wait_ge(s_wfirst, 1)
            copy = eng.value_load(flag_i[0:1, 3:4], min_val=0, max_val=1)
            with eng.If(copy > 0):
                eng.dma_start(attr_s[0:E, :].rearrange("(p c) f -> p (c f)", c=COLS),
                              edge_attr.rearrange("(p c) f -> p (c f)", c=COLS)).then_inc(s_att, 16)
                eng.wait_ge(s_att, 16)
            with eng.Else():
                eng.sem_inc(apart_pool, 1)
            phase_end(eng, 0)

            def gather(k, u, s_recs_in, used, field, table, s_out):
                q, v, a = at(k, u)
                eng.wait_ge(s_recs_in[a], v * 16 + 16)
                wait(eng, used, q - GSET + 1)
                standing(eng, apart_pool)
                for g in range(GRP):
                    where = bass.IndirectOffsetOnAxis(ap=erec[:, a, 3 * g + field:3 * g + field + 1], axis=0)
                    eng.indirect_dma_start(out=Gt[:, a % GSET, g, :], out_offset=None, in_=table[:, :],
                                           in_offset=where).then_inc(s_out[a % GSET], 16)

            def stage_src(t, h, before):
                wait(eng, s_scat[h], before * (16 * HALF))
                to = slice(h * HALF, (h + 1) * HALF)
                eng.tensor_copy(sidx[0:ROWS, to], pos_src[:, bass.ds(t * HALF, HALF)]).then_inc(s_gl, 1)
                eng.tensor_copy(srec[0:ROWS, to, :], rec[:, bass.ds(t * HALF, HALF), :]).then_inc(s_gl, 1)

            def scatter_src(c, h):
                c = h * HALF + c
                where = bass.IndirectOffsetOnAxis(ap=sidx[0:ROWS, c:c + 1], axis=0)
                eng.indirect_dma_start(out=rec_s[:, :], out_offset=where, in_=srec[0:ROWS, c, :],
                                       in_offset=None).then_inc(s_scat[h], 16)

            def move_begin():
                eng.wait_ge(s_srcpos, 1)
                stage_src(0, 0, 0)
                eng.wait_ge(s_gl, 3)
                for c in range(HALF):
                    scatter_src(c, 0)

            def move(j, u):
                t = u - (MOVE_FROM - 1)
                if j == 0:
                    stage_src(t, 0, t)
                    eng.wait_ge(s_gl, t * 2 + 3)
                    standing(eng, apart_pool)
                for c in range(j * HALF // LSET, (j + 1) * HALF // LSET):
                    scatter_src(c, 0)

            def gathers1(count, narrow):
                steps(eng, lambda k, u, do: gather(k, u, s_ldr, e1["msg"], 0, h1, s_g), ("gather", 0),
                      count=count, ahead=GSET, fill=move, fills=(MOVE_FROM, MOVE_TO), before=move_begin)

            either(eng, 0, gathers1)
            phase_end(eng, 1)
            def move_pair(i):
                for h in range(2):
                    t = i * 2 + (MOVED + h)
                    stage_src(t, h, i + (0 if h else MOVED))
                    eng.wait_ge(s_gl, t * 2 + 3)
                    standing(eng, apart_pool)
                    for c in range(HALF):
                        scatter_src(c, h)

            move_pair(0)
            with eng.Fori(1, MOVE_PAIRS) as i:
                move_pair(i)
            for h in range(2):
                eng.wait_ge(s_scat[h], (MOVE_PAIRS + (0 if h else MOVED)) * (16 * HALF))
            eng.sem_inc(s_order, 1)
            phase_end(eng, 5)

            def gathers2(count, narrow):
                steps(eng, lambda k, u, do: gather(k, u, s_rec2, e2["agg"], 1, h2, s_g2), ("gather", 0),
                      count=count, ahead=GSET)

            either(eng, 1, gathers2)
            phase_end(eng, 6)

            def add_tile(k, u, do):
                t, _, a = at(k, u, per=NSET)
                eng.wait_ge(n3["cT"], t + 1)
                v = XT[:, :, bass.ds(t * P, P)]
                if isinstance(t, int) and t == 0:
                    eng.tensor_copy(added, v).then_inc(n3["sum"], 1)
                else:
                    eng.wait_ge(n3["sum"], t)
                    eng.tensor_tensor(added, added, v, ALU.add).then_inc(n3["sum"], 1)

            steps(eng, add_tile, ("add", 0), count=TILES, per=NSET, ahead=NSET)
            for k in range(7, 9):
                phase_end(eng, k)

        @block.scalar
        def _(eng):
            chain = Chain(eng, s_act)
            mat = lambda a: a.rearrange("(k p) n -> p k n", p=P)
            line = lambda a: a.rearrange("(e n) -> e n", e=1)
            down = lambda a: a.rearrange("(c p) -> p c", p=P)
            for t, v in ((wA, mat(aw_W)), (m2_sb, mat(m2_W)), (WrS, mat(Wr))):
                eng.dma_start(t[:, :, :], v).then_inc(s_w, 16)
            eng.wait_ge(s_zero, 1)
            for g in range(GRP):
                eng.dma_start(m1e[g * GI:(g + 1) * GI, g, :], m1_W).then_inc(s_w, 16)
                eng.dma_start(m1e[GRP * GI:GRP * GI + 1, g, :], line(m1_b)).then_inc(s_w, 16)
            eng.dma_start(bcol[:, 0:2], down(o1_b)).then_inc(s_w, 16)
            eng.dma_start(b2row[:, :], line(m2_b).to_broadcast([3, H])).then_inc(s_w, 16)
            eng.dma_start(rowA[:, :], line(aw_b).to_broadcast([P, H])).then_inc(s_w, 16)
            eng.dma_start(rowB[:, :], line(o2_b).to_broadcast([P, H])).then_inc(s_w, 16)
            eng.dma_start(rowD[:, :], wr.rearrange("f e -> e f").to_broadcast([P, H])).then_inc(s_w, 16)
            eng.dma_start(c1[:, 7:8], br.rearrange("(e n) -> e n", e=1).to_broadcast([P, 1])).then_inc(s_w, 16)
            eng.dma_start(sm[0:1, 11, :], line(br1)).then_inc(s_w, 16)
            eng.wait_ge(s_recs, 1)
            eng.activation(tmpc, ew, ACT.Sin, scale=TWO_PI).then_inc(s_cos, 1)

            def root(k, tiles=slice(0, TILES)):
                eng.wait_ge(s_var, k)
                eng.activation(rstd[:, tiles], vtmp[:, tiles], ACT.Sqrt).then_inc(s_rstd, 1)

            def transposed(s, dest, limit=None, **beside):
                def step(k, u, do):
                    t, _, a = at(k, u, per=NSET)
                    eng.wait_ge(s["T"], t + 1)
                    if limit is not None:
                        wait(eng, s[limit], t - NSET + 1)
                    eng.activation(dest(t, a), bank[a][:, 0:H].rearrange("p (k n) -> p k n", k=2),
                                   ACT.Copy).then_inc(s["cT"], 1)
                steps(eng, step, ("copy", 0), count=TILES, per=NSET, ahead=NSET, **beside)

            eng.wait_ge(s_recs, 2)

            def count_src(j, u):
                for n in range(2 if j == 0 else 1):
                    b = u * 5 + (j + (n if j == 0 else 1))
                    eng.wait_ge(s_cos, b + 1)
                    eng.activation(rankc, src_hi, ACT.Sign, scale=-1.0, bias=rs[0:ROWS, bass.ds(b, 1)],
                                   accum_out=cnt[0:ROWS, 1, bass.ds(b, 1)]).then_inc(s_cos, 1)

            root(1)
            transposed(p1, lambda t, a: xT[:, a, :, :], "mm", fill=count_src, fills=(0, TILES // 5))
            phase_end(eng, 0)

            eng.preload_act_table_set("natural_log_exp_and_others")

            def step1(s, u, do):
                q, _, a = at(s, u)
                b = a % 2
                if "exp1" in do:
                    eng.wait_ge(e1["L1"], q + 1)
                    wait(eng, e1["S1"], q - 1)
                    eng.activation(Eb1[:, b, :], bank[2 + b][:, :], ACT.Abs).then_inc(e1["abs1"], 1)
                    eng.wait_ge(e1["abs1"], q + 1)
                    eng.activation(Eb1[:, b, :], Eb1[:, b, :], ACT.Exp, scale=-1.0).then_inc(e1["exp1"], 1)
                q1, _, a1 = at(s, u, -2)
                b1_ = a1 % 2
                if "exp2" in do:
                    eng.wait_ge(e1["L2"], q1 + 1)
                    wait(eng, e1["msg"], q1 - 1)
                    eng.activation(Eb2[:, b1_, :], bank[4 + b1_][:, :], ACT.Exp).then_inc(e1["exp2"], 1)
                if "exp1" in do:
                    eng.wait_ge(e1["exp1"], q + 1)
                    eng.activation(Eb1[:, b, :], Eb1[:, b, :], ACT.Ln, bias=1.0).then_inc(e1["ln1"], 1)
                if "exp2" in do:
                    eng.wait_ge(e1["clamp2"], q1 + 1)
                    eng.activation(Eb2[:, b1_, :], Eb2[:, b1_, :], ACT.Ln, bias=1.0).then_inc(e1["ln2"], 1)
                q2, _, a2 = at(s, u, 2)
                b2_ = a2 % 2
                if "copy" in do:
                    eng.wait_ge(e1["T"], q2 + 1)
                    wait(eng, e1["L1"], q2 - 1)
                    eng.activation(attrT[0:GRP * GI, b2_, :], bank[b2_][0:GRP * GI, 0:P],
                                   ACT.Copy).then_inc(e1["cT"], 1)

            either(eng, 0, lambda count, narrow: steps(eng, step1, ("exp1", 0), ("exp2", 2), ("copy", -2), count=count))
            phase_end(eng, 1)

            eng.dma_start(o1_sb, mat(o1_W)).then_inc(s_w, 16)
            eng.dma_start(o2_sb, mat(o2_W)).then_inc(s_w, 16)

            def out1(k, u, do):
                q, _, b = at(k, u, per=2)
                if "L1" in do:
                    eng.wait_ge(o["L1"], q + 1)
                    wait(eng, o["S"], q - 1)
                    for h in range(2):
                        ins = eng.activation(Eb1[:, b, h * 256:h * 256 + 256],
                                             bank[2 + b][:, h * 256:h * 256 + 256], ACT.Exp, bias=bcol[:, h:h + 1])
                    ins.then_inc(o["exp"], 1)
                    eng.wait_ge(o["clamp"], q + 1)
                    eng.activation(Eb1[:, b, :], Eb1[:, b, :], ACT.Ln, bias=1.0).then_inc(o["ln"], 1)

            steps(eng, out1, ("L1", 0), count=PAIRS, per=2)
            phase_end(eng, 2)
            eng.dma_start(w1_sb, mat(w1)).then_inc(s_w2, 16)
            eng.dma_start(w2_sb, w2.rearrange("(c p) n -> p c n", p=P)).then_inc(s_w2, 16)
            eng.dma_start(bcol[:, 8:16], down(b1)).then_inc(s_w2, 16)
            eng.dma_start(rowC[:, :], line(b2).to_broadcast([P, H])).then_inc(s_w2, 16)
            eng.dma_start(wA[:, :, :], mat(L_WT)).then_inc(s_w2, 16)
            root(2)
            block_of = lambda t, a: XT[:, :, bass.ds(t * P, P)]
            eng.wait_ge(n2["begin"], 1)

            def norm2(k, u, do):
                if "norm" in do:
                    t, _, a = at(k, u, per=NSET)
                    wait(eng, n2["T"], t - NSET + 1)
                    wait(eng, n2["use"], t - NSET + 1)
                    wait(eng, s_jk, t - NSET + 1)
                    eng.activation(xn[:, a, :], X[:, bass.ds(t, 1), :].rearrange("p a n -> p (a n)"), ACT.Identity,
                                   bias=dtmp[:, bass.ds(t, 1)], scale=rstd[:, bass.ds(t, 1)]).then_inc(n2["xn"], 1)
                if "copy" in do:
                    t, _, a = at(k, u, -1, per=NSET)
                    eng.wait_ge(n2["T"], t + 1)
                    eng.activation(block_of(t, a), bank[a][:, 0:H].rearrange("p (k n) -> p k n", k=2),
                                   ACT.Copy).then_inc(n2["cT"], 1)

            steps(eng, norm2, ("norm", 0), ("copy", 1), count=TILES, per=NSET, ahead=NSET)
            eng.wait_ge(s_w2, 80)
            phase_end(eng, 3)

            def ffn_act(f, func, batches=False):
                def step(q, b):
                    for c in range(FCH):
                        m = FCH * q + c
                        eng.wait_ge(f["L1"], m + 1)
                        if c == 0:
                            wait(eng, f["L2"], q - 1)
                        eng.activation(Hb[:, b, c, :], bank[c % 4][:, 0:256], func,
                                       bias=bcol[:, 8 + c:9 + c]).then_inc(f["act"], 1)
                if batches:
                    for q in range(LAG):
                        step(q, q % 2)
                    with eng.Fori(0, BATCHES - 1) as i:
                        for j in range(BATCH):
                            step(i * BATCH + (LAG + j), (1 + j) % 2)
                            if j == 0:
                                root(i + 5, bass.ds(i * (2 * BATCH), 2 * BATCH))
                    root(BATCHES + 4, slice(2 * (PAIRS - LAG), 2 * (PAIRS - 1)))
                    root(BATCHES + 5, slice(2 * (PAIRS - 1), TILES))
                    return
                for q in range(3):
                    step(q, q % 2)
                with eng.Fori(0, (PAIRS - 3) // 2) as u:
                    for j in range(2):
                        step(u * 2 + 3 + j, (1 + j) % 2)

            ffn_act(f1, ACT.Gelu_apprx_tanh)
            phase_end(eng, 4)
            eng.wait_ge(s_deg, 1)
            eng.activation(rs[:, :], rs_t[:, :], ACT.Sqrt).then_inc(s_deg, 1)
            root(3)
            eng.dma_start(rowA[:, :], line(gamma).to_broadcast([P, H])).then_inc(s_w2, 16)
            eng.dma_start(rowB[:, :], line(beta).to_broadcast([P, H])).then_inc(s_w2, 16)

            def node2(k, u, do):
                if "copy" in do:
                    t, _, a = at(k, u, per=NSET)
                    eng.wait_ge(p2["T"], t + 1)
                    wait(eng, p2["mm"], t - NSET + 1)
                    eng.activation(xT[:, a, :, :], bank[a][:, 0:H].rearrange("p (k n) -> p k n", k=2),
                                   ACT.Copy).then_inc(p2["cT"], 1)
                if "out" in do:
                    t, v, a = at(k, u, -3, per=NSET)
                    eng.wait_ge(p2["self"], t + 1)
                    wait(eng, s_h[1][a], v * 16)
                    eng.activation(ob[:, a, :], bank[4 + a][:, 0:H], ACT.Copy,
                                   scale=rs[:, bass.ds(t, 1)]).then_inc(p2["out"], 1)

            steps(eng, node2, ("copy", 0), ("out", 3), count=TILES, per=NSET, ahead=NSET)
            eng.wait_ge(s_w2, 112)
            phase_end(eng, 5)
            phase_end(eng, 6)
            root(4)
            transposed(n3, block_of)
            for k in range(3):
                eng.wait_ge(s_w5, k + 1)
                n = 2 if k == 2 else NEXP
                eng.activation(sm[0:1, 3, 0:n], sm[0:1, 2, 0:n], ACT.Exp).then_inc(s_mqp, 1)
            phase_end(eng, 7)
            ffn_act(f2, ACT.Gelu, batches=True)
            phase_end(eng, 8)

        @block.tensor
        def _(eng):
            eng.wait_ge(s_const, 9)
            eng.wait_ge(s_cnt, 2)
            eng.matmul(bank[7][:, 0:1], ones[0:ROWS, :], c1[0:ROWS, 0:1], start=True, stop=True).then_inc(s_tot, 1)
            eng.wait_ge(s_w, 16 * 14)
            for k in range(2):
                eng.matmul(bank[6][0:3, 0:H], ones[:, 0:3], m2_sb[:, k, :], start=(k == 0), stop=(k == 1))
            eng.drain().then_inc(s_pe, 1)

            def count_edges():
                eng.wait_ge(s_cnt, 3)
                eng.matmul(bank[0][:, 0:TILES], ones[0:ROWS, :], cnt[0:ROWS, 0, :], start=True, stop=True)
                eng.matmul(bank[0][:, 64:64 + TILES], ones[0:ROWS, :], cnt[0:ROWS, 1, :], start=True, stop=True)
                eng.matmul(bank[5][0:ROWS, 192:192 + TILES], tri[0:ROWS, 0:ROWS], cnt[0:ROWS, 0, :], start=True, stop=True)
                eng.matmul(bank[5][0:ROWS, 256:256 + TILES], tri[0:ROWS, 0:ROWS], cnt[0:ROWS, 1, :], start=True, stop=True)\
                   .then_inc(s_tot, 1)

            def schedule(k):
                eng.wait_ge(s_mq, k)
                eng.matmul(bank[6][:, 0:NQ], dcast[:, :], Mq[:, :], start=True, stop=True)
                eng.matmul(bank[7][:, 0:NQ], vcast[:, :], Mq[:, :], start=True, stop=True).then_inc(s_sched, 1)

            def transposes(s, t, a):
                eng.wait_ge(s["xn"], t + 1)
                wait(eng, s["cT"], t - NSET + 1)
                for k in range(2):
                    ins = eng.transpose(bank[a][:, k * P:(k + 1) * P], xn[:, a, k * P:(k + 1) * P], ident[:, :])
                ins.then_inc(s["T"], 1)

            def node_products(s):
                def step(k, u, do):
                    if "T" in do:
                        t, _, a = at(k, u, per=NSET)
                        transposes(s, t, a)
                    if "mm" in do:
                        t, _, a = at(k, u, -2, per=NSET)
                        eng.wait_ge(s["cT"], t + 1)
                        wait(eng, s["out"], t - NSET + 1)
                        for c in range(2):
                            ins = eng.matmul(bank[4 + a][:, 0:H], xT[:, a, c, :], wA[:, c, :],
                                             start=(c == 0), stop=(c == 1))
                        ins.then_inc(s["mm"], 1)
                steps(eng, step, ("T", 0), ("mm", 2), count=TILES, per=NSET, ahead=NSET)

            node_products(p1)
            count_edges()
            schedule(1)

            def cast_first(k):
                eng.wait_ge(s_wfirst, k + 1)
                eng.matmul(bank[6][:, 0:NT], ones[0:1, :], first_f, start=True, stop=True).then_inc(s_wcast, 1)

            cast_first(0)
            phase_end(eng, 0)

            def step1(s, u, do, width):
                q4, _, a4 = at(s, u, 1)
                b = a4 % 2
                if "L1" in do:
                    eng.wait_ge(e1["cT"], q4 + 1)
                    wait(eng, e1["S1"], q4 - 1)
                    for h in range(2):
                        for g in range(GRP):
                            ins = eng.matmul(bank[2 + b][:, h * 256 + g * P:h * 256 + (g + 1) * P],
                                             m1e[:, g, h * P:(h + 1) * P], attrT[0:GRP * GI + 1, b, :],
                                             start=True, stop=True)
                    ins.then_inc(e1["L1"], 1)
                q1, _, a1 = at(s, u, -1)
                b = a1 % 2
                if "L2" in do:
                    eng.wait_ge(e1["S1"], q1 + 1)
                    wait(eng, e1["max2"], q1 - 1)
                    for g in range(GRP):
                        v = bank[4 + b][:, g * H:(g + 1) * H]
                        for k in range(2):
                            eng.matmul(v, S1[:, b, k, g * P:(g + 1) * P], m2_sb[:, k, :], start=(k == 0), stop=False)
                        ins = eng.matmul(v, ones_b[:, :], b2spl[:, :], start=False, stop=True)
                    ins.then_inc(e1["L2"], 1)
                q2, _, a2 = at(s, u, -3)
                b = a2 % 2
                if "agg" in do:
                    eng.wait_ge(e1["msg"], q2 + 1)
                    eng.wait_ge(e1["oh"], q2 + 1)
                    wait(eng, e1["add"], q2 - 1)
                    for h in range(2):
                        for g in range(GRP):
                            ins = eng.matmul(bank[6 + b][:, h * P:h * P + width], Mb[:, b, g, h * P:(h + 1) * P],
                                             Ob[:, b, g, 0:width], start=(g == 0), stop=(g == GRP - 1))
                    ins.then_inc(e1["agg"], 1)
                q3, u3, a3 = at(s, u, 3)
                b = a3 % 2
                if "T" in do:
                    eng.wait_ge(s_ld[a3], u3 * 16 + 16)
                    wait(eng, e1["cT"], q3 - 1)
                    standing(eng, apart_pe)
                    eng.transpose(bank[b][0:GRP * GI, 0:P], attr[:, a3, :], ident[:, :]).then_inc(e1["T"], 1)

            def products1(count, narrow):
                steps(eng, lambda s, u, do: step1(s, u, do, WIN if narrow else P),
                      ("L2", 1), ("agg", 3), ("T", -3), ("L1", -1), count=count)

            either(eng, 0, products1)
            phase_end(eng, 1)

            eng.wait_ge(s_w, 16 * 16)
            for k in range(2):
                ins = eng.matmul(bank[7][:, 0:H], ones[:, :], o2_sb[:, k, :], start=(k == 0), stop=(k == 1))
            ins.then_inc(s_pe, 1)

            def out1(k, u, do):
                q, _, b = at(k, u, per=2)
                if "L1" in do:
                    wait(eng, o["S"], q - 1)
                    for h in range(2):
                        for i in range(2):
                            ins = eng.matmul(bank[2 + b][:, h * 256:h * 256 + 256], o1_sb[:, i, h * P:(h + 1) * P],
                                             XT[:, i, bass.ds(q * 256, 256)], start=(i == 0), stop=(i == 1))
                    ins.then_inc(o["L1"], 1)
                if "L2" in do:
                    r, _, c = at(k, u, -2, per=2)
                    eng.wait_ge(o["S"], r + 1)
                    wait(eng, o["add"], r - 1)
                    for g in range(2):
                        for i in range(2):
                            ins = eng.matmul(bank[4 + c][:, g * H:(g + 1) * H], S1[:, c, i, g * P:(g + 1) * P],
                                             o2_sb[:, i, :], start=(i == 0), stop=(i == 1))
                    ins.then_inc(o["L2"], 1)

            steps(eng, out1, ("L1", 0), ("L2", 2), count=PAIRS, per=2)
            phase_end(eng, 2)

            def norm_transposes(s):
                def step(k, u, do):
                    t, _, a = at(k, u, per=NSET)
                    transposes(s, t, a)
                steps(eng, step, ("T", 0), count=TILES, per=NSET, ahead=NSET)

            norm_transposes(n2)
            for r in range(8):
                eng.wait_ge(s_topk, r + 1)
                eng.matmul(bank[4][:, 0:15], ones[:, :], gates[:, 8, 0:15], start=True, stop=True).then_inc(s_ctp, 1)
            eng.wait_ge(s_topk, 9)
            eng.matmul(bank[4][:, 0:TILES], ones[:, :], gates[:, 0, :], start=True, stop=True)
            eng.matmul(bank[4][:, 64:64 + TILES], ones[:, :], gates[:, 1, :], start=True, stop=True)
            eng.matmul(bank[4][:, 128:128 + TILES], tri[:, :], gates[:, 1, :], start=True, stop=True).then_inc(s_ctp, 1)
            phase_end(eng, 3)

            def ffn(f, degrees=False):
                def count_degrees(q, b, first=False, last=False):
                    eng.wait_ge(s_ohl, q + 1)
                    for c in range(DCOL):
                        ins = eng.matmul(bank[5][:, 0:TILES], ohl[b][0:ROWS, c, :], ohh[b][0:ROWS, c, :],
                                         start=(first and c == 0), stop=(last and c == DCOL - 1))
                    ins.then_inc(s_ctrd, 1)

                def step(q, b, do):
                    if degrees and "L2" in do:
                        peeled = isinstance(q, int)
                        count_degrees(q - 1, 1 - b, peeled and q == 1, peeled and q == PAIRS)
                    if "L1" in do:
                        for c in range(FCH):
                            m = FCH * q + c
                            wait(eng, f["act"], m - 3)
                            for k in range(2):
                                ins = eng.matmul(bank[c % 4][:, 0:256], w1_sb[:, k, c * P:(c + 1) * P],
                                                 XT[:, k, bass.ds(q * 256, 256)], start=(k == 0), stop=(k == 1))
                            ins.then_inc(f["L1"], 1)
                    if "L2" in do:
                        r, d = q - 1, 1 - b
                        eng.wait_ge(f["act"], r * FCH + FCH)
                        wait(eng, f["y"], r - 1)
                        for g in range(2):
                            for c in range(FCH):
                                ins = eng.matmul(bank[6 + d][:, g * H:(g + 1) * H], Hb[:, d, c, g * P:(g + 1) * P],
                                                 w2_sb[:, c, :], start=(c == 0), stop=(c == FCH - 1))
                        ins.then_inc(f["L2"], 1)
                pair_steps(eng, step)

            ffn(f1, degrees=True)
            phase_end(eng, 4)
            schedule(2)
            node_products(p2)
            cast_first(1)
            phase_end(eng, 5)

            def products2(count, narrow):
                blocks = 2 if narrow else 1
                def agg2(k, u, do):
                    q, v, a = at(k, u)
                    b = a % 2
                    eng.wait_ge(s_g2[a % GSET], gathered(v, a))
                    eng.wait_ge(e2["oh"], q + 1)
                    wait(eng, e2["add"], (q - 1) * blocks)
                    for j in range(blocks):
                        for g in range(GRP):
                            hot = Ow[:, b, g, j * P:(j + 1) * P] if narrow else Ob[:, b, g, :]
                            ins = eng.matmul(bank[b][:, j * H:(j + 1) * H], hot, Gt[:, a % GSET, g, :],
                                             start=(g == 0), stop=(g == GRP - 1))
                    ins.then_inc(e2["agg"], 1)
                steps(eng, agg2, ("agg", 0), count=count)

            either(eng, 1, products2)
            phase_end(eng, 6)
            norm_transposes(n3)
            eng.wait_ge(s_topk, 10)
            for k in range(2):
                ins = eng.matmul(bank[4][0:1, 0:NEXP], c1[:, k:k + 1], WrS[:, k, :], start=(k == 0), stop=(k == 1))
            ins.then_inc(s_ctp, 1)
            eng.wait_ge(s_topk, 11)
            eng.matmul(bank[4][:, 64:66], ones[0:1, :], sm[0:1, 8, 0:2], start=True, stop=True).then_inc(s_ctp, 1)
            phase_end(eng, 7)
            ffn(f2)
            phase_end(eng, 8)

        @block.vector
        def _(eng):
            chain = Chain(eng, s_dve)
            eng.wait_ge(s_const, 3)
            chain(eng.tensor_copy(iota_f[:, :], iota_i[:, :]))
            chain(eng.tensor_copy(pidx[:, :], pidx_i[:, :]))
            chain(eng.tensor_copy(iota_b[:, :], iota_i[:, 0:P]))
            chain(eng.tensor_scalar(ident[:, :], iota_f[:, 0:P], pidx[:, 0:1], None, ALU.is_equal))
            chain(eng.tensor_scalar(tri[:, :], iota_f[:, 0:P], pidx[:, 0:1], None, ALU.is_gt))
            chain(eng.tensor_scalar(valid[:, :], node_i[:, :], float(N), None, ALU.is_lt))
            chain(eng.tensor_copy(iota16[:, :], iota_i[:, 0:16]))
            chain(eng.tensor_scalar(rs[:, :], iota_f[:, 0:TILES], 0.5, None, ALU.add))
            eng.sem_inc(s_cnt, 1)
            eng.wait_ge(s_edges, 80)
            eng.wait_ge(s_const, 8)
            chain(eng.tensor_tensor(maskc, dst_i, nxt_i, ALU.is_gt))
            chain(eng.tensor_reduce(c1[0:ROWS, 0:1], maskc, AX.X, ALU.add))
            eng.sem_inc(s_cnt, 1)
            chain(eng.tensor_scalar(ew, ew, 0.5 / CUTOFF, 0.25, ALU.mult, ALU.add))
            chain(eng.tensor_scalar(tmpc, ew, ROUND, None, ALU.add))
            chain(eng.tensor_scalar(tmpc, tmpc, ROUND, None, ALU.subtract))
            chain(eng.tensor_tensor(ew, ew, tmpc, ALU.subtract))
            eng.sem_inc(s_recs, 1)
            chain(eng.tensor_copy(rec[:, :, 0], src_i))
            chain(eng.tensor_copy(rec[:, :, 1], dst_i))
            chain(eng.tensor_scalar(nxt_i, dst_i, 7, None, ALU.logical_shift_right))
            chain(eng.tensor_copy(dst_hi, nxt_i))
            chain(eng.tensor_scalar(nxt_i, src_i, 7, None, ALU.logical_shift_right))
            chain(eng.tensor_copy(src_hi, nxt_i))
            chain(eng.tensor_scalar(nxt_i, src_i, P - 1, None, ALU.bitwise_and))
            chain(eng.tensor_copy(src_lo, nxt_i))
            eng.wait_ge(s_cos, 1)
            chain(eng.tensor_scalar(recf[:, :, 2], tmpc, 0.5, 0.5, ALU.mult, ALU.add))
            eng.sem_inc(s_recs, 1)
            eng.wait_ge(s_tot, 1)
            chain(eng.tensor_scalar(flag_i[:, 0:1], bank[7][:, 0:1], 0.5, None, ALU.is_gt))
            eng.sem_inc(s_flag, 1)

            def first_of(row, k):
                chain(eng.tensor_tensor_scan(s50[:, 6, :], tot[:, k, :], zero50[:, :], 0.0, ALU.add, ALU.add))
                chain(eng.tensor_tensor(row, s50[:, 6, :], tot[:, k, :], ALU.subtract))

            def schedule(k, turn):
                start, tiles, first, base, delta = (s50[:, j, :] for j in range(5))
                first_of(start, k)
                chain(eng.tensor_scalar(s50_i[:, :], tot[:, k, :], float(SUP - 1), None, ALU.add))
                chain(eng.tensor_scalar(s50_i[:, :], s50_i[:, :], SUP.bit_length() - 1, None, ALU.logical_shift_right))
                chain(eng.tensor_copy(tiles, s50_i[:, :]))
                chain(eng.tensor_tensor_scan(s50[:, 6, :], tiles, zero50[:, :], 0.0, ALU.add, ALU.add))
                chain(eng.tensor_tensor(first, s50[:, 6, :], tiles, ALU.subtract))
                chain(eng.scalar_tensor_tensor(base, first, float(-SUP), start, ALU.mult, ALU.add))
                chain(eng.tensor_copy(delta, base))
                chain(eng.tensor_tensor(delta[:, 1:TILES], base[:, 1:TILES], base[:, 0:TILES - 1], ALU.subtract))
                for v, c in ((first, 2), (delta, 3)):
                    chain(eng.tensor_tensor(s50[:, 5, :], v, ident[:, 0:TILES], ALU.mult))
                    chain(eng.tensor_reduce(c1[:, c:c + 1], s50[:, 5, :], AX.X, ALU.add))
                chain(eng.tensor_scalar(vcast, pidx[:, 0:1].to_broadcast([P, P]), float(TILES), None, ALU.is_lt))
                chain(eng.tensor_scalar(dcast[:, :], c1[:, 3:4].to_broadcast([P, P]), 0.0, None, ALU.add))
                chain(eng.tensor_scalar(Mq[:, :], iota_f[:, 0:NQ], c1[:, 2:3], None, ALU.is_ge))
                eng.sem_inc(s_mq, 1)
                eng.wait_ge(s_sched, turn)
                chain(eng.scalar_tensor_tensor(nbase[:, :], iota_f[:, 0:NQ], float(SUP), bank[6][:, 0:NQ],
                                               ALU.mult, ALU.add))
                chain(eng.tensor_scalar(offs_i[:, :], nbase[:, :], float(E), None, ALU.min))
                chain(eng.tensor_scalar(blk_i[:, :], bank[7][:, 0:NQ], -1.0, None, ALU.add))
                chain(eng.tensor_scalar(nbase[:, :], bank[7][:, 0:NQ], -float(P), float(P), ALU.mult, ALU.add))

            def places_begin(link, k, off_at):
                link(eng.tensor_tensor_scan(s50[:, 6, :], tot[:, k, :], zero50[:, :], 0.0, ALU.add, ALU.add))
                link(eng.tensor_tensor(s50[:, 0, :], s50[:, 6, :], tot[:, k, :], ALU.subtract))
                link(eng.scalar_tensor_tensor(off0[0:ROWS, :], bank[5][0:ROWS, off_at:off_at + TILES], -1.0,
                                              s50[0:ROWS, 0, :], ALU.add, ALU.add))
                link(eng.memset(tmpc, 0.0))
                link(eng.memset(rankc, 0.0))

            def places_of(key, b, part):
                if part == 0:
                    return eng.tensor_scalar(maskc, key, iota_f[0:ROWS, bass.ds(b, 1)], None, ALU.is_equal)
                if part == 1:
                    return eng.tensor_tensor_scan(scanc, maskc, tmpc, off0[0:ROWS, bass.ds(b, 1)], ALU.add, ALU.add)
                return eng.copy_predicated(rankc, maskc_i, scanc)

            def measure(t, tile, s_out):
                eng.bn_stats(stat[:, bass.ds(t, 1), :].rearrange("p a k -> p (a k)"), tile).then_inc(s_out, 1)

            def measure_all():
                with eng.Fori(0, TILES // 5) as u:
                    for j in range(5):
                        measure(u * 5 + j, tile_of_x(u * 5 + j), s_stat)

            def combine(tiles):
                me, mo, ve, vo = (stat[:, tiles, k] for k in (1, 4, 2, 5))
                m, d, v = mean[:, tiles], dtmp[:, tiles], vtmp[:, tiles]
                chain(eng.tensor_tensor(m, me, mo, ALU.add))
                chain(eng.tensor_tensor(d, me, mo, ALU.subtract))
                chain(eng.tensor_tensor(v, ve, vo, ALU.add))
                chain(eng.tensor_scalar(m, m, 0.5, None, ALU.mult))
                chain(eng.tensor_tensor(d, d, d, ALU.mult))
                chain(eng.tensor_scalar(d, d, 0.25, LN_EPS, ALU.mult, ALU.add))
                chain(eng.scalar_tensor_tensor(v, v, 1.0 / H, d, ALU.mult, ALU.add))
                standing(eng, apart_dve)
                chain(eng.reciprocal(v, v))
                eng.sem_inc(s_var, 1)

            def statistics(turn):
                eng.wait_ge(s_stat, TILES * turn)
                combine(slice(0, TILES))
                eng.wait_ge(s_rstd, turn)
                chain(eng.tensor_tensor(rstd, rstd, valid[:, :], ALU.mult))

            tile_of_x = lambda t: X[:, bass.ds(t, 1), :].rearrange("p a n -> p (a n)")

            def normed(dest, t, source=None):
                return eng.tensor_scalar(dest, source if source is not None else tile_of_x(t),
                                         mean[:, bass.ds(t, 1)], rstd[:, bass.ds(t, 1)], ALU.subtract, ALU.mult)

            def node_tiles(s, s_dma, finish, **beside):
                def step(k, u, do):
                    if "norm" in do:
                        t, _, a = at(k, u, per=NSET)
                        wait(eng, s["T"], t - NSET + 1)
                        normed(xn[:, a, :], t).then_inc(s["xn"], 1)
                    if "finish" in do:
                        t, v, a = at(k, u, -3, per=NSET)
                        eng.wait_ge(s["mm"], t + 1)
                        if s_dma:
                            wait(eng, s_dma[a], v * 16)
                        finish(t, a)
                steps(eng, step, ("norm", 0), ("finish", 3), count=TILES, per=NSET, ahead=NSET, **beside)

            eng.wait_ge(s_x, 32)
            measure_all()
            statistics(1)

            def finish1(t, a):
                eng.tensor_tensor(ob[:, a, :], bank[4 + a][:, 0:H], rowA[:, :], ALU.add).then_inc(p1["out"], 1)

            def count_dst(j, u):
                for n in range(2 if j == 0 else 1):
                    b = u * 5 + (j + (n if j == 0 else 1))
                    eng.wait_ge(s_cnts, b + 1)
                    eng.tensor_scalar(maskc, dst_hi, iota_f[0:ROWS, bass.ds(b, 1)], 0.0, ALU.is_equal,
                                      ALU.add, accum_out=cnt[0:ROWS, 0, bass.ds(b, 1)]).then_inc(s_cnts, 1)

            eng.sem_inc(s_cnts, 1)
            eng.wait_ge(s_pe, 1)
            eng.wait_ge(s_w, 16 * 14)
            chain(eng.scalar_tensor_tensor(b2row[:, :], bank[6][0:3, 0:H], -LOG2, b2row[:, :], ALU.mult, ALU.add))
            part = rowC[0:3, :]
            chain(eng.memset(part, 0.0))
            for k in range(3):
                chain(eng.tensor_copy(b2spl[0:3, :], b2row[:, :]))
                chain(eng.tensor_tensor(b2row[:, :], b2row[:, :], b2spl[0:3, :], ALU.subtract))
                chain(eng.tensor_scalar(c1[0:3, 1:2], pidx[0:3, :], float(k), None, ALU.is_equal))
                chain(eng.scalar_tensor_tensor(part, b2spl[0:3, :], c1[0:3, 1:2], part, ALU.mult, ALU.add))
            chain(eng.tensor_copy(b2spl[0:3, :], part))
            node_tiles(p1, s_h[0], finish1, fill=count_dst, fills=(0, TILES // 5))
            eng.wait_ge(s_cnts, TILES + 1)
            eng.wait_ge(s_cos, TILES + 1)
            upto = s50[0:ROWS, 6, :]
            chain(eng.tensor_scalar(upto, cnt[0:ROWS, 1, :], 0.5, COLS / 2, ALU.mult, ALU.add))
            chain(eng.tensor_copy(cnt[0:ROWS, 1, 0:1], upto[:, 0:1]))
            chain(eng.tensor_tensor(cnt[0:ROWS, 1, 1:TILES], upto[:, 1:TILES], upto[:, 0:TILES - 1], ALU.subtract))
            eng.sem_inc(s_cnt, 1)
            eng.wait_ge(s_tot, 2)
            chain(eng.tensor_copy(tot[:, :, :], bank[0][:, 0:128].rearrange("p (k t) -> p k t", k=2)[:, :, 0:TILES]))
            schedule(0, 1)
            unsorted = eng.value_load(flag_i[0:1, 0:1], min_val=0, max_val=1)
            with eng.If(unsorted > 0):
                link = Chain(eng, s_dvu)
                places_begin(link, 0, 192)
                with eng.Fori(0, TILES) as b:
                    link.enter(b, 0, 3)
                    for part in range(3):
                        if part == 2:
                            standing(eng, apart_dve)
                        link(places_of(dst_hi, b, part))
                link.leave(TILES)
                link(eng.tensor_copy(pos_dst, rankc))
                eng.sem_inc(s_dstpos, 1)
            with eng.Else():
                eng.sem_inc(s_dstpos, 1)
            places_begin(chain, 1, 256)

            def windows(k):
                eng.wait_ge(s_win, 48 * (k + 1))
                if k:
                    chain(eng.tensor_scalar(ends, ends, 7, None, ALU.logical_shift_right))
                chain(eng.tensor_tensor(spread, ends[:, 1, :], ends[:, 0, :], ALU.subtract))
                narrow, in_order = c1[0:1, 6:7], spread[:, 0:1]
                chain(eng.tensor_reduce(narrow, spread, AX.X, ALU.max))
                chain(eng.tensor_scalar(narrow, narrow, float(2 if k else WIN), None, ALU.is_lt))
                if k == 0:
                    chain(eng.tensor_scalar(in_order, flag_i[0:1, 0:1], 1.0, None, ALU.is_lt))
                    chain(eng.tensor_tensor(narrow, narrow, in_order, ALU.mult))
                    chain(eng.tensor_tensor(flag_i[0:1, 3:4], in_order, narrow, ALU.subtract))
                chain(eng.tensor_copy(flag_i[0:1, k + 1:k + 2], narrow))
                chain(eng.tensor_scalar(first_f, ends[:, 0, :], float(TILES - 2 if k else NPAD - WIN), None, ALU.min))
                eng.sem_inc(s_wfirst, 1)
                eng.wait_ge(s_wcast, k + 1)
                chosen = eng.value_load(flag_i[0:1, k + 1:k + 2], min_val=0, max_val=1)
                with eng.If(chosen > 0):
                    link = Chain(eng, s_narrow[k])
                    link(eng.tensor_scalar(nbase[:, 0:NT], bank[6][:, 0:NT], float(-P if k else -1), None, ALU.mult))
                    link(eng.tensor_copy(blk_i[0:1, 0:NT], first_f))
                with eng.Else():
                    eng.sem_inc(s_narrow[k], 2)

            windows(0)
            phase_end(eng, 0)

            def step1(s, u, do, width):
                q0, _, a0 = at(s, u)
                b0 = a0 % 2
                q1, u1, a1 = at(s, u, -2)
                b1_ = a1 % 2
                q2, _, a2 = at(s, u, -4)
                b2_ = a2 % 2
                if "two" in do:
                    eng.wait_ge(e1["exp2"], q1 + 1)
                    eng.tensor_scalar(Eb2[:, b1_, :], Eb2[:, b1_, :], EXP_TOP, None, ALU.min).then_inc(e1["clamp2"], 1)
                if "one" in do:
                    eng.wait_ge(e1["ln1"], q0 + 1)
                    wait(eng, e1["L2"], q0 - 1)
                    eng.scalar_tensor_tensor(S1[:, b0, :, :].rearrange("p k n -> p (k n)"), bank[2 + b0][:, :], 0.0,
                                             Eb1[:, b0, :], ALU.max, ALU.add).then_inc(e1["S1"], 1)
                if "two" in do:
                    eng.wait_ge(s_ldr[a1], u1 * 16 + 16)
                    wait(eng, e1["agg"], q1 - 1)
                    er = erec[:, a1, :].rearrange("p (g k) -> p g k", k=3)
                    eng.tensor_tensor(dl[:, b1_, :], er[:, :, 1], nbase[:, bass.ds(q1, 1)].to_broadcast([P, GRP]),
                                      ALU.add).then_inc(s_dl, 1)
                    eng.wait_ge(s_dl, q1 + 1)
                    for g in range(GRP):
                        ins = eng.tensor_scalar(Ob[:, b1_, g, 0:width], iota_f[:, 0:width], dl[:, b1_, g:g + 1],
                                                erec[:, a1, 3 * g + 2:3 * g + 3].bitcast(F32), ALU.is_equal, ALU.mult)
                    ins.then_inc(e1["oh"], 1)
                    eng.wait_ge(e1["ln2"], q1 + 1)
                    eng.tensor_tensor(Eb2[:, b1_, :], bank[4 + b1_][:, :], Eb2[:, b1_, :], ALU.max).then_inc(e1["max2"], 1)
                if "add" in do:
                    r = eng.value_load(blk_i[0:1, bass.ds(q2, 1)], min_val=0,
                                       max_val=TILES - 1 if width == P else NPAD - width)
                    eng.wait_ge(e1["agg"], q2 + 1)
                    wait(eng, e1["add"], q2)
                    v = XT[:, :, bass.ds(r * P if width == P else r, width)]
                    eng.tensor_tensor(v, bank[6 + b2_][:, 0:256].rearrange("p (h n) -> p h n", h=2)[:, :, 0:width], v,
                                      ALU.add).then_inc(e1["add"], 1)
                if "two" in do:
                    eng.wait_ge(s_g[a1 % GSET], gathered(u1, a1))
                    eng.wait_ge(e1["max2"], q1 + 1)
                    eng.scalar_tensor_tensor(Mb[:, b1_, :, :].rearrange("p g n -> p (g n)"), Eb2[:, b1_, :], -LOG2,
                                             Gt[:, a1 % GSET, :, :].rearrange("p g n -> p (g n)"), ALU.add, ALU.mult)\
                       .then_inc(e1["msg"], 1)

            def order(j, u):
                if j in (0, 1, 2, 4, 5, 6):
                    n, part = j - j // 4, j % 4
                    if part:
                        eng.wait_ge(s_fill, u * 6 + n)
                    if part == 2:
                        standing(eng, apart_dve)
                    places_of(src_hi, u * 2 + j // 4, part).then_inc(s_fill, 1)

            def order_end():
                eng.wait_ge(s_fill, 3 * TILES)
                eng.tensor_copy(pos_src, rankc).then_inc(s_srcpos, 1)

            def arithmetic1(count, narrow):
                steps(eng, lambda s, u, do: step1(s, u, do, WIN if narrow else P), ("one", 0), ("two", 2), ("add", 4),
                      count=count, fill=order, fills=(0, ORDER_TURNS), after=order_end)

            either(eng, 0, arithmetic1)
            phase_end(eng, 1)

            eng.wait_ge(s_pe, 2)
            chain(eng.scalar_tensor_tensor(rowB[:, :], bank[7][:, 0:H], -LOG2, rowB[:, :], ALU.mult, ALU.add))

            def out1(k, u, do):
                q, _, b = at(k, u, per=2)
                if "L1" in do:
                    eng.wait_ge(o["exp"], q + 1)
                    eng.tensor_scalar(Eb1[:, b, :], Eb1[:, b, :], EXP_TOP, None, ALU.min).then_inc(o["clamp"], 1)
                if "L2" in do:
                    r, _, c = at(k, u, -2, per=2)
                    eng.wait_ge(o["L2"], r + 1)
                    wait(eng, o["add"], r)
                    v = X[:, bass.ds(r * 2, 2), :]
                    t3 = tmp.rearrange("p (g n) -> p g n", g=2)
                    eng.tensor_tensor(t3, bank[4 + c][:, :].rearrange("p (g n) -> p g n", g=2),
                                      rowB[:, :].unsqueeze(1).to_broadcast([P, 2, H]), ALU.add).then_inc(s_tmp, 1)
                    eng.wait_ge(s_tmp, r + 1)
                    eng.tensor_tensor(v, v, t3, ALU.add).then_inc(o["add"], 1)
                if "L1" in do:
                    eng.wait_ge(o["ln"], q + 1)
                    wait(eng, o["L2"], q - 1)
                    for h in range(2):
                        ins = eng.scalar_tensor_tensor(S1[:, b, h, :], bank[2 + b][:, h * 256:h * 256 + 256],
                                                       bcol[:, h:h + 1], Eb1[:, b, h * 256:h * 256 + 256],
                                                       ALU.add, ALU.max)
                    ins.then_inc(o["S"], 1)
                if "L2" in do:
                    eng.wait_ge(o["add"], r + 1)
                    for g in range(2):
                        measure(r * 2 + g, tile_of_x(r * 2 + g), s_stat)

            steps(eng, out1, ("L1", 0), ("L2", 2), count=PAIRS, per=2)
            phase_end(eng, 2)

            statistics(2)
            chain(eng.scalar_tensor_tensor(dtmp, mean, -1.0, rstd, ALU.mult, ALU.mult))
            eng.sem_inc(n2["begin"], 1)

            def norm2(k, u, do):
                t, _, a = at(k, u, per=NSET)
                eng.wait_ge(n2["xn"], t + 1)
                eng.tensor_tensor(tile_of_x(t), tile_of_x(t), xn[:, a, :], ALU.add).then_inc(n2["use"], 1)
                wait(eng, s_jk, t - 1)
                eng.scalar_tensor_tensor(tmp[:, (a % 2) * H:(a % 2 + 1) * H], xn[:, a, :], 1.0, rowD[:, :],
                                         ALU.mult, ALU.mult, accum_out=wrt[:, bass.ds(t, 1)]).then_inc(s_jk, 1)

            steps(eng, norm2, ("use", 0), count=TILES, per=NSET, ahead=NSET)
            eng.wait_ge(s_jk, TILES)
            chain(eng.tensor_scalar(wrt[:, :], wrt[:, :], c1[:, 7:8], None, ALU.add))
            chain(eng.tensor_tensor(gates[:, 2, :], wrt[:, :], valid[:, :], ALU.mult))
            chain(eng.tensor_scalar(gates[:, 3, :], valid[:, :], -LOW, LOW, ALU.mult, ALU.add))
            chain(eng.tensor_tensor(gates[:, 2, :], gates[:, 2, :], gates[:, 3, :], ALU.add))
            cand, sign, best, digit = (key_i[:, k, 0:15] for k in range(4))
            chain(eng.memset(best, 0))
            for r in range(8):
                shift = 28 - 4 * r
                chain(eng.tensor_scalar(cand, iota16[:, 1:16], shift, None, ALU.logical_shift_left))
                chain(eng.tensor_tensor(cand, cand, best, ALU.bitwise_or))
                chain(eng.tensor_scalar(cand, cand, -2 ** 31, None, ALU.bitwise_xor))
                chain(eng.tensor_scalar(sign, cand, 31, 2 ** 31 - 1, ALU.arith_shift_right, ALU.bitwise_and))
                chain(eng.tensor_tensor(cand, cand, sign, ALU.bitwise_xor))
                chain(eng.tensor_tensor(cmpb, gates[:, 2, :].unsqueeze(1).to_broadcast([P, 15, TILES]),
                                        cand.bitcast(F32).unsqueeze(2).to_broadcast([P, 15, TILES]), ALU.is_ge))
                chain(eng.tensor_reduce(gates[:, 8, 0:15], cmpb, AX.X, ALU.add))
                eng.sem_inc(s_topk, 1)
                eng.wait_ge(s_ctp, r + 1)
                chain(eng.tensor_scalar(gates[:, 9, 0:15], bank[4][:, 0:15], float(K_SEL), None, ALU.is_ge))
                chain(eng.tensor_reduce(c1[:, 4:5], gates[:, 9, 0:15], AX.X, ALU.add))
                chain(eng.tensor_copy(digit, c1[:, 4:5].to_broadcast([P, 15])))
                chain(eng.tensor_scalar(digit, digit, shift, None, ALU.logical_shift_left))
                chain(eng.tensor_tensor(best, best, digit, ALU.bitwise_or))
            chain(eng.tensor_scalar(cand, best, -2 ** 31, None, ALU.bitwise_xor))
            chain(eng.tensor_scalar(sign, cand, 31, 2 ** 31 - 1, ALU.arith_shift_right, ALU.bitwise_and))
            chain(eng.tensor_tensor(cand, cand, sign, ALU.bitwise_xor))
            least = cand.bitcast(F32)[:, 0:1]
            chain(eng.tensor_scalar(gates[:, 0, :], gates[:, 2, :], least, None, ALU.is_gt))
            chain(eng.tensor_scalar(gates[:, 1, :], gates[:, 2, :], least, None, ALU.is_equal))
            eng.sem_inc(s_topk, 1)
            eng.wait_ge(s_ctp, 9)
            chain(eng.tensor_copy(gates[:, 4, :], bank[4][:, 64:64 + TILES]))
            chain(eng.tensor_tensor_scan(gates[:, 5, :], gates[:, 4, :], zero50[:, :], 0.0, ALU.add, ALU.add))
            chain(eng.tensor_tensor(gates[:, 5, :], gates[:, 5, :], gates[:, 4, :], ALU.subtract))
            chain(eng.tensor_tensor(gates[:, 5, :], gates[:, 5, :], bank[4][:, 128:128 + TILES], ALU.add))
            chain(eng.tensor_reduce(c1[:, 5:6], bank[4][:, 0:TILES], AX.X, ALU.add))
            chain(eng.tensor_scalar(gates[:, 5, :], gates[:, 5, :], c1[:, 5:6], None, ALU.add))
            chain(eng.tensor_scalar(gates[:, 5, :], gates[:, 5, :], float(K_SEL), None, ALU.is_lt))
            chain(eng.tensor_tensor(gates[:, 5, :], gates[:, 5, :], gates[:, 1, :], ALU.mult))
            chain(eng.tensor_tensor(gates[:, 5, :], gates[:, 5, :], gates[:, 0, :], ALU.add))
            chain(eng.tensor_tensor(gate[:, :], gates[:, 5, :], wrt[:, :], ALU.mult))
            phase_end(eng, 3)

            def ffn1(q, b, do):
                if "L1" in do:
                    wait(eng, s_ctrd, q - 1)
                    for oh, key, n in ((ohl[b], src_lo, P), (ohh[b], src_hi, TILES)):
                        ins = eng.tensor_tensor(oh[0:ROWS, :, :],
                                                iota_b[0:ROWS, 0:n].unsqueeze(1).to_broadcast([ROWS, DCOL, n]),
                                                key[:, bass.ds(q * DCOL, DCOL)].unsqueeze(2)
                                                .to_broadcast([ROWS, DCOL, n]), ALU.is_equal)
                    ins.then_inc(s_ohl, 1)
                if "L2" in do:
                    r, c = q - 1, 1 - b
                    eng.wait_ge(f1["L2"], r + 1)
                    wait(eng, s_x1, r * 2)
                    t3 = tmp.rearrange("p (g n) -> p g n", g=2)
                    eng.tensor_tensor(t3, bank[6 + c][:, :].rearrange("p (g n) -> p g n", g=2),
                                      rowC[:, :].unsqueeze(1).to_broadcast([P, 2, H]), ALU.add).then_inc(f1["y"], 1)
                    eng.wait_ge(f1["y"], r + 1)
                    for g in range(2):
                        v = tile_of_x(r * 2 + g)
                        eng.scalar_tensor_tensor(v, tmp[:, g * H:(g + 1) * H], gate[:, bass.ds(r * 2 + g, 1)], v,
                                                 ALU.mult, ALU.add).then_inc(s_x1, 1)
                    for g in range(2):
                        eng.wait_ge(s_x1, r * 2 + g + 1)
                        measure(r * 2 + g, tile_of_x(r * 2 + g), s_stat)

            pair_steps(eng, ffn1)
            eng.wait_ge(s_ctrd, PAIRS)
            chain(eng.tensor_scalar(rs_t[:, :], bank[5][:, 0:TILES], 1.0, None, ALU.add))
            chain(eng.reciprocal(rs_t[:, :], rs_t[:, :]))
            phase_end(eng, 4)
            eng.sem_inc(s_deg, 1)
            eng.wait_ge(s_deg, 2)
            statistics(3)
            schedule(1, 2)

            def finish2(t, a):
                eng.scalar_tensor_tensor(tile_of_x(t), bank[4 + a][:, 0:H], rs_t[:, bass.ds(t, 1)], tile_of_x(t),
                                         ALU.mult, ALU.add).then_inc(p2["self"], 1)

            node_tiles(p2, None, finish2)
            windows(1)
            phase_end(eng, 5)

            def arithmetic2(count, narrow):
                blocks, hots = (2, Ow) if narrow else (1, Ob)
                def step2(k, u, do):
                    if "hot" in do:
                        q, v, a = at(k, u)
                        b = a % 2
                        eng.wait_ge(s_rec2[a], v * 16 + 16)
                        wait(eng, e2["agg"], q - 1)
                        er = erec[:, a, :].rearrange("p (g k) -> p g k", k=3)
                        eng.tensor_tensor(dl[:, b, :], er[:, :, 0], nbase[:, bass.ds(q, 1)].to_broadcast([P, GRP]),
                                          ALU.add).then_inc(s_dl2, 1)
                        eng.wait_ge(s_dl2, q + 1)
                        for g in range(GRP):
                            ins = eng.tensor_scalar(hots[:, b, g, :], iota_f[:, 0:blocks * P], dl[:, b, g:g + 1], None,
                                                    ALU.is_equal)
                        ins.then_inc(e2["oh"], 1)
                    if "add" in do:
                        q, _, a = at(k, u, -1)
                        b = a % 2
                        r = eng.value_load(blk_i[0:1, bass.ds(q, 1)], min_val=0, max_val=TILES - blocks)
                        eng.wait_ge(e2["agg"], q + 1)
                        wait(eng, e2["add"], q * blocks)
                        for j in range(blocks):
                            v = X[:, bass.ds(r + j, 1), :].rearrange("p a n -> p (a n)")
                            eng.scalar_tensor_tensor(v, bank[b][:, j * H:(j + 1) * H], rs[:, bass.ds(r + j, 1)], v,
                                                     ALU.mult, ALU.add).then_inc(e2["add"], 1)
                steps(eng, step2, ("hot", 0), ("add", 1), count=count)

            either(eng, 1, arithmetic2)
            phase_end(eng, 6)

            measure_all()
            statistics(4)

            def norm3(k, u, do):
                t, _, a = at(k, u, per=NSET)
                wait(eng, n3["T"], t - NSET + 1)
                normed(xn[:, a, :], t).then_inc(n3["xn"], 1)

            steps(eng, norm3, ("norm", 0), count=TILES, per=NSET, ahead=NSET)
            eng.wait_ge(n3["sum"], TILES)
            chain(eng.tensor_reduce(c1[:, 0:2], added, AX.X, ALU.add))
            chain(eng.tensor_scalar(c1[:, 0:2], c1[:, 0:2], 1.0 / N, None, ALU.mult))
            eng.sem_inc(s_topk, 1)
            eng.wait_ge(s_ctp, 10)
            row = lambda k, n=NEXP: sm[0:1, k, 0:n]
            one = lambda k: zst[0:1, k:k + 1]

            def softmax(k, v, n):
                chain(eng.tensor_reduce(one(0), v, AX.X, ALU.max))
                chain(eng.tensor_scalar(row(2, n), v, one(0), None, ALU.subtract))
                eng.sem_inc(s_w5, 1)
                eng.wait_ge(s_mqp, k)
                chain(eng.tensor_reduce(one(1), row(3, n), AX.X, ALU.add))
                chain(eng.reciprocal(one(2), one(1)))
                chain(eng.tensor_scalar(row(4, n), row(3, n), one(2), None, ALU.mult))

            chain(eng.tensor_tensor(row(1), bank[4][0:1, 0:NEXP], row(11), ALU.add))
            softmax(1, row(1), NEXP)
            chain(eng.tensor_scalar(row(5), row(4), float(N), None, ALU.mult))
            chain(eng.reciprocal(row(6), row(5)))
            chain(eng.tensor_scalar(row(6), row(6), CAPACITY, -1.0, ALU.mult, ALU.add))
            chain(eng.tensor_scalar(row(5), row(5), CAPACITY, None, ALU.is_gt))
            chain(eng.tensor_tensor(row(6), row(6), row(5), ALU.mult))
            chain(eng.tensor_scalar(row(6), row(6), 1.0, None, ALU.add))
            chain(eng.tensor_tensor(row(7), row(4), row(6), ALU.mult))
            softmax(2, row(7), NEXP)
            chain(eng.tensor_copy(row(9), row(4)))
            chain(eng.max(row(10), row(9)))
            chain(eng.max_index(sm_i[0:1, :], row(10), row(9)))
            chain(eng.tensor_copy(ex_i[0:1, :], sm_i[0:1, 0:2]))
            eng.sem_inc(s_sel, 1)
            softmax(3, row(10, 2), 2)
            chain(eng.tensor_copy(row(8, 2), row(4, 2)))
            eng.sem_inc(s_topk, 1)
            eng.wait_ge(s_ctp, 11)
            chain(eng.tensor_copy(c1[:, 4:6], bank[4][:, 64:66]))
            eng.wait_ge(s_w4, 16 * 8)
            for j in range(2):
                v = w2_sb[:, 4 * j:4 * j + 4, :]
                chain(eng.tensor_scalar(v, v, c1[:, 4 + j:5 + j], None, ALU.mult))
            chain(eng.tensor_scalar(rowC[:, :], rowC[:, :], c1[:, 4:5], None, ALU.mult))
            chain(eng.scalar_tensor_tensor(rowC[:, :], rowD[:, :], c1[:, 5:6], rowC[:, :], ALU.mult, ALU.add))
            phase_end(eng, 7)

            def experts(r, c):
                wait(eng, s_z, r * 3)
                for g in range(2):
                    normed(tmp[:, g * H:(g + 1) * H], r * 2 + g).then_inc(s_y2, 1)
                eng.wait_ge(f2["L2"], r + 1)
                eng.wait_ge(s_y2, r * 2 + 2)
                z = XT[:, :, bass.ds(r * 256, 256)]
                t3 = tmp.rearrange("p (g n) -> p g n", g=2)
                eng.tensor_tensor(t3, bank[6 + c][:, :].rearrange("p (g n) -> p g n", g=2), t3,
                                  ALU.add).then_inc(f2["y"], 1)
                v = X[:, bass.ds(r * 2, 2), :]
                eng.tensor_tensor(v, v, rowB[:, :].unsqueeze(1).to_broadcast([P, 2, H]), ALU.add).then_inc(s_z, 1)
                eng.wait_ge(f2["y"], r + 1)
                eng.tensor_tensor(z, t3, rowC[:, :].unsqueeze(1).to_broadcast([P, 2, H]), ALU.add).then_inc(s_zz, 1)
                eng.wait_ge(s_zz, r + 1)
                for g in range(2):
                    measure(r * 2 + g, XT[:, g, bass.ds(r * 256, 256)], s_z)

            def final(p, before, c, batch=None):
                if batch is not None:
                    eng.wait_ge(s_rstd, batch + 5)
                wait(eng, s_h[2][c], before * 16)
                v = ob[:, 2 * c:2 * c + 2, :]
                for g in range(2):
                    normed(ob[:, 2 * c + g, :], p * 2 + g, XT[:, g, bass.ds(p * 256, 256)]).then_inc(s_fin, 1)
                eng.wait_ge(s_fin, p * 4 + 2)
                eng.tensor_tensor(v, v, rowA[:, :].unsqueeze(1).to_broadcast([P, 2, H]), ALU.mult).then_inc(s_fin, 1)
                eng.wait_ge(s_fin, p * 4 + 3)
                eng.tensor_tensor(v, v, X[:, bass.ds(p * 2, 2), :], ALU.add).then_inc(s_fin, 1)

            def measured(batch, pairs=BATCH):
                eng.wait_ge(s_z, (batch * BATCH + pairs) * 3)
                combine(bass.ds(batch * (2 * BATCH), 2 * pairs))

            def batch_of(i):
                for j in range(BATCH):
                    experts(i * BATCH + (BATCH + j), j % 2)
                    final(i * BATCH + j, i * (BATCH // 2) + j // 2, j % 2, i if j == 0 else None)
                measured(i + 1)

            for r in range(BATCH):
                experts(r, r % 2)
            measured(0)
            batch_of(0)
            with eng.Fori(1, BATCHES - 1) as i:
                chain.enter(i, 1, 8)
                batch_of(i)
            chain.leave(BATCHES - 2)
            experts(PAIRS - 1, (PAIRS - 1) % 2)
            for p in range(PAIRS - LAG, PAIRS - 1):
                final(p, p // 2, p % 2, BATCHES - 1 if p == PAIRS - LAG else None)
            measured(BATCHES, 1)
            final(PAIRS - 1, (PAIRS - 1) // 2, (PAIRS - 1) % 2, BATCHES)
            phase_end(eng, 8)


_INS = ["x", "src", "dst", "edge_attr_50", "edge_weight", "L0_gnn_aw_W", "L0_gnn_aw_b", "L0_gnn_m1_W", "L0_gnn_m1_b",
        "L0_gnn_m2_W", "L0_gnn_m2_b", "L0_gnn_o1_W", "L0_gnn_o1_b", "L0_gnn_o2_W", "L0_gnn_o2_b", "L0_ffn_wr",
        "L0_ffn_br", "L0_ffn_w1", "L0_ffn_b1", "L0_ffn_w2", "L0_ffn_b2", "L1_gnn_W", "L1_ffn_Wr", "L1_ffn_br",
        "L1_ffn_W1", "L1_ffn_b1", "L1_ffn_W2", "L1_ffn_b2", "L1_ffn_gamma", "L1_ffn_beta"]


def kernel(**inputs):
    import numpy as _np
    import concourse.bacc as _bacc
    from concourse import mybir as _mybir
    from concourse.bass_utils import run_bass_kernel_spmd as _run

    nc = _bacc.Bacc("TRN2", target_bir_lowering=False, num_devices=1)
    arrays, args = {}, []
    for name in _INS:
        a = _np.asarray(inputs[name])
        a = _np.ascontiguousarray(a.T if name == "L1_gnn_W" else a)
        arrays[f"in_{name}"] = a
        args.append(nc.dram_tensor(f"in_{name}", a.shape, _mybir.dt.from_np(a.dtype), kind="ExternalInput").ap())
    shape = inputs["x"].shape
    args.append(nc.dram_tensor("out_x", shape, _mybir.dt.float32, kind="ExternalOutput").ap())
    gnn_ffn_kernel(nc, *args)
    r = _run(nc, [arrays], core_ids=[0])
    return r.results[0]["out_x"]
```
